# Optimizing a Trainium2 kernel written in Bass

```python
import numpy as np
import jax
import jax.numpy as jnp

def _softmax(x, axis=-1):
    return jax.nn.softmax(x, axis=axis)

def _gelu(x):
    return jax.nn.gelu(x, approximate=True)

def _silu(x):
    return jax.nn.silu(x)

def _sigmoid(x):
    return jax.nn.sigmoid(x)

def _layernorm(x, axis=-1, eps=1e-05):
    m = jnp.mean(x, axis=axis, keepdims=True)
    v = jnp.var(x, axis=axis, keepdims=True)
    return (x - m) / jnp.sqrt(v + eps)

def _scatter_add(tgt, idx, src, axis=0):
    return tgt.at[idx].add(src)

def _segment_sum(src, seg, n):
    return jax.ops.segment_sum(src, seg, n)
kernel_name = 'mk_xattn_seq_d2_seqx_r4_65af5c'

def setup_inputs(seed: int=0):
    np.random.seed(seed)
    _w = jnp.asarray

    def _rec_inputs():
        import jax
        import jax.numpy as jnp
        _rk = jax.random.key(seed)
        x = 7.22e-05 + 1 * jax.random.normal(jax.random.fold_in(_rk, 1), (4, 1024, 256), jnp.float32)
        _lenS = 1024 - jax.random.randint(jax.random.fold_in(_rk, 7), (4,), 0, max(1, 1024 // 4) + 1, jnp.int32)
        _lenS2 = 154 - jax.random.randint(jax.random.fold_in(_rk, 8), (4,), 0, max(1, 154 // 4) + 1, jnp.int32)
        _ctx_1024P = jax.random.normal(jax.random.fold_in(_rk, 11), (4, 16, 256), jnp.float32)
        _ctx_1024c = jax.random.dirichlet(jax.random.fold_in(_rk, 511), 0.3 * jnp.ones((16,), jnp.float32), (4, 154))
        _ctx_1024t = jnp.einsum('bsk,bkd->bsd', _ctx_1024c, _ctx_1024P)
        _ctx_1024t = _ctx_1024t * jax.lax.rsqrt(jnp.mean(jnp.square(_ctx_1024t)) + 1e-12) * 0.953939
        ctx_1024 = 0.00208318 + 0.999174 * (_ctx_1024t + 0.3 * jax.random.normal(jax.random.fold_in(_rk, 611), (4, 154, 256), jnp.float32))
        return (x, ctx_1024)
    x, ctx_1024 = _rec_inputs()

    def _L0_xattn_setup():
        import jax, jax.numpy as jnp
        import numpy as np
        from functools import partial
        HEADS = 16
        DIM_HEAD = 64
        SCALE = DIM_HEAD ** (-0.5)
        MAX_ALLOWABLE = 256 * 256 * 8
        EPS = 1e-05

        def ln32(x, scale, bias):
            x32 = x.astype(jnp.float32)
            mean = jnp.mean(x32, axis=-1, keepdims=True)
            var = jnp.mean(jnp.square(x32 - mean), axis=-1, keepdims=True)
            y = (x32 - mean) * jax.lax.rsqrt(var + EPS) * scale.astype(jnp.float32) + bias.astype(jnp.float32)
            return y.astype(x.dtype)

        def heads_to_batch(t):
            b, s, d = t.shape
            return t.reshape(b, s, HEADS, d // HEADS).transpose(0, 2, 1, 3).reshape(b * HEADS, s, d // HEADS)

        def batch_to_heads(t):
            bh, s, dh = t.shape
            return t.reshape(bh // HEADS, HEADS, s, dh).transpose(0, 2, 1, 3).reshape(bh // HEADS, s, dh * HEADS)

        def _max_pow2(n):
            i = 1
            while n % 2 == 0:
                i *= 2
                n //= 2
            return i

        def sdpa(q, k, v):
            scores = jnp.einsum('bid,bjd->bij', q, k) * SCALE
            probs = jax.nn.softmax(scores, axis=2)
            return jnp.einsum('bij,bjd->bid', probs, v)

        def lowmem_attention(q, k, v):
            dimprod = q.shape[0] * q.shape[1] * k.shape[1]
            true_divisor = dimprod / MAX_ALLOWABLE
            if true_divisor < 1:
                n_splits = 1
            elif true_divisor >= q.shape[0]:
                n_splits = q.shape[0]
            else:
                nearest_pow2 = 2 ** np.round(np.log2(true_divisor))
                n_splits = int(min(_max_pow2(q.shape[0]), nearest_pow2))
            nq, nk, nv = [h.reshape(n_splits, h.shape[0] // n_splits, h.shape[-2], h.shape[-1]) for h in (q, k, v)]
            outs = jax.lax.scan(lambda c, a: (None, sdpa(*a)), None, (nq, nk, nv))[1]
            return outs.reshape(-1, outs.shape[-2], outs.shape[-1])

        def attention(x, ctx, Wq, Wkv, Wo, bo):
            q = x @ Wq
            k, v = jnp.split(ctx @ Wkv, 2, axis=-1)
            out = lowmem_attention(heads_to_batch(q), heads_to_batch(k), heads_to_batch(v))
            return batch_to_heads(out) @ Wo + bo

        def geglu_ff(x, Wff1, bff1, Wff2, bff2):
            h = x @ Wff1 + bff1
            lin, gelu = jnp.split(h, 2, axis=-1)
            h = lin * (gelu * jax.nn.sigmoid(1.702 * gelu))
            return h @ Wff2 + bff2
        key = jax.random.key(seed)
        ks = jax.random.split(key, 12)
        B, S, D, CTX = (4, 512, 256, 77)
        s = 0.02
        return {'hidden_states': jax.random.normal(ks[0], (B, S, D), jnp.float32), 'context': jax.random.normal(ks[1], (B, CTX, D), jnp.float32), 'Wq1': jax.random.normal(ks[2], (D, D), jnp.float32) * s, 'Wkv1': jax.random.normal(ks[3], (D, 2 * D), jnp.float32) * s, 'Wo1': jax.random.normal(ks[4], (D, D), jnp.float32) * s, 'bo1': jnp.zeros((D,), jnp.float32), 'Wq2': jax.random.normal(ks[5], (D, D), jnp.float32) * s, 'Wkv2': jax.random.normal(ks[6], (D, 2 * D), jnp.float32) * s, 'Wo2': jax.random.normal(ks[7], (D, D), jnp.float32) * s, 'bo2': jnp.zeros((D,), jnp.float32), 'Wff1': jax.random.normal(ks[8], (D, 8 * D), jnp.float32) * s, 'bff1': jnp.zeros((8 * D,), jnp.float32), 'Wff2': jax.random.normal(ks[9], (4 * D, D), jnp.float32) * s, 'bff2': jnp.zeros((D,), jnp.float32), 'ln1_s': jnp.ones((D,), jnp.float32), 'ln1_b': jnp.zeros((D,), jnp.float32), 'ln2_s': jnp.ones((D,), jnp.float32), 'ln2_b': jnp.zeros((D,), jnp.float32), 'ln3_s': jnp.ones((D,), jnp.float32), 'ln3_b': jnp.zeros((D,), jnp.float32)}
    _L0_xattn_all = _L0_xattn_setup()
    _L0_xattn_in = {k: v for k, v in _L0_xattn_all.items() if k in ('Wq1', 'Wkv1', 'Wo1', 'bo1', 'Wq2', 'Wkv2', 'Wo2', 'bo2', 'Wff1', 'bff1', 'Wff2', 'bff2', 'ln1_s', 'ln1_b', 'ln2_s', 'ln2_b', 'ln3_s', 'ln3_b')}
    del _L0_xattn_all

    def _L1_xattn_setup():
        import jax, jax.numpy as jnp
        import numpy as np
        B, S, F = (4, 512, 256)
        key = jax.random.key(seed)
        ks = jax.random.split(key, 9)
        s = 1.0 / np.sqrt(F)
        return {'q': jax.random.normal(ks[0], (B, S, F), jnp.float32), 'k': jax.random.normal(ks[1], (B, S, F), jnp.float32), 'v': jax.random.normal(ks[2], (B, S, F), jnp.float32), 'Wq': jax.random.normal(ks[3], (F, F), jnp.float32) * s, 'bq': jax.random.normal(ks[4], (F,), jnp.float32) * s, 'Wk': jax.random.normal(ks[5], (F, F), jnp.float32) * s, 'bk': jax.random.normal(ks[6], (F,), jnp.float32) * s, 'Wv': jax.random.normal(ks[7], (F, F), jnp.float32) * s, 'bv': jax.random.normal(ks[8], (F,), jnp.float32) * s}
    _L1_xattn_all = _L1_xattn_setup()
    _L1_xattn_in = {k: v for k, v in _L1_xattn_all.items() if k in ('Wq', 'bq', 'Wk', 'bk', 'Wv', 'bv')}
    del _L1_xattn_all
    return {'x': x, 'ctx_1024': ctx_1024, 'L0_xattn_Wq1': _L0_xattn_in['Wq1'], 'L0_xattn_Wkv1': _L0_xattn_in['Wkv1'], 'L0_xattn_Wo1': _L0_xattn_in['Wo1'], 'L0_xattn_bo1': _L0_xattn_in['bo1'], 'L0_xattn_Wq2': _L0_xattn_in['Wq2'], 'L0_xattn_Wkv2': _L0_xattn_in['Wkv2'], 'L0_xattn_Wo2': _L0_xattn_in['Wo2'], 'L0_xattn_bo2': _L0_xattn_in['bo2'], 'L0_xattn_Wff1': _L0_xattn_in['Wff1'], 'L0_xattn_bff1': _L0_xattn_in['bff1'], 'L0_xattn_Wff2': _L0_xattn_in['Wff2'], 'L0_xattn_bff2': _L0_xattn_in['bff2'], 'L0_xattn_ln1_s': _L0_xattn_in['ln1_s'], 'L0_xattn_ln1_b': _L0_xattn_in['ln1_b'], 'L0_xattn_ln2_s': _L0_xattn_in['ln2_s'], 'L0_xattn_ln2_b': _L0_xattn_in['ln2_b'], 'L0_xattn_ln3_s': _L0_xattn_in['ln3_s'], 'L0_xattn_ln3_b': _L0_xattn_in['ln3_b'], 'L1_xattn_Wq': _L1_xattn_in['Wq'], 'L1_xattn_bq': _L1_xattn_in['bq'], 'L1_xattn_Wk': _L1_xattn_in['Wk'], 'L1_xattn_bk': _L1_xattn_in['bk'], 'L1_xattn_Wv': _L1_xattn_in['Wv'], 'L1_xattn_bv': _L1_xattn_in['bv']}

def reference(x, ctx_1024, L0_xattn_Wq1, L0_xattn_Wkv1, L0_xattn_Wo1, L0_xattn_bo1, L0_xattn_Wq2, L0_xattn_Wkv2, L0_xattn_Wo2, L0_xattn_bo2, L0_xattn_Wff1, L0_xattn_bff1, L0_xattn_Wff2, L0_xattn_bff2, L0_xattn_ln1_s, L0_xattn_ln1_b, L0_xattn_ln2_s, L0_xattn_ln2_b, L0_xattn_ln3_s, L0_xattn_ln3_b, L1_xattn_Wq, L1_xattn_bq, L1_xattn_Wk, L1_xattn_bk, L1_xattn_Wv, L1_xattn_bv):
    import jax
    import jax.numpy as jnp

    def _L0_xattn_ref(hidden_states, context, Wq1, Wkv1, Wo1, bo1, Wq2, Wkv2, Wo2, bo2, Wff1, bff1, Wff2, bff2, ln1_s, ln1_b, ln2_s, ln2_b, ln3_s, ln3_b):
        import jax, jax.numpy as jnp
        import numpy as np
        from functools import partial
        HEADS = 16
        DIM_HEAD = 64
        SCALE = DIM_HEAD ** (-0.5)
        MAX_ALLOWABLE = 256 * 256 * 8
        EPS = 1e-05

        def ln32(x, scale, bias):
            x32 = x.astype(jnp.float32)
            mean = jnp.mean(x32, axis=-1, keepdims=True)
            var = jnp.mean(jnp.square(x32 - mean), axis=-1, keepdims=True)
            y = (x32 - mean) * jax.lax.rsqrt(var + EPS) * scale.astype(jnp.float32) + bias.astype(jnp.float32)
            return y.astype(x.dtype)

        def heads_to_batch(t):
            b, s, d = t.shape
            return t.reshape(b, s, HEADS, d // HEADS).transpose(0, 2, 1, 3).reshape(b * HEADS, s, d // HEADS)

        def batch_to_heads(t):
            bh, s, dh = t.shape
            return t.reshape(bh // HEADS, HEADS, s, dh).transpose(0, 2, 1, 3).reshape(bh // HEADS, s, dh * HEADS)

        def _max_pow2(n):
            i = 1
            while n % 2 == 0:
                i *= 2
                n //= 2
            return i

        def sdpa(q, k, v):
            scores = jnp.einsum('bid,bjd->bij', q, k) * SCALE
            probs = jax.nn.softmax(scores, axis=2)
            return jnp.einsum('bij,bjd->bid', probs, v)

        def lowmem_attention(q, k, v):
            dimprod = q.shape[0] * q.shape[1] * k.shape[1]
            true_divisor = dimprod / MAX_ALLOWABLE
            if true_divisor < 1:
                n_splits = 1
            elif true_divisor >= q.shape[0]:
                n_splits = q.shape[0]
            else:
                nearest_pow2 = 2 ** np.round(np.log2(true_divisor))
                n_splits = int(min(_max_pow2(q.shape[0]), nearest_pow2))
            nq, nk, nv = [h.reshape(n_splits, h.shape[0] // n_splits, h.shape[-2], h.shape[-1]) for h in (q, k, v)]
            outs = jax.lax.scan(lambda c, a: (None, sdpa(*a)), None, (nq, nk, nv))[1]
            return outs.reshape(-1, outs.shape[-2], outs.shape[-1])

        def attention(x, ctx, Wq, Wkv, Wo, bo):
            q = x @ Wq
            k, v = jnp.split(ctx @ Wkv, 2, axis=-1)
            out = lowmem_attention(heads_to_batch(q), heads_to_batch(k), heads_to_batch(v))
            return batch_to_heads(out) @ Wo + bo

        def geglu_ff(x, Wff1, bff1, Wff2, bff2):
            h = x @ Wff1 + bff1
            lin, gelu = jnp.split(h, 2, axis=-1)
            h = lin * (gelu * jax.nn.sigmoid(1.702 * gelu))
            return h @ Wff2 + bff2
        x = hidden_states
        x = attention(ln32(x, ln1_s, ln1_b), ln32(x, ln1_s, ln1_b), Wq1, Wkv1, Wo1, bo1) + x
        x = attention(ln32(x, ln2_s, ln2_b), context, Wq2, Wkv2, Wo2, bo2) + x
        x = geglu_ff(ln32(x, ln3_s, ln3_b), Wff1, bff1, Wff2, bff2) + x
        return x

    def _L1_xattn_ref(q, k, v, Wq, bq, Wk, bk, Wv, bv):
        import jax, jax.numpy as jnp
        import numpy as np
        B, S, F = (4, 512, 256)
        qp = jnp.einsum('bsf,gf->bsg', q, Wq) + bq
        kp = jnp.einsum('bsf,gf->bsg', k, Wk) + bk
        vp = jnp.einsum('bsf,gf->bsg', v, Wv) + bv
        attn = jax.nn.softmax(jnp.einsum('bqf,bkf->bqk', qp, kp), axis=-1)
        return jnp.einsum('bqk,bkf->bqf', attn, vp) + q
    x = _L0_xattn_ref(x, ctx_1024, L0_xattn_Wq1, L0_xattn_Wkv1, L0_xattn_Wo1, L0_xattn_bo1, L0_xattn_Wq2, L0_xattn_Wkv2, L0_xattn_Wo2, L0_xattn_bo2, L0_xattn_Wff1, L0_xattn_bff1, L0_xattn_Wff2, L0_xattn_bff2, L0_xattn_ln1_s, L0_xattn_ln1_b, L0_xattn_ln2_s, L0_xattn_ln2_b, L0_xattn_ln3_s, L0_xattn_ln3_b)
    x = _L1_xattn_ref(x, ctx_1024, ctx_1024, L1_xattn_Wq, L1_xattn_bq, L1_xattn_Wk, L1_xattn_bk, L1_xattn_Wv, L1_xattn_bv)
    return x

_drawn_inputs = setup_inputs


def setup_inputs(seed=0):
    import zlib

    import numpy as np

    out = dict(_drawn_inputs(seed))
    spreads = {'L0_xattn_bo1': (0.0, 0.1),
     'L0_xattn_bo2': (0.0, 0.1),
     'L0_xattn_bff1': (0.0, 0.1),
     'L0_xattn_bff2': (0.0, 0.1),
     'L0_xattn_ln1_s': (1.0, 0.6),
     'L0_xattn_ln1_b': (0.0, 0.388),
     'L0_xattn_ln2_s': (1.0, 0.6),
     'L0_xattn_ln2_b': (0.0, 2.0),
     'L0_xattn_ln3_s': (1.0, 0.6),
     'L0_xattn_ln3_b': (0.0, 0.558)}
    factors = {'L0_xattn_Wq1': 8.0, 'L0_xattn_Wo1': 2.742, 'L0_xattn_Wq2': 8.0, 'L1_xattn_bk': 64.0}
    for name, (base, spread) in spreads.items():
        noise = np.random.default_rng([zlib.crc32(name.encode()), seed]).standard_normal(out[name].shape)
        drawn = base * np.exp(spread * noise) if base else spread * noise
        out[name] = jnp.asarray(drawn.astype(out[name].dtype))
    for name, factor in factors.items():
        out[name] = (out[name] * factor).astype(out[name].dtype)
    return out
```

```python
from contextlib import ExitStack

import concourse.bass as bass
from concourse import mybir

F32 = mybir.dt.float32
BF16 = mybir.dt.bfloat16
ALU = mybir.AluOpType
ACT = mybir.ActivationFunctionType
AX_X = mybir.AxisListType.X

P = 128
B, S, D = 4, 1024, 256
H, DH = 16, 16
KD = D // P
CTX = 154
CT = CTX // 2
NCT = B * 2
CH = 256
TT = CH // P
NCH = B * S // CH
G = 4
W = P // G
NG = B * H // G
QH, QW = 2, 512
KT = S // P
STEPS = QH * KT
SLOTS = 2 * STEPS
NQ = S // P
PAIRS = G * NQ
FF = 4 * D
FM = FF // P
EPS = 1e-5
SCALE = 64 ** -0.5
GELU_A = 1.702

Q_PART = (0, 0, 0, 1, 1, 2)
K_PART = (0, 1, 2, 0, 1, 0)
ROWS = len(Q_PART) * DH
SHIFT = 2

PRE_STEPS, POST_STEPS = 6, 48
MAX_FROM, MAX_OVER, MAX_TURN = 4, 24, 28

ATT_LAG, MAX_LAG, POST_LAG = 6, 5, 10


def stages(n):
    return n < NCH, 0 <= n - MAX_LAG < NG, 0 <= n - ATT_LAG < NG, 0 <= n - POST_LAG < NCH


ON = 1
SEGMENTS = [(0, 4), (4, 6), (6, 10), (10, 16), (16, 20), (20, 22), (22, 26)]


def share(total, slot):
    return -(-total * (slot + 1) // SLOTS)


def max_pairs(slot):
    return min(PAIRS, max(0, -(-PAIRS * (slot + 1 - MAX_FROM) // MAX_OVER)))


def xattn_kernel(nc, t, out):
    ctx = ExitStack()
    with ctx:
        def sb(name, shape, dt=F32):
            return ctx.enter_context(nc.sbuf_tensor(name, shape, dt))

        def ps(name, shape):
            return ctx.enter_context(nc.psum_tensor(name, shape, F32))

        def sem(name):
            return ctx.enter_context(nc.semaphore(name))

        parts_s = nc.dram_tensor("parts_s", (2, 3, B * D, S), BF16).ap()
        v_s = nc.dram_tensor("v_s", (B * S, H * W), F32).ap()
        o1_s = nc.dram_tensor("o1_s", (B * H * W, S), F32).ap()
        q2_s = nc.dram_tensor("q2_s", (3, NCH * D, CH), BF16).ap()
        o2_s = nc.dram_tensor("o2_s", (NCH * H * W, CH), F32).ap()
        k2_s = nc.dram_tensor("k2_s", (3, D, B * CTX), BF16).ap()
        v2_s = nc.dram_tensor("v2_s", (B * CTX, H * W), F32).ap()
        kp_s = nc.dram_tensor("kp_s", (D, B * CTX), F32).ap()
        vp_s = nc.dram_tensor("vp_s", (B * CTX, D), F32).ap()

        ident = sb("ident", [P, P])
        neghalf = sb("neghalf", [P, TT])
        wq1 = sb("wq1", [P, KD, D])
        wkv1 = sb("wkv1", [P, KD, 2 * D])
        wo1 = sb("wo1", [P, KD, D])
        wq2 = sb("wq2", [P, KD, D])
        wo2 = sb("wo2", [P, KD, D])
        wff1 = sb("wff1", [P, KD, 2 * FF])
        wff2 = sb("wff2", [P, FM, D])
        bo1 = sb("bo1", [P, D])
        bo2 = sb("bo2", [P, D])
        bff2 = sb("bff2", [P, D])
        bvl = sb("bvl", [P, D])
        cols = sb("cols", [P, 2 * FM + 8 * KD])
        bff1 = cols[:, 0:2 * FM]
        ln_s, ln_b = [cols[:, 2 * FM + 3 * KD * i:2 * FM + 3 * KD * (i + 1)].rearrange(
            "p (l k) -> p l k", l=3) for i in range(2)]
        bql, bkl = [cols[:, 2 * FM + KD * i:2 * FM + KD * (i + 1)] for i in (6, 7)]
        b_tanh = sb("b_tanh", [P, FM])
        b_half = sb("b_half", [P, FM])
        wlT = sb("wlT", [P, 3, KD, D])
        qst_full = [sb(f"qst{u}", [P, G, S], BF16) for u in range(2)]
        qst = [q[0:ROWS + SHIFT, :, :] for q in qst_full]
        kst = [sb(f"kst{u}", [ROWS + SHIFT, G, S], BF16) for u in range(2)]
        vg = [sb(f"vg{u}", [P, KT, G * W]) for u in range(2)]
        probs = sb("probs", [P, 2, G, QW])
        o_sb = sb("o_sb", [P, QH, QW])
        mxq = sb("mxq", [P, PAIRS])
        sh_hi = sb("sh_hi", [PAIRS, P], BF16)
        sh_lo = sb("sh_lo", [PAIRS, P], BF16)
        pre_x = sb("pre_x", [P, TT, D])
        pre_st = sb("pre_st", [P, TT, 6])
        pre_mv = sb("pre_mv", [P, TT, 2])
        pre_ve = sb("pre_ve", [P, TT])
        pre_rs = sb("pre_rs", [P, TT])
        pre_xn = sb("pre_xn", [P, TT, D])
        pre_yT = sb("pre_yT", [P, KD, CH])
        qk_hi = [sb(f"qk_hi{i}", [P, KD * CH], BF16) for i in range(2)]
        qk_mid = [sb(f"qk_mid{i}", [P, KD * CH], BF16) for i in range(2)]
        qk_lo = [sb(f"qk_lo{i}", [P, KD * CH], BF16) for i in range(2)]
        qk_rest = [sb(f"qk_rest{i}", [P, KD * CH]) for i in range(2)]
        v_sb = sb("v_sb", [P, TT, H, W])
        x0 = sb("x0", [P, TT, D])
        x1 = sb("x1", [P, TT, D])
        x2 = sb("x2", [P, TT, D])
        x3 = sb("x3", [P, TT, D])
        xb = sb("xb", [P, TT, D])
        oT = sb("oT", [P, KD, CH])
        den = sb("den", [P, KD, CH])
        st = sb("st", [P, TT, 6])
        mv = sb("mv", [P, TT, 2])
        ve = sb("ve", [P, TT])
        rs = sb("rs", [P, TT])
        xn = sb("xn", [P, TT, D])
        yT = sb("yT", [P, KD, CH])
        q2_hi = sb("q2_hi", [P, KD * CH], BF16)
        q2_mid = sb("q2_mid", [P, KD * CH], BF16)
        q2_lo = sb("q2_lo", [P, KD * CH], BF16)
        q2_rest = sb("q2_rest", [P, KD * CH])
        q2st_full = sb("q2st", [P, H, CH], BF16)
        q2st = q2st_full[0:ROWS + SHIFT, :, :]
        k2st = sb("k2st", [ROWS + SHIFT, H, CTX], BF16)
        v2 = sb("v2", [CT, 2, H * W])
        kpT = sb("kpT", [P, KD, CTX])
        vp = sb("vp", [CT, 2, D])
        mx2 = sb("mx2", [P, H, TT])
        sh2_hi = sb("sh2_hi", [H * TT, P], BF16)
        sh2_lo = sb("sh2_lo", [H * TT, P], BF16)
        probs2 = sb("probs2", [CT, 8, 2 * CH])
        o2_sb = sb("o2_sb", [P, 2, 2 * CH])
        th = sb("th", [P, 2, CH])
        gb = sb("gb", [P, 2, CH])
        gate = sb("gate", [P, 2, CH])
        hT = sb("hT", [P, FM, CH])
        mx3 = sb("mx3", [P, TT])
        nm3 = sb("nm3", [P, TT])
        sum3 = sb("sum3", [P, TT])
        inv3 = sb("inv3", [P, TT])
        p3 = th[:, :, 0:CTX]
        p3T = gb[0:CT, :, :]
        v2_all = probs[0:CT, :, :, :].rearrange("p a g q -> p (a g q)").rearrange("p (c n) -> p c n", c=NCT)
        vp_all = probs2[0:CT, 0:4, :].rearrange("p a q -> p (a q)").rearrange("p (c n) -> p c n", c=NCT)
        ctx_n = probs2[0:CT, 4:8, :].rearrange("p a q -> p (a q)").rearrange("p (c n) -> p c n", c=NCT)
        cols_n = den[0:2 * FM + 8 * KD, 0, 0:P]
        wkv2 = hT[:, 0:4, :].rearrange("p a q -> p (a q)").rearrange("p (k n) -> p k n", k=KD)
        wl_n = [x[:, :, :] for x in (x0, x1, x2)]
        ctxT, kp_all = [q[:, :, :].rearrange("p g s -> p (g s)").bitcast(F32)[:, 0:KD * B * CTX].rearrange(
            "p (k n) -> p k n", k=KD) for q in qst_full]
        k2_part = [q2st_full[:, :, :].rearrange("p h s -> p (h s)")[:, i * KD * B * CTX:(i + 1) * KD * B * CTX].rearrange(
            "p (k n) -> p k n", k=KD) for i in range(3)]
        k2_rest = o_sb[:, :, 0:B * CTX // 2]

        ps_max = ps("ps_max", [P, 2 * 512])
        ps_s = [ps(f"ps_s{i}", [P, 512]) for i in range(2)]
        ps_o = ps("ps_o", [P, 512])
        ps_w = [ps(f"ps_w{i}", [P, 512]) for i in range(3)]

        s_load = sem("setup_loaded")
        s_const = sem("setup_constants")
        s_ct = sem("setup_ctx_turned")
        s_ctT = sem("setup_ctxT")
        s_wt = sem("setup_weight_turned")
        s_wlT = sem("setup_wlT")
        s_k2 = sem("setup_k2")
        s_k2hi = sem("setup_k2_hi")
        s_k2rest = sem("setup_k2_rest")
        s_k2mid = sem("setup_k2_mid")
        s_k2lo = sem("setup_k2_lo")
        s_kp = sem("setup_kp")
        s_kpb = sem("setup_kp_biased")
        s_v2 = sem("setup_v2_vp")
        s_v2c = sem("setup_v2_copied")
        s_vpb = sem("setup_vp_biased")
        s_zero = sem("setup_v2_zeroed")
        s_store = sem("setup_stored")
        s_ones = sem("setup_ones_rows")
        s_colT = sem("setup_cols_turned")
        s_cols = sem("setup_cols")
        s_bias = sem("setup_gate_biases")
        p_sp = sem("sp_passed")
        p_pool = sem("pool_passed")
        p_dve = sem("dve_passed")
        loop_sems = []

        def loop_sem(name):
            loop_sems.append(sem(name))
            return loop_sems[-1]

        a_x = loop_sem("pre_x_loaded")
        a_st = loop_sem("pre_stats")
        a_mv = loop_sem("pre_mean_var")
        a_ve = loop_sem("pre_var_eps")
        a_rs = loop_sem("pre_rstd")
        a_xn = loop_sem("pre_normalised")
        a_T = loop_sem("pre_turned")
        a_y = loop_sem("pre_y")
        a_p = [loop_sem("pre_q"), loop_sem("pre_k")]
        a_hi = [loop_sem("pre_q_hi"), loop_sem("pre_k_hi")]
        a_rest = [loop_sem("pre_q_rest"), loop_sem("pre_k_rest")]
        a_mid = [loop_sem("pre_q_mid"), loop_sem("pre_k_mid")]
        a_lo = [loop_sem("pre_q_lo"), loop_sem("pre_k_lo")]
        a_v = loop_sem("pre_v")
        a_vc = loop_sem("pre_v_copied")
        a_qkst = loop_sem("pre_parts_stored")
        a_vst = loop_sem("pre_v_stored")
        g_stack = loop_sem("att_stacks_loaded")
        g_mt = loop_sem("att_max_tile")
        g_mx = loop_sem("att_max")
        g_mT = loop_sem("att_max_turned")
        g_shi = loop_sem("att_shift_hi")
        g_slo = loop_sem("att_shift_lo")
        g_shl = loop_sem("att_shift_loaded")
        g_s = loop_sem("att_scores")
        g_e = loop_sem("att_exp")
        g_av = loop_sem("att_pv")
        g_o = loop_sem("att_o_copied")
        g_ost = [loop_sem(f"att_o_stored{i}") for i in range(QH)]
        c_in = loop_sem("post_in_loaded")
        c_kv = loop_sem("post_ctx_loaded")
        c_xb = [loop_sem(f"post_x_bias{i}") for i in range(3)]
        c_rd = [loop_sem(f"post_inv_den{i}") for i in range(2)]
        c_on = [loop_sem(f"post_o_normed{i}") for i in range(2)]
        c_wo = [loop_sem(f"post_wo{i}") for i in range(2)]
        c_x = [loop_sem(f"post_x{i + 1}") for i in range(3)]
        c_st = [loop_sem(f"post_stats{i}") for i in range(2)]
        c_mv = [loop_sem(f"post_mean_var{i}") for i in range(2)]
        c_ve = [loop_sem(f"post_var_eps{i}") for i in range(2)]
        c_rs = [loop_sem(f"post_rstd{i}") for i in range(2)]
        c_xn = [loop_sem(f"post_normalised{i}") for i in range(2)]
        c_T = [loop_sem(f"post_turned{i}") for i in range(3)]
        c_y = [loop_sem(f"post_y{i}") for i in range(3)]
        c_q2 = loop_sem("post_q2")
        c_q2hi = loop_sem("post_q2_hi")
        c_q2rest = loop_sem("post_q2_rest")
        c_q2mid = loop_sem("post_q2_mid")
        c_q2lo = loop_sem("post_q2_lo")
        c_q2st = loop_sem("post_q2_stored")
        c_q2stack = loop_sem("post_q2_stack_loaded")
        c_mt = loop_sem("post_max_tile")
        c_mx = loop_sem("post_max")
        c_mT = loop_sem("post_max_turned")
        c_shi = loop_sem("post_shift_hi")
        c_slo = loop_sem("post_shift_lo")
        c_shl = loop_sem("post_shift_loaded")
        c_s = loop_sem("post_scores")
        c_e = loop_sem("post_exp")
        c_av = loop_sem("post_pv")
        c_o = loop_sem("post_o_copied")
        c_ost = loop_sem("post_o_stored")
        c_o2 = loop_sem("post_o2_loaded")
        c_f1 = loop_sem("post_ff1")
        c_th = loop_sem("post_tanh")
        c_gb = loop_sem("post_gate_half")
        c_gt = loop_sem("post_gate")
        c_h = loop_sem("post_hidden")
        c_f2 = loop_sem("post_ff2")
        c_qp = loop_sem("post_qp")
        c_qpb = loop_sem("post_qp_biased")
        c_s3 = loop_sem("post_scores3")
        c_mx3 = loop_sem("post_max3")
        c_nm3 = loop_sem("post_neg_max3")
        c_e3 = loop_sem("post_exp3")
        c_inv3 = loop_sem("post_inv_sum3")
        c_pT = loop_sem("post_probs3_turned")
        c_pTc = loop_sem("post_probs3T")
        c_av3 = loop_sem("post_pv3")
        c_out = loop_sem("post_out")
        c_outst = loop_sem("post_out_stored")

        Q2F = 6

        def q2_heads(f):
            h0 = 3 * (f % Q2F)
            return f // Q2F, h0, min(3, H - h0)

        def within(v, hi):
            return v if isinstance(v, int) else nc.s_assert_within(
                v, 0, hi, skip_runtime_bounds_check_because="the loops' bounds are fixed by the shapes")

        def run(eng, body):
            for n0, n1 in SEGMENTS:
                if n1 - n0 == 2:
                    for u in range(2):
                        body(n0 + u, u, stages(n0 + u))
                    continue
                with eng.Fori(n0 // 2, n1 // 2) as pair:
                    for u in range(2):
                        body(pair * 2 + u, u, stages(n0 + u))

        def walk(n, flags, pre, post, slot_work, tail):
            has_pre, has_max, has_att, has_post = flags
            total = PRE_STEPS * has_pre + POST_STEPS * has_post
            done = 0

            def steps():
                if has_pre:
                    yield from pre(n)
                if has_post:
                    yield from post(n - POST_LAG, has_pre)

            work = steps()
            if has_max or has_att:
                for slot in range(SLOTS):
                    slot_work(slot)
                    while done < share(total, slot):
                        next(work)
                        done += 1
                tail()
            for _ in work:
                done += 1
            assert done == total

        block = ctx.enter_context(nc.Block())

        @block.sync
        def _(sp):
            def wt(w):
                return w.rearrange("(k p) n -> p k n", p=P)

            def row(v):
                return v.partition_broadcast(P)

            loads = [
                (ctx_n, t["ctx_1024"].rearrange("b (a p) d -> p (b a) d", p=CT)),
                (wkv2, wt(t["L0_xattn_Wkv2"])),
                (wl_n[0], wt(t["L1_xattn_Wq"])), (wl_n[1], wt(t["L1_xattn_Wk"])), (wl_n[2], wt(t["L1_xattn_Wv"])),
                (bvl[:, :], row(t["L1_xattn_bv"])),
                (wq1[:, :, :], wt(t["L0_xattn_Wq1"])), (wkv1[:, :, :], wt(t["L0_xattn_Wkv1"])),
                (wo1[:, :, :], wt(t["L0_xattn_Wo1"])), (wq2[:, :, :], wt(t["L0_xattn_Wq2"])),
                (wo2[:, :, :], wt(t["L0_xattn_Wo2"])), (wff1[:, :, :], wt(t["L0_xattn_Wff1"])),
                (wff2[:, :, :], wt(t["L0_xattn_Wff2"])),
                (bo1[:, :], row(t["L0_xattn_bo1"])), (bo2[:, :], row(t["L0_xattn_bo2"])),
                (bff2[:, :], row(t["L0_xattn_bff2"])),
            ]
            at = 0
            for name in ["L0_xattn_bff1"] + [f"L0_xattn_ln{i + 1}_{c}" for c in "sb" for i in range(3)] + [
                    "L1_xattn_bq", "L1_xattn_bk"]:
                rows = t[name].shape[0] // P
                loads.append((cols_n[at:at + rows, :], t[name].rearrange("(k p) -> k p", p=P)))
                at += rows
            assert len(loads) == N_LOADS
            for dst, src in loads:
                sp.dma_start(dst, src).then_inc(s_load, 16)
            for s in loop_sems:
                sp.sem_inc(s, ON)
            sp.wait_ge(s_k2hi, 4)
            sp.wait_ge(s_k2mid, 4)
            sp.wait_ge(s_k2lo, 4)
            for i in range(3):
                sp.dma_start(k2_s[i].rearrange("(k p) n -> p k n", p=P), k2_part[i][:, :, :]).then_inc(s_store, 16)
            sp.wait_ge(s_kpb, 4)
            sp.dma_start(kp_s.rearrange("(k p) n -> p k n", p=P), kp_all[:, :, :]).then_inc(s_store, 16)
            sp.wait_ge(s_v2c, NCT)
            sp.dma_start(v2_s.rearrange("(c p) n -> p c n", p=CT), v2_all).then_inc(s_store, 16)
            sp.wait_ge(s_vpb, NCT)
            sp.dma_start(vp_s.rearrange("(c p) n -> p c n", p=CT), vp_all).then_inc(s_store, 16)
            sp.wait_ge(s_store, 6 * 16)

            def wait(of, count):
                sp.wait_ge(of, count)
                sp.sem_inc(p_sp, 1)

            def pre(p):
                wait(a_xn, ON + p * 2)
                sp.dma_start(pre_x[:, :, :], t["x"].rearrange("b s d -> (b s) d").rearrange(
                    "(c i p) d -> c p i d", i=TT, p=P)[p]).then_inc(a_x, 16)
                for _ in range(PRE_STEPS - 1):
                    yield
                b, c = within(p // (S // CH), B - 1), p % (S // CH)
                for kind in range(2):
                    wait(a_lo[kind], ON + p + 1)
                    for i, part in enumerate((qk_hi, qk_mid, qk_lo)):
                        dst = parts_s[kind, i].rearrange("(b k p) (c s) -> b c p k s", b=B, p=P, s=CH)[b, c]
                        sp.dma_start(dst, part[kind][:, :].rearrange("p (k s) -> p k s", k=KD)).then_inc(a_qkst, 16)
                wait(a_vc, ON + p + 1)
                sp.dma_start(v_s.rearrange("(c i p) n -> c p i n", i=TT, p=P)[p],
                             v_sb[:, :, :, :].rearrange("p i h w -> p i (h w)")).then_inc(a_vst, 16)
                yield

            def load_stacks(m, par):
                b = m // G
                wait(a_qkst, ON + (b + 1) * (S // CH) * 96)
                wait(a_vst, ON + (b + 1) * (S // CH) * 16)
                if not isinstance(m, int) or m >= 2:
                    wait(g_s, ON + (m - 1) * 64)
                    wait(g_av, ON + (m - 1) * STEPS)
                for r in range(6):
                    for kind, stack, part in ((0, qst, Q_PART[r]), (1, kst, K_PART[r])):
                        sp.dma_start(stack[par][r * DH:(r + 1) * DH, :, :],
                                     parts_s[kind, part].rearrange("(m j d) s -> m d j s", j=G, d=DH)[m]
                                     ).then_inc(g_stack, 16)
                src = v_s.rearrange("(b k p) (g n) -> b g p k n", b=B, p=P, g=H // G)
                sp.dma_start(vg[par][:, :, :], src[within(m // G, B - 1), m % G]).then_inc(g_stack, 16)

            def load_o(dst, dst_den, src, done):
                rows = src.rearrange("(k h w) s -> k h w s", k=KD, w=W)
                for k in range(KD):
                    sp.dma_start(dst[:, k, :], rows[k, :, 0:DH, :]).then_inc(done, 16)
                    sp.dma_start(dst_den[:, k, :], rows[k, :, DH:DH + 1, :].to_broadcast(
                        [P // DH, DH, CH])).then_inc(done, 16)

            def post(o, has_pre):
                b, c = within(o // (S // CH), B - 1), o % (S // CH)
                wait(c_out, ON + o * 2)
                sp.dma_start(x0[:, :, :], t["x"].rearrange("b s d -> (b s) d").rearrange(
                    "(c i p) d -> c p i d", i=TT, p=P)[o]).then_inc(c_in, 16)
                for i in range(QH):
                    wait(g_ost[i], ON + (o // (S // CH) + 1) * (H // G) * 16)
                load_o(oT, den, o1_s.rearrange("(b r) (c s) -> b c r s", b=B, s=CH)[b, c], c_in)
                for r in range(6):
                    sp.dma_start(k2st[r * DH:(r + 1) * DH, :, :],
                                 k2_s[K_PART[r]].rearrange("(h d) (b n) -> b d h n", d=DH, b=B)[b]
                                 ).then_inc(c_kv, 16)
                sp.dma_start(v2[:, :, :], v2_s.rearrange("(b a p) n -> b p a n", b=B, p=CT)[b]).then_inc(c_kv, 16)
                sp.dma_start(kpT[:, :, :], kp_s.rearrange("(k p) (b n) -> b p k n", p=P, b=B)[b]).then_inc(c_kv, 16)
                sp.dma_start(vp[:, :, :], vp_s.rearrange("(b a p) n -> b p a n", b=B, p=CT)[b]).then_inc(c_kv, 16)
                for _ in range(6):
                    yield
                wait(c_q2lo, ON + o + 1)
                for i, part in enumerate((q2_hi, q2_mid, q2_lo)):
                    sp.dma_start(q2_s[i].rearrange("(o k p) s -> o p k s", k=KD, p=P)[o],
                                 part[:, :].rearrange("p (k s) -> p k s", k=KD)).then_inc(c_q2st, 16)
                wait(c_q2st, ON + (o + 1) * 48)
                for r in range(6):
                    sp.dma_start(q2st[r * DH:(r + 1) * DH, :, :],
                                 q2_s[Q_PART[r]].rearrange("(o h d) s -> o d h s", h=H, d=DH)[o]
                                 ).then_inc(c_q2stack, 16)
                for _ in range(8):
                    yield
                wait(c_slo, ON + o + 1)
                for row_, part in ((ROWS, sh2_hi), (ROWS + 1, sh2_lo)):
                    sp.dma_start(q2st[row_:row_ + 1, :, :].rearrange("a h (i p) -> a (h i) p", i=TT),
                                 part[:, :]).then_inc(c_shl, 16)
                yield
                for _ in range(4):
                    yield
                for e in range(2):
                    wait(c_o, ON + o * 2 + e + 1)
                    sp.dma_start(o2_s.rearrange("(o e g p) s -> o e p g s", e=2, g=2, p=P)[o, e],
                                 o2_sb[:, e, :].rearrange("p (g s) -> p g s", g=2)).then_inc(c_ost, 16)
                    if e == 0:
                        for _ in range(4):
                            yield
                wait(c_ost, ON + (o + 1) * 32)
                load_o(oT, den, o2_s.rearrange("(o r) s -> o r s", o=NCH)[o], c_o2)
                for _ in range(24):
                    yield
                wait(c_out, ON + (o + 1) * 2)
                sp.dma_start(out.rearrange("b s d -> (b s) d").rearrange(
                    "(c i p) d -> c p i d", i=TT, p=P)[o], x0[:, :, :]).then_inc(c_outst, 16)
                wait(c_outst, ON + (o + 1) * 16)
                yield

            def body(n, u, flags):
                has_pre, has_max, has_att, has_post = flags
                grp, m = n - ATT_LAG, n - MAX_LAG
                if isinstance(n, int) and n == 4:
                    load_stacks(0, 0)
                    load_stacks(1, 1)

                def slot_work(slot):
                    if has_max and slot == MAX_TURN:
                        wait(g_slo, ON + m + 1)
                        for row_, part in ((ROWS, sh_hi), (ROWS + 1, sh_lo)):
                            sp.dma_start(qst[1 - u][row_:row_ + 1, :, :].rearrange("a j (q p) -> a (j q) p", p=P),
                                         part[:, :]).then_inc(g_shl, 16)
                    if has_att and slot == SLOTS // 2 + 1:
                        store_o(0)

                def store_o(qh):
                    wait(g_o, ON + grp * QH + qh + 1)
                    sp.dma_start(o1_s.rearrange("(m p) (q s) -> m q p s", p=P, q=QH)[grp, qh],
                                 o_sb[:, qh, :]).then_inc(g_ost[qh], 16)

                def tail():
                    if has_att:
                        store_o(1)
                        if has_max:
                            if not isinstance(n, int):
                                load_stacks(within(grp + 2, NG - 1), u)

                walk(n, flags, pre, post, slot_work, tail)

            run(sp, body)
            sp.wait_ge(c_outst, ON + NCH * 16)

        @block.gpsimd
        def _(pool):
            nc.gpsimd.memset(ident[:, :], 0.0).then_inc(s_const, 1)
            pool.wait_ge(s_const, 1)
            nc.gpsimd.affine_select(out=ident[:, :], in_=ident[:, :], compare_op=ALU.not_equal, fill=1.0, base=0,
                                    pattern=[[-1, P]], channel_multiplier=1).then_inc(s_const, 1)
            nc.gpsimd.memset(neghalf[:, :], -0.5).then_inc(s_const, 1)
            v = v_sb[:, :, :, :]
            nc.gpsimd.memset(v, 0.0).then_inc(s_const, 1)
            pool.wait_ge(s_const, 4)
            nc.gpsimd.memset(v[:, :, :, DH:DH + 1], 1.0).then_inc(s_const, 1)
            nc.gpsimd.memset(v2_all, 0.0).then_inc(s_zero, 1)
            pool.wait_ge(s_zero, 1)
            nc.gpsimd.memset(v2_all.rearrange("p c (h w) -> p (c h) w", w=W)[:, :, DH:DH + 1], 1.0).then_inc(s_zero, 1)
            pool.wait_ge(s_cols, 1)
            nc.gpsimd.tensor_scalar(b_tanh[:, :], bff1[:, FM:2 * FM], GELU_A / 2, 0.0, ALU.mult, ALU.add).then_inc(s_bias, 1)
            nc.gpsimd.tensor_scalar(b_half[:, :], bff1[:, FM:2 * FM], 0.5, 0.0, ALU.mult, ALU.add).then_inc(s_bias, 1)
            for f in range(4):
                k, half = divmod(f, 2)
                span = slice(half * B * CTX // 2, (half + 1) * B * CTX // 2)
                pool.wait_ge(s_k2rest, f + 1)
                nc.gpsimd.tensor_copy(k2_part[1][:, k, span], k2_rest[:, f % 2, :]).then_inc(s_k2mid, 1)
                pool.wait_ge(s_k2mid, f + 1)
                nc.gpsimd.tensor_tensor(k2_part[2][:, k, span], k2_rest[:, f % 2, :], k2_part[1][:, k, span],
                                        ALU.subtract).then_inc(s_k2lo, 1)

            def rstd(mean_var, var_eps, rstd_, ready, eps_done, done, count):
                pool.wait_ge(ready, ON + count * 2)
                pool.sem_inc(p_pool, 1)
                nc.gpsimd.tensor_scalar(var_eps[:, :], mean_var[:, :, 1], EPS, 0.0, ALU.add, ALU.add).then_inc(eps_done, 1)
                pool.wait_ge(eps_done, ON + count)
                nc.gpsimd.tensor_tensor(rstd_[:, :], var_eps[:, :], neghalf[:, :], ALU.pow).then_inc(done, 1)

            def parts(rest, mid, lo, rest_ready, mid_ready, lo_ready, count):
                pool.wait_ge(rest_ready, ON + count)
                pool.sem_inc(p_pool, 1)
                nc.gpsimd.tensor_copy(mid[:, :], rest[:, :]).then_inc(mid_ready, 1)
                pool.wait_ge(mid_ready, ON + count)
                nc.gpsimd.tensor_tensor(lo[:, :], rest[:, :], mid[:, :], ALU.subtract).then_inc(lo_ready, 1)

            def pre(p):
                rstd(pre_mv, pre_ve, pre_rs, a_mv, a_ve, a_rs, p + 1)
                for _ in range(4):
                    yield
                pool.wait_ge(a_qkst, ON + p * 96)
                parts(qk_rest[0], qk_mid[0], qk_lo[0], a_rest[0], a_mid[0], a_lo[0], p + 1)
                yield
                parts(qk_rest[1], qk_mid[1], qk_lo[1], a_rest[1], a_mid[1], a_lo[1], p + 1)
                yield

            def add_bias(dst, x, bias, done):
                for i in range(TT):
                    last = nc.gpsimd.tensor_tensor(dst[:, i, :], x[:, i, :], bias[:, :], ALU.add)
                last.then_inc(done, 1)

            def post(o, has_pre):
                pool.wait_ge(c_in, ON + (o + 1) * 80)
                add_bias(xb, x0, bo1, c_xb[0])
                for _ in range(3):
                    yield
                rstd(mv, ve, rs, c_mv[0], c_ve[0], c_rs[0], o + 1)
                yield
                pool.wait_ge(c_x[0], ON + o + 1)
                add_bias(xb, x1, bo2, c_xb[1])
                for _ in range(2):
                    yield
                parts(q2_rest, q2_mid, q2_lo, c_q2rest, c_q2mid, c_q2lo, o + 1)
                for _ in range(20):
                    yield
                rstd(mv, ve, rs, c_mv[1], c_ve[1], c_rs[1], o + 1)
                yield
                pool.wait_ge(c_x[1], ON + o + 1)
                add_bias(xb, x2, bff2, c_xb[2])
                for _ in range(21):
                    yield

            def body(n, u, flags):
                walk(n, flags, pre, post, lambda slot: None, lambda: None)

            run(pool, body)

        @block.scalar
        def _(act):
            act.wait_ge(s_load, N_LOADS * 16)
            act.wait_ge(s_colT, 1)
            nc.scalar.copy(cols[:, :], ps_o[:, 0:2 * FM + 8 * KD]).then_inc(s_cols, 1)
            act.wait_ge(s_cols, 1)
            for c in range(NCT):
                act.wait_ge(s_ct, c + 1)
                nc.scalar.copy(ctxT[:, :, c * CT:(c + 1) * CT],
                               ps_w[c % 3][:, 0:2 * P].rearrange("p (k n) -> p k n", k=KD)[:, :, 0:CT]).then_inc(s_ctT, 1)
            for w in range(3):
                act.wait_ge(s_wt, w + 1)
                nc.scalar.copy(wlT[:, w, :, :].rearrange("p k n -> p (k n)"), ps_w[w][:, :]).then_inc(s_wlT, 1)
            half = B * CTX // 2
            for f in range(4):
                k, span = f // 2, slice((f % 2) * half, (f % 2 + 1) * half)
                act.wait_ge(s_k2, f + 1)
                nc.scalar.copy(k2_part[0][:, k, span], ps_s[f % 2][:, 0:half]).then_inc(s_k2hi, 1)
                act.wait_ge(s_kp, f + 1)
                nc.scalar.activation(kp_all[:, k, span], ps_w[f % 2][:, 0:half], ACT.Identity,
                                     bias=bkl[:, k:k + 1]).then_inc(s_kpb, 1)
            act.wait_ge(s_zero, 2)
            for c in range(NCT):
                act.wait_ge(s_v2, c + 1)
                nc.scalar.copy(v2_all[:, c, :].rearrange("p (h w) -> p h w", w=W)[:, :, 0:DH],
                               ps_w[c % 3][0:CT, 0:D].rearrange("p (h d) -> p h d", d=DH)).then_inc(s_v2c, 1)
            act.wait_ge(s_const, 5)
            act.wait_ge(s_bias, 2)

            def affine(dst, src, layer, done):
                for k in range(KD):
                    nc.scalar.activation(dst[:, k, :], src[:, k * CH:(k + 1) * CH], ACT.Identity,
                                         scale=ln_s[:, layer, k:k + 1], bias=ln_b[:, layer, k:k + 1]).then_inc(done, 1)

            def pre(p):
                yield
                yield
                act.wait_ge(a_T, ON + p + 1)
                affine(pre_yT, ps_w[0], 0, a_y)
                yield
                act.wait_ge(a_qkst, ON + p * 96)
                act.wait_ge(a_p[0], ON + p + 1)
                nc.scalar.copy(qk_hi[0][:, :], ps_w[1][:, :]).then_inc(a_hi[0], 1)
                yield
                act.wait_ge(a_p[1], ON + p + 1)
                nc.scalar.copy(qk_hi[1][:, :], ps_w[2][:, :]).then_inc(a_hi[1], 1)
                yield
                act.wait_ge(a_vst, ON + p * 16)
                act.wait_ge(a_v, ON + p + 1)
                nc.scalar.copy(v_sb[:, :, :, 0:DH].rearrange("p i h d -> p (i h) d"),
                               ps_w[0][:, :].rearrange("p (n d) -> p n d", d=DH)).then_inc(a_vc, 1)
                yield

            def post(o, has_pre):
                for _ in range(5):
                    yield
                act.wait_ge(c_T[0], ON + o + 1)
                affine(yT, ps_w[1], 1, c_y[0])
                yield
                act.wait_ge(c_q2st, ON + o * 48)
                act.wait_ge(c_q2, ON + o + 1)
                nc.scalar.copy(q2_hi[:, :], ps_w[2][:, :]).then_inc(c_q2hi, 1)
                for _ in range(9):
                    yield

                def exp2(h):
                    act.wait_ge(c_s, ON + o * H + h + 1)
                    act.wait_ge(c_av, ON + o * 4 + max(0, h // G - 1))
                    nc.scalar.activation(probs2[:, h % 8, :], ps_w[1 + h % 2][0:CT, :], ACT.Exp,
                                         scale=SCALE).then_inc(c_e, 1)

                def o_copy(e):
                    if e == 0:
                        act.wait_ge(c_ost, ON + o * 32)
                    act.wait_ge(c_av, ON + o * 4 + 2 * e + 2)
                    nc.scalar.copy(o2_sb[:, e, :], ps_w[0][:, :]).then_inc(c_o, 1)

                for i in range(8):
                    exp2(2 * i)
                    exp2(2 * i + 1)
                    if i == 4:
                        o_copy(0)
                    yield
                o_copy(1)
                for _ in range(5):
                    yield
                act.wait_ge(c_T[1], ON + o + 1)
                affine(yT, ps_w[2], 2, c_y[1])
                yield
                for m in range(FM):
                    bank = ps_w[m % 3]
                    act.wait_ge(c_f1, ON + o * FM + m + 1)
                    act.wait_ge(c_gt, ON + o * FM + max(0, m - 1))
                    nc.scalar.activation(th[:, m % 2, :], bank[:, CH:2 * CH], ACT.Tanh, scale=GELU_A / 2,
                                         bias=b_tanh[:, m:m + 1]).then_inc(c_th, 1)
                    nc.scalar.activation(gb[:, m % 2, :], bank[:, CH:2 * CH], ACT.Identity, scale=0.5,
                                         bias=b_half[:, m:m + 1]).then_inc(c_gb, 1)
                    yield
                for _ in range(5):
                    yield
                act.wait_ge(c_T[2], ON + o + 1)
                nc.scalar.copy(yT[:, :, :].rearrange("p k s -> p (k s)"), ps_w[0][:, :]).then_inc(c_y[2], 1)
                yield
                act.wait_ge(c_qp, ON + o + 1)
                for k in range(KD):
                    nc.scalar.activation(oT[:, k, :], ps_w[1][:, k * CH:(k + 1) * CH], ACT.Identity,
                                         bias=bql[:, k:k + 1]).then_inc(c_qpb, 1)
                yield
                yield
                act.wait_ge(c_nm3, ON + o + 1)
                for i in range(TT):
                    nc.scalar.activation(p3[:, i, :], ps_w[2][:, i * CH:i * CH + CTX], ACT.Exp,
                                         bias=nm3[:, i:i + 1], accum_out=sum3[:, i:i + 1]).then_inc(c_e3, 1)
                yield
                act.wait_ge(c_pT, ON + o + 1)
                nc.scalar.copy(p3T[:, :, :].rearrange("p a s -> p (a s)"), ps_w[0][0:CT, :]).then_inc(c_pTc, 1)
                yield
                yield

            def body(n, u, flags):
                has_pre, has_max, has_att, has_post = flags
                grp = n - ATT_LAG

                def exp_tile(c, j):
                    act.wait_ge(g_s, ON + grp * 64 + c * G + j + 1)
                    act.wait_ge(g_av, ON + grp * STEPS + max(0, c - 1))
                    nc.scalar.activation(probs[:, c % 2, j, :], ps_s[j % 2][:, :], ACT.Exp, scale=SCALE).then_inc(g_e, 1)

                def o_copy(qh):
                    act.wait_ge(g_av, ON + grp * STEPS + (qh + 1) * KT)
                    act.wait_ge(g_ost[qh], ON + grp * 16)
                    nc.scalar.copy(o_sb[:, qh, :], ps_o[:, :]).then_inc(g_o, 1)

                def slot_work(slot):
                    if has_att:
                        c, pair = divmod(slot, 2)
                        exp_tile(c, 2 * pair)
                        exp_tile(c, 2 * pair + 1)
                        if slot == SLOTS // 2:
                            o_copy(0)

                def tail():
                    if has_att:
                        o_copy(1)

                walk(n, flags, pre, post, slot_work, tail)

            run(act, body)

        @block.vector
        def _(dve):
            for tile in (kst[0], kst[1], k2st):
                nc.vector.memset(tile[ROWS:ROWS + SHIFT, :, :], 1.0).then_inc(s_ones, 1)
            dve.wait_ge(s_load, N_LOADS * 16)
            dve.wait_ge(s_cols, 1)
            half = B * CTX // 2
            for f in range(4):
                k, span = f // 2, slice((f % 2) * half, (f % 2 + 1) * half)
                dve.wait_ge(s_k2hi, f + 1)
                if f >= 2:
                    dve.wait_ge(s_k2lo, f - 1)
                nc.vector.tensor_tensor(k2_rest[:, f % 2, :], ps_s[f % 2][:, 0:half], k2_part[0][:, k, span],
                                        ALU.subtract).then_inc(s_k2rest, 1)
            for c in range(NCT):
                dve.wait_ge(s_v2c, c + 1)
                nc.vector.tensor_tensor(vp_all[:, c, :], ps_w[c % 3][0:CT, D:2 * D], bvl[0:CT, :],
                                        ALU.add).then_inc(s_vpb, 1)

            def stats(x, stat, mean_var, stat_done, mv_done, base):
                for i in range(TT):
                    nc.vector.bn_stats(stat[:, i, :], x[:, i, :]).then_inc(stat_done, 1)
                dve.wait_ge(stat_done, ON + base + TT)
                dve.sem_inc(p_dve, 1)
                for i in range(TT):
                    nc.vector.bn_aggr(mean_var[:, i, :], stat[:, i, :]).then_inc(mv_done, 1)

            def normalise(dst, x, mean_var, rstd_, done):
                for i in range(TT):
                    nc.vector.tensor_scalar(dst[:, i, :], x[:, i, :], mean_var[:, i, 0:1], rstd_[:, i:i + 1],
                                            ALU.subtract, ALU.mult).then_inc(done, 1)

            def pre(p):
                dve.wait_ge(a_x, ON + (p + 1) * 16)
                stats(pre_x, pre_st, pre_mv, a_st, a_mv, p * 2)
                yield
                dve.wait_ge(a_rs, ON + p + 1)
                dve.wait_ge(a_T, ON + p)
                normalise(pre_xn, pre_x, pre_mv, pre_rs, a_xn)
                yield
                yield
                for kind in range(2):
                    dve.wait_ge(a_hi[kind], ON + p + 1)
                    dve.wait_ge(a_lo[kind], ON + p)
                    nc.vector.tensor_tensor(qk_rest[kind][:, :], ps_w[1 + kind][:, :], qk_hi[kind][:, :],
                                            ALU.subtract).then_inc(a_rest[kind], 1)
                    yield
                yield

            def norm_o(which, o):
                flat = den[:, :, :].rearrange("p k s -> p (k s)")
                o_flat = oT[:, :, :].rearrange("p k s -> p (k s)")
                nc.vector.reciprocal(flat, flat).then_inc(c_rd[which], 1)
                dve.wait_ge(c_rd[which], ON + o + 1)
                nc.vector.tensor_tensor(o_flat, o_flat, flat, ALU.mult).then_inc(c_on[which], 1)

            def residual(which, dst, bank, o):
                dve.wait_ge(c_xb[which], ON + o + 1)
                nc.vector.tensor_tensor(dst[:, :, :].rearrange("p i d -> p (i d)"), bank[:, :],
                                        xb[:, :, :].rearrange("p i d -> p (i d)"), ALU.add).then_inc(c_x[which], 1)
                dve.wait_ge(c_x[which], ON + o + 1)

            def post(o, has_pre):
                yield
                dve.wait_ge(c_in, ON + (o + 1) * 80)
                norm_o(0, o)
                yield
                yield
                dve.wait_ge(c_wo[0], ON + o + 1)
                residual(0, x1, ps_w[0], o)
                stats(x1, st, mv, c_st[0], c_mv[0], o * 2)
                yield
                dve.wait_ge(c_rs[0], ON + o + 1)
                normalise(xn, x1, mv, rs, c_xn[0])
                yield
                yield
                dve.wait_ge(c_q2hi, ON + o + 1)
                nc.vector.tensor_tensor(q2_rest[:, :], ps_w[2][:, :], q2_hi[:, :], ALU.subtract).then_inc(c_q2rest, 1)
                yield
                yield
                for f in range(2 * Q2F):
                    i, h0, nh = q2_heads(f)
                    dve.wait_ge(c_mt, ON + o * 2 * Q2F + f + 1)
                    nc.vector.tensor_reduce(mx2[:, h0:h0 + nh, i], ps_w[f % 3][:, 0:nh * CTX].rearrange(
                        "p (h n) -> p h n", h=nh), AX_X, ALU.max).then_inc(c_mx, 1)
                    if f % 2:
                        yield
                dve.wait_ge(c_mT, ON + o + 1)
                negative(ps_w[0][0:H * TT, 0:P], sh2_hi, sh2_lo, c_shi, c_slo, o + 1)
                yield
                for _ in range(9):
                    yield
                dve.wait_ge(c_o2, ON + (o + 1) * 64)
                norm_o(1, o)
                yield
                yield
                dve.wait_ge(c_wo[1], ON + o + 1)
                residual(1, x2, ps_w[1], o)
                stats(x2, st, mv, c_st[1], c_mv[1], o * 2)
                yield
                dve.wait_ge(c_rs[1], ON + o + 1)
                normalise(xn, x2, mv, rs, c_xn[1])
                yield
                yield
                for m in range(FM):
                    dve.wait_ge(c_th, ON + o * FM + m + 1)
                    dve.wait_ge(c_gb, ON + o * FM + m + 1)
                    nc.vector.scalar_tensor_tensor(gate[:, m % 2, :], th[:, m % 2, :], 1.0, gb[:, m % 2, :],
                                                   ALU.add, ALU.mult).then_inc(c_gt, 1)
                    dve.wait_ge(c_gt, ON + o * FM + m + 1)
                    nc.vector.scalar_tensor_tensor(hT[:, m, :], ps_w[m % 3][:, 0:CH], bff1[:, m:m + 1],
                                                   gate[:, m % 2, :], ALU.add, ALU.mult).then_inc(c_h, 1)
                    yield
                for _ in range(4):
                    yield
                dve.wait_ge(c_f2, ON + o + 1)
                residual(2, x3, ps_w[2], o)
                yield
                yield
                yield
                dve.wait_ge(c_s3, ON + o + 1)
                nc.vector.tensor_reduce(mx3[:, :], ps_w[2][:, :].rearrange("p (i n) -> p i n", i=TT)[:, :, 0:CTX],
                                        AX_X, ALU.max).then_inc(c_mx3, 1)
                dve.wait_ge(c_mx3, ON + o + 1)
                nc.vector.tensor_scalar(nm3[:, :], mx3[:, :], -1.0, None, ALU.mult).then_inc(c_nm3, 1)
                yield
                dve.wait_ge(c_e3, ON + (o + 1) * TT)
                nc.vector.reciprocal(inv3[:, :], sum3[:, :]).then_inc(c_inv3, 1)
                yield
                yield
                dve.wait_ge(c_inv3, ON + o + 1)
                dve.wait_ge(c_av3, ON + o + 1)
                for i in range(TT):
                    nc.vector.scalar_tensor_tensor(x0[:, i, :], ps_w[1][:, i * D:(i + 1) * D], inv3[:, i:i + 1],
                                                   x3[:, i, :], ALU.mult, ALU.add).then_inc(c_out, 1)
                yield

            def negative(src, hi, lo, hi_done, lo_done, count):
                nc.vector.tensor_scalar(hi[:, :], src, -1.0, None, ALU.mult).then_inc(hi_done, 1)
                dve.wait_ge(hi_done, ON + count)
                nc.vector.scalar_tensor_tensor(lo[:, :], src, -1.0, hi[:, :], ALU.mult, ALU.subtract).then_inc(lo_done, 1)

            def body(n, u, flags):
                has_pre, has_max, has_att, has_post = flags
                m = n - MAX_LAG

                def slot_work(slot):
                    if has_max:
                        for i in range(max_pairs(slot - 1), max_pairs(slot)):
                            dve.wait_ge(g_mt, ON + m * PAIRS + i + 1)
                            nc.vector.tensor_reduce(mxq[:, i:i + 1], ps_max[:, :], AX_X, ALU.max).then_inc(g_mx, 1)
                        if slot == MAX_TURN:
                            dve.wait_ge(g_mT, ON + m + 1)
                            dve.wait_ge(g_shl, ON + m * 32)
                            negative(ps_max[0:PAIRS, 0:P], sh_hi, sh_lo, g_shi, g_slo, m + 1)

                walk(n, flags, pre, post, slot_work, lambda: None)

            run(dve, body)

        @block.tensor
        def _(pe):
            mm = nc.tensor.matmul
            pe.wait_ge(s_load, N_LOADS * 16)
            pe.wait_ge(s_const, 2)
            nc.tensor.transpose(ps_o[:, 0:2 * FM + 8 * KD], cols_n, ident[0:2 * FM + 8 * KD, 0:2 * FM + 8 * KD]
                                ).then_inc(s_colT, 1)
            for c in range(NCT):
                if c >= 3:
                    pe.wait_ge(s_ctT, c - 2)
                for k in range(KD):
                    last = nc.tensor.transpose(ps_w[c % 3][:, k * P:k * P + CT], ctx_n[:, c, k * P:(k + 1) * P],
                                               ident[0:CT, 0:CT])
                last.then_inc(s_ct, 1)
            for w in range(3):
                pe.wait_ge(s_ctT, NCT)
                for kf in range(KD):
                    for kg in range(KD):
                        last = nc.tensor.transpose(ps_w[w][:, kf * D + kg * P:kf * D + (kg + 1) * P],
                                                   wl_n[w][:, kg, kf * P:(kf + 1) * P], ident[:, :])
                last.then_inc(s_wt, 1)
            pe.wait_ge(s_wlT, 3)
            half = B * CTX // 2
            for f in range(4):
                m, span = f // 2, slice((f % 2) * half, (f % 2 + 1) * half)
                if f >= 2:
                    pe.wait_ge(s_k2rest, f - 1)
                for k in range(KD):
                    last = mm(ps_s[f % 2][:, 0:half], wkv2[:, k, m * P:(m + 1) * P], ctxT[:, k, span],
                              start=(k == 0), stop=(k == KD - 1))
                last.then_inc(s_k2, 1)
                if f >= 2:
                    pe.wait_ge(s_kpb, f - 1)
                for k in range(KD):
                    last = mm(ps_w[f % 2][:, 0:half], wlT[:, 1, k, m * P:(m + 1) * P], ctxT[:, k, span],
                              start=(k == 0), stop=(k == KD - 1))
                last.then_inc(s_kp, 1)
            pe.wait_ge(s_kpb, 4)
            for c in range(NCT):
                if c >= 3:
                    pe.wait_ge(s_vpb, c - 2)
                for k in range(KD):
                    mm(ps_w[c % 3][0:CT, 0:D], ctxT[:, k, c * CT:(c + 1) * CT], wkv2[:, k, D:2 * D],
                       start=(k == 0), stop=(k == KD - 1))
                for k in range(KD):
                    last = mm(ps_w[c % 3][0:CT, D:2 * D], ctxT[:, k, c * CT:(c + 1) * CT], wlT[:, 2, k, :],
                              start=(k == 0), stop=(k == KD - 1))
                last.then_inc(s_v2, 1)
            pe.wait_ge(s_vpb, NCT)
            pe.wait_ge(s_const, 5)
            pe.wait_ge(s_ones, 3)

            def turn(bank, x):
                for k in range(KD):
                    for i in range(TT):
                        last = nc.tensor.transpose(bank[:, k * CH + i * P:k * CH + (i + 1) * P],
                                                   x[:, i, k * P:(k + 1) * P], ident[:, :])
                return last

            def project(bank, w, y):
                for m in range(KD):
                    for k in range(KD):
                        last = mm(bank[:, m * CH:(m + 1) * CH], w[:, k, m * P:(m + 1) * P], y[:, k, :],
                                  start=(k == 0), stop=(k == KD - 1))
                return last

            def project_rows(bank, y, w):
                for i in range(TT):
                    for k in range(KD):
                        last = mm(bank[:, i * D:(i + 1) * D], y[:, k, i * P:(i + 1) * P], w[:, k, :],
                                  start=(k == 0), stop=(k == KD - 1))
                return last

            def pre(p, chunks_out):
                yield
                yield
                pe.wait_ge(a_vc, ON + p)
                pe.wait_ge(a_rest[0], ON + p)
                pe.wait_ge(a_rest[1], ON + p)
                if chunks_out is not None:
                    pe.wait_ge(c_out, ON + chunks_out * 2)
                pe.wait_ge(a_xn, ON + (p + 1) * 2)
                turn(ps_w[0], pre_xn).then_inc(a_T, 1)
                yield
                pe.wait_ge(a_y, ON + (p + 1) * 2)
                project(ps_w[1], wq1, pre_yT).then_inc(a_p[0], 1)
                yield
                project(ps_w[2], wkv1, pre_yT).then_inc(a_p[1], 1)
                yield
                project_rows(ps_w[0], pre_yT, wkv1[:, :, D:2 * D]).then_inc(a_v, 1)
                yield

            def post(o, has_pre):
                yield
                yield
                if has_pre:
                    pe.wait_ge(a_vc, ON + o + POST_LAG + 1)
                    pe.wait_ge(a_rest[0], ON + o + POST_LAG + 1)
                    pe.wait_ge(a_rest[1], ON + o + POST_LAG + 1)
                pe.wait_ge(c_out, ON + o * 2)
                pe.wait_ge(c_on[0], ON + o + 1)
                project_rows(ps_w[0], oT, wo1).then_inc(c_wo[0], 1)
                yield
                yield
                yield
                pe.wait_ge(c_xn[0], ON + (o + 1) * 2)
                turn(ps_w[1], xn).then_inc(c_T[0], 1)
                yield
                pe.wait_ge(c_y[0], ON + (o + 1) * 2)
                project(ps_w[2], wq2, yT).then_inc(c_q2, 1)
                yield
                yield
                for f in range(2 * Q2F):
                    if f == 0:
                        pe.wait_ge(c_q2stack, ON + (o + 1) * 96)
                        pe.wait_ge(c_kv, ON + (o + 1) * 144)
                    if f >= 3:
                        pe.wait_ge(c_mx, ON + o * 2 * Q2F + f - 2)
                    i, h0, nh = q2_heads(f)
                    for j in range(nh):
                        last = mm(ps_w[f % 3][:, j * CTX:(j + 1) * CTX], q2st[0:ROWS, h0 + j, i * P:(i + 1) * P],
                                  k2st[0:ROWS, h0 + j, :], start=True, stop=True)
                    last.then_inc(c_mt, 1)
                    if f % 2:
                        yield
                pe.wait_ge(c_mx, ON + (o + 1) * 2 * Q2F)
                nc.tensor.transpose(ps_w[0][0:H * TT, 0:P], mx2[:, :, :].rearrange("p h i -> p (h i)"),
                                    ident[:, :]).then_inc(c_mT, 1)
                yield

                def scores2(h):
                    if h == 0:
                        pe.wait_ge(c_shl, ON + (o + 1) * 32)
                    if h >= 2:
                        pe.wait_ge(c_e, ON + o * H + h - 1)
                    for a in range(2):
                        last = mm(ps_w[1 + h % 2][0:CT, a * CH:(a + 1) * CH], k2st[:, h, a * CT:(a + 1) * CT],
                                  q2st[:, h, :], start=True, stop=True)
                    last.then_inc(c_s, 1)

                def values2(g):
                    pe.wait_ge(c_e, ON + o * H + G * g + G)
                    if g == 2:
                        pe.wait_ge(c_o, ON + o * 2 + 1)
                    for a in range(2):
                        for j in range(G):
                            h = G * g + j
                            last = mm(ps_w[0][j * W:(j + 1) * W, (g % 2) * CH:(g % 2 + 1) * CH],
                                      v2[:, a, h * W:(h + 1) * W], probs2[:, h % 8, a * CH:(a + 1) * CH],
                                      start=(a == 0), stop=(a == 1), tile_position=(0, j * W))
                    last.then_inc(c_av, 1)

                for i in range(8):
                    scores2(2 * i)
                    scores2(2 * i + 1)
                    if i >= 2 and i % 2 == 0:
                        values2(i // 2 - 1)
                    yield
                values2(3)
                yield
                yield
                pe.wait_ge(c_on[1], ON + o + 1)
                project_rows(ps_w[1], oT, wo2).then_inc(c_wo[1], 1)
                yield
                yield
                yield
                pe.wait_ge(c_xn[1], ON + (o + 1) * 2)
                turn(ps_w[2], xn).then_inc(c_T[1], 1)
                yield
                pe.wait_ge(c_y[1], ON + (o + 1) * 2)
                pe.wait_ge(c_o, ON + (o + 1) * 2)
                for m in range(FM):
                    if m >= 3:
                        pe.wait_ge(c_h, ON + o * FM + m - 2)
                    for part in range(2):
                        for k in range(KD):
                            last = mm(ps_w[m % 3][:, part * CH:(part + 1) * CH],
                                      wff1[:, k, (part * FM + m) * P:(part * FM + m + 1) * P], yT[:, k, :],
                                      start=(k == 0), stop=(k == KD - 1))
                    last.then_inc(c_f1, 1)
                    yield
                pe.wait_ge(c_h, ON + (o + 1) * FM)
                for q in range(4):
                    i = q // 2
                    for m in range((q % 2) * FM // 2, (q % 2 + 1) * FM // 2):
                        last = mm(ps_w[2][:, i * D:(i + 1) * D], hT[:, m, i * P:(i + 1) * P], wff2[:, m, :],
                                  start=(m == 0), stop=(m == FM - 1))
                    if q == 3:
                        last.then_inc(c_f2, 1)
                    yield
                yield
                pe.wait_ge(c_x[2], ON + o + 1)
                turn(ps_w[0], x3).then_inc(c_T[2], 1)
                yield
                pe.wait_ge(c_y[2], ON + o + 1)
                project(ps_w[1], wlT[:, 0, :, :], yT).then_inc(c_qp, 1)
                yield
                pe.wait_ge(c_qpb, ON + (o + 1) * 2)
                for i in range(TT):
                    for k in range(KD):
                        last = mm(ps_w[2][:, i * CH:i * CH + CTX], oT[:, k, i * P:(i + 1) * P], kpT[:, k, :],
                                  start=(k == 0), stop=(k == KD - 1))
                last.then_inc(c_s3, 1)
                yield
                yield
                pe.wait_ge(c_e3, ON + (o + 1) * TT)
                for a in range(2):
                    for i in range(TT):
                        last = nc.tensor.transpose(ps_w[0][0:CT, a * CH + i * P:a * CH + (i + 1) * P],
                                                   p3[:, i, a * CT:(a + 1) * CT], ident[:, :])
                last.then_inc(c_pT, 1)
                yield
                pe.wait_ge(c_pTc, ON + o + 1)
                for i in range(TT):
                    for a in range(2):
                        last = mm(ps_w[1][:, i * D:(i + 1) * D], p3T[:, a, i * P:(i + 1) * P], vp[:, a, :],
                                  start=(a == 0), stop=(a == 1))
                last.then_inc(c_av3, 1)
                yield

            def body(n, u, flags):
                has_pre, has_max, has_att, has_post = flags
                grp, m = n - ATT_LAG, n - MAX_LAG

                def max_tile(i):
                    j, q = divmod(i, NQ)
                    qs, ks = qst[1 - u], kst[1 - u]
                    if i == 0:
                        pe.wait_ge(g_stack, ON + (m + 1) * 13 * 16)
                        pe.wait_ge(g_slo, ON + m)
                    pe.wait_ge(g_mx, ON + m * PAIRS + i)
                    for k in range(2):
                        last = mm(ps_max[:, k * 512:(k + 1) * 512], qs[0:ROWS, j, q * P:(q + 1) * P],
                                  ks[0:ROWS, j, k * 512:(k + 1) * 512], start=True, stop=True)
                    last.then_inc(g_mt, 1)

                def scores(c, j):
                    qh, kt = divmod(c, KT)
                    if c == 0 and j == 0:
                        pe.wait_ge(g_shl, ON + (grp + 1) * 32)
                    pe.wait_ge(g_e, ON + grp * 64 + max(0, c * G + j - 1))
                    mm(ps_s[j % 2][:, :], kst[u][:, j, kt * P:(kt + 1) * P],
                       qst[u][:, j, qh * QW:(qh + 1) * QW], start=True, stop=True).then_inc(g_s, 1)

                def values(c):
                    qh, kt = divmod(c, KT)
                    pe.wait_ge(g_e, ON + grp * 64 + (c + 1) * G)
                    if kt == 0:
                        pe.wait_ge(g_o, ON + grp * QH + qh)
                    for j in range(G):
                        last = mm(ps_o[j * W:(j + 1) * W, :], vg[u][:, kt, j * W:(j + 1) * W],
                                  probs[:, c % 2, j, :], start=(kt == 0), stop=(kt == KT - 1),
                                  tile_position=(0, j * W))
                    last.then_inc(g_av, 1)

                def slot_work(slot):
                    if has_max:
                        for i in range(max_pairs(slot - 1), max_pairs(slot)):
                            max_tile(i)
                        if slot == MAX_TURN:
                            pe.wait_ge(g_mx, ON + (m + 1) * PAIRS)
                            nc.tensor.transpose(ps_max[0:PAIRS, 0:P], mxq[:, :], ident[:, :]).then_inc(g_mT, 1)
                    if has_att:
                        c, pair = divmod(slot, 2)
                        scores(c, 2 * pair)
                        scores(c, 2 * pair + 1)
                        if pair == 0 and c > 0:
                            values(c - 1)

                def tail():
                    if has_att:
                        values(STEPS - 1)

                chunks_out = None
                if has_pre and has_post:
                    chunks_out = n - POST_LAG
                walk(n, flags, lambda p: pre(p, chunks_out), post, slot_work, tail)

            run(pe, body)


N_LOADS = 25

_INS = ["x", "ctx_1024"] + ["L0_xattn_" + s for s in (
    "Wq1", "Wkv1", "Wo1", "bo1", "Wq2", "Wkv2", "Wo2", "bo2", "Wff1", "bff1", "Wff2", "bff2",
    "ln1_s", "ln1_b", "ln2_s", "ln2_b", "ln3_s", "ln3_b")] + ["L1_xattn_" + s for s in (
        "Wq", "bq", "Wk", "bk", "Wv", "bv")]


def kernel(**inputs):
    import numpy as _np
    import concourse.bacc as _bacc
    from concourse import mybir as _mybir
    from concourse.bass_utils import run_bass_kernel_spmd as _run

    nc = _bacc.Bacc("TRN2", target_bir_lowering=False, num_devices=1)
    arrays, tensors = {}, {}
    for name in _INS:
        a = _np.ascontiguousarray(inputs[name])
        arrays[f"in_{name}_dram"] = a
        tensors[name] = nc.dram_tensor(f"in_{name}_dram", a.shape, _mybir.dt.from_np(a.dtype),
                                       kind="ExternalInput").ap()
    out = nc.dram_tensor("out_dram", (B, S, D), _mybir.dt.from_np(_np.dtype("float32")), kind="ExternalOutput").ap()
    xattn_kernel(nc, tensors, out)
    r = _run(nc, [arrays], core_ids=[0])
    return r.results[0]["out_dram"]
```

```python
from contextlib import ExitStack

import concourse.bass as bass
from concourse import mybir

F32 = mybir.dt.float32
BF16 = mybir.dt.bfloat16
ALU = mybir.AluOpType
ACT = mybir.ActivationFunctionType
AX_X = mybir.AxisListType.X

P = 128
B, S, D = 4, 1024, 256
H, DH = 16, 16
KD = D // P
CTX = 154
CT = CTX // 2
NCT = B * 2
CH = 256
TT = CH // P
NCH = B * S // CH
G = 4
W = P // G
NG = B * H // G
QH, QW = 2, 512
KT = S // P
STEPS = QH * KT
SLOTS = 2 * STEPS
NQ = S // P
PAIRS = G * NQ
FF = 4 * D
FM = FF // P
EPS = 1e-5
SCALE = 64 ** -0.5
GELU_A = 1.702

PART_AT = ((0, 1, 2), (2, 1, 0))
STACK = ((0, 1, 0), (1, 2, 2))
ROWS = 6 * DH
SHIFT = 2

MAX_LAG, ATT_LAG, MID_LAG, CROSS_LAG, LAST_LAG = 4, 5, 9, 10, 11
PRE_STEPS, MID_STEPS, CROSS_STEPS, LAST_STEPS = 8, 9, 36, 27
PRE_AT, CROSS_AT, LAST_AT = (1, 5, 22), (0, 0, 24), (1, 1, 32)
CROSS_LOAD, DEN_LOAD, DEN_INV, LAST_LOAD = 26, 25, 27, 29
SUB = 3
MAX_FROM, MAX_MID, MAX_END, MAX_TURN = 4, 14, 29, 29
MAX_EARLY = 21


def stages(n):
    return (n < NCH,) + tuple(0 <= n - lag < NCH for lag in (MAX_LAG, ATT_LAG, MID_LAG, CROSS_LAG, LAST_LAG))


ON = 1
SEGMENTS = [(0, 4), (4, 6), (6, 8), (8, 10), (10, 12), (12, 16), (16, 20), (20, 22), (22, 24), (24, 26), (26, 27)]


def share(total, slot, at):
    if slot < at[0] or total == 0:
        return 0
    return 1 + min(total - 1, max(0, -(-(total - 1) * (slot + 1 - at[1]) // (at[2] - at[1]))))


def max_tiles(at):
    place = at + 1 - SUB * MAX_FROM
    early, late = SUB * (MAX_MID - MAX_FROM), SUB * (MAX_END - MAX_MID)
    if place <= early:
        return max(0, -(-MAX_EARLY * place // early))
    return min(2 * PAIRS, MAX_EARLY - (MAX_EARLY - 2 * PAIRS) * (place - early) // late)


def xattn_kernel(nc, t, out):
    ctx = ExitStack()
    with ctx:
        def sb(name, shape, dt=F32):
            return ctx.enter_context(nc.sbuf_tensor(name, shape, dt))

        def ps(name, shape):
            return ctx.enter_context(nc.psum_tensor(name, shape, F32))

        def sem(name):
            return ctx.enter_context(nc.semaphore(name))

        parts_s = nc.dram_tensor("parts_s", (2, B * P * 3, KD, S), BF16).ap()
        v_s = nc.dram_tensor("v_s", (B * S, H * W), F32).ap()
        o1_s = nc.dram_tensor("o1_s", (B * H * W, S), F32).ap()
        q2_s = nc.dram_tensor("q2_s", (NCH * P * 3, KD, CH), BF16).ap()
        o2_s = nc.dram_tensor("o2_s", (NCH * H * W, CH), F32).ap()
        k2_s = nc.dram_tensor("k2_s", (P * 3, B, KD * CTX), BF16).ap()
        v2_s = nc.dram_tensor("v2_s", (B * CTX, H * W), F32).ap()
        kp_s = nc.dram_tensor("kp_s", (D, B * CTX), F32).ap()
        vp_s = nc.dram_tensor("vp_s", (B * CTX, D), F32).ap()

        ident = sb("ident", [P, P])
        neghalf = sb("neghalf", [P, TT])
        wq1 = sb("wq1", [P, KD, D])
        wkv1 = sb("wkv1", [P, KD, 2 * D])
        wo1 = sb("wo1", [P, KD, D])
        wq2 = sb("wq2", [P, KD, D])
        wo2 = sb("wo2", [P, KD, D])
        wff1 = sb("wff1", [P, KD, 2 * FF])
        wff2 = sb("wff2", [P, FM, D])
        bo1 = sb("bo1", [P, D])
        bo2 = sb("bo2", [P, D])
        bff2 = sb("bff2", [P, D])
        bvl = sb("bvl", [P, D])
        cols = sb("cols", [P, 2 * FM + 8 * KD])
        bff1 = cols[:, 0:2 * FM]
        ln_s, ln_b = [cols[:, 2 * FM + 3 * KD * i:2 * FM + 3 * KD * (i + 1)].rearrange(
            "p (l k) -> p l k", l=3) for i in range(2)]
        bql, bkl = [cols[:, 2 * FM + KD * i:2 * FM + KD * (i + 1)] for i in (6, 7)]
        b_tanh = sb("b_tanh", [P, FM])
        b_half = sb("b_half", [P, FM])
        wlT = sb("wlT", [P, 3, KD, D])
        qst_full = [sb(f"qst{u}", [P, G, S], BF16) for u in range(2)]
        qst = [q[0:ROWS + SHIFT, :, :] for q in qst_full]
        kst = [sb(f"kst{u}", [ROWS + SHIFT, G, S], BF16) for u in range(2)]
        vg = [sb(f"vg{u}", [P, KT, G * W]) for u in range(2)]
        probs = sb("probs", [P, 2, G, QW])
        o_sb = sb("o_sb", [P, QH, QW])
        mxh = sb("mxh", [P, PAIRS, 2])
        mxq = sb("mxq", [P, PAIRS])
        sh_hi = sb("sh_hi", [PAIRS, P], BF16)
        sh_lo = sb("sh_lo", [PAIRS, P], BF16)
        pre_x = sb("pre_x", [P, TT, D])
        pre_st = sb("pre_st", [P, TT, 6])
        pre_mv = sb("pre_mv", [P, TT, 2])
        pre_ve = sb("pre_ve", [P, TT])
        pre_rs = sb("pre_rs", [P, TT])
        pre_yT = sb("pre_yT", [P, KD, CH])
        qk_parts = [sb(f"qk_parts{i}", [P, 3, KD * CH], BF16) for i in range(2)]
        qk_f = [sb(f"qk_f{i}", [P, KD * CH]) for i in range(2)]
        v_sb = sb("v_sb", [P, TT, H, W])
        x0 = sb("x0", [P, TT, D])
        x1 = [sb(f"x1_{u}", [P, TT, D]) for u in range(2)]
        oT = sb("oT", [P, KD, CH])
        den = sb("den", [P, KD, CH])
        x2 = sb("x2", [P, TT, D])
        xb = sb("xb", [P, TT, D])
        oT2 = sb("oT2", [P, KD, CH])
        den2 = sb("den2", [P, KD, CH])
        st, mv, ve, rs = [[sb(f"{name}{i}", shape) for i in range(2)] for name, shape in (
            ("st", [P, TT, 6]), ("mv", [P, TT, 2]), ("ve", [P, TT]), ("rs", [P, TT]))]
        q2_parts = sb("q2_parts", [P, 3, KD * CH], BF16)
        q2_f = sb("q2_f", [P, KD * CH])
        q2st_full = sb("q2st", [P, H, CH], BF16)
        q2st = q2st_full[0:ROWS + SHIFT, :, :]
        k2st = sb("k2st", [ROWS + SHIFT, H, CTX], BF16)
        v2 = sb("v2", [CT, 2, H * W])
        kpT = sb("kpT", [P, KD, CTX])
        vp = sb("vp", [CT, 2, D])
        mx2 = sb("mx2", [P, H, TT])
        sh2_hi = sb("sh2_hi", [H * TT, P], BF16)
        sh2_lo = sb("sh2_lo", [H * TT, P], BF16)
        probs2_full = sb("probs2", [P, 8, 2 * CH])
        probs2 = probs2_full[0:CT, :, :]
        o2_sb = sb("o2_sb", [P, 2, 2 * CH])
        th = sb("th", [P, 2, CH])
        gb = sb("gb", [P, 2, CH])
        hT = sb("hT", [P, FM, CH])
        mx3 = sb("mx3", [P, TT])
        nm3 = sb("nm3", [P, TT])
        sum3 = sb("sum3", [P, TT])
        inv3 = sb("inv3", [P, TT])
        den_c = [sb(f"den_c{i}", [P, H * CH // P]) for i in range(2)]
        p3 = th[:, :, 0:CTX]
        p3T = gb[0:CT, :, :]
        oT_rows, den_rows, oT2_rows = [x[:, :, :].rearrange("p k s -> p (k s)").rearrange(
            "p (i d) -> p i d", i=TT) for x in (oT, den, oT2)]
        v2_all = probs[0:CT, :, :, :].rearrange("p a g q -> p (a g q)").rearrange("p (c n) -> p c n", c=NCT)
        vp_all = probs2[0:CT, 0:4, :].rearrange("p a q -> p (a q)").rearrange("p (c n) -> p c n", c=NCT)
        ctx_n = probs2[0:CT, 4:8, :].rearrange("p a q -> p (a q)").rearrange("p (c n) -> p c n", c=NCT)
        cols_n = den[0:2 * FM + 8 * KD, 0, 0:P]
        wkv2 = hT[:, 0:4, :].rearrange("p a q -> p (a q)").rearrange("p (k n) -> p k n", k=KD)
        wl_n = [x[:, :, :] for x in (x0, xb, x2)]
        ctxT = [hT[:, 4:8, :].rearrange("p a q -> p (a q)")[:, 0:B * CTX],
                q2_parts[:, :, :].rearrange("p t n -> p (t n)").bitcast(F32)[:, 0:B * CTX]]
        kp_all = probs2_full[:, 4:8, :].rearrange("p a q -> p (a q)")[:, 0:KD * B * CTX].rearrange(
            "p (k n) -> p k n", k=KD)
        k2_part = [q2st_full[:, :, :].rearrange("p h s -> p (h s)")[:, i * KD * B * CTX:(i + 1) * KD * B * CTX].rearrange(
            "p (b k n) -> p b k n", b=B, k=KD) for i in range(3)]
        k2_rest = o_sb[:, :, 0:B * CTX // 2].rearrange("p f (b n) -> p f b n", n=CTX)

        ps_max = [ps(f"ps_max{i}", [P, 512]) for i in range(2)]
        ps_s = [ps(f"ps_s{i}", [P, 512]) for i in range(2)]
        ps_o = ps("ps_o", [P, 512])
        ps_last = ps("ps_last", [P, 512])
        ps_cross = ps("ps_cross", [P, 512])
        ps_pre = ps("ps_pre", [P, 512])
        cross_banks = ([ps_cross, ps_cross], ps_s)
        last_banks = ([ps_last, ps_last], [ps_last, ps_max[0]])
        ps_w = [ps_last, ps_cross, ps_max[0]]

        s_load = sem("setup_pre_loaded")
        s_load2 = sem("setup_rest_loaded")
        s_const = sem("setup_constants")
        s_ct = sem("setup_ctx_turned")
        s_ctT = sem("setup_ctxT")
        s_wt = sem("setup_weight_turned")
        s_wlT = sem("setup_wlT")
        s_k2 = sem("setup_k2")
        s_k2hi = sem("setup_k2_hi")
        s_k2rest = sem("setup_k2_rest")
        s_k2mid = sem("setup_k2_mid")
        s_k2lo = sem("setup_k2_lo")
        s_kp = sem("setup_kp")
        s_kpb = sem("setup_kp_biased")
        s_v2 = sem("setup_v2_vp")
        s_v2c = sem("setup_v2_copied")
        s_vpb = sem("setup_vp_biased")
        s_zero = sem("setup_v2_zeroed")
        s_store = sem("setup_stored")
        s_ones = sem("setup_ones_rows")
        s_colT = sem("setup_cols_turned")
        s_cols = sem("setup_cols")
        s_bias = sem("setup_gate_biases")
        p_sp = sem("sp_passed")
        p_pool = sem("pool_passed")
        p_dve = sem("dve_passed")
        loop_sems = []

        def loop_sem(name):
            loop_sems.append(sem(name))
            return loop_sems[-1]

        a_x = loop_sem("pre_x_loaded")
        a_st = loop_sem("pre_stats")
        a_mv = loop_sem("pre_mean_var")
        a_ve = loop_sem("pre_var_eps")
        a_rs = loop_sem("pre_rstd")
        a_xn = loop_sem("pre_normalised")
        a_T = loop_sem("pre_turned")
        a_y = loop_sem("pre_y")
        a_p = [loop_sem("pre_q"), loop_sem("pre_k")]
        a_f = [loop_sem("pre_q_copied"), loop_sem("pre_k_copied")]
        a_hi = [loop_sem("pre_q_hi"), loop_sem("pre_k_hi")]
        a_rest = [loop_sem("pre_q_rest"), loop_sem("pre_k_rest")]
        a_mid = [loop_sem("pre_q_mid"), loop_sem("pre_k_mid")]
        a_lo = [loop_sem("pre_q_lo"), loop_sem("pre_k_lo")]
        a_v = loop_sem("pre_v")
        a_vc = loop_sem("pre_v_copied")
        a_qkst = loop_sem("pre_parts_stored")
        a_vst = loop_sem("pre_v_stored")
        g_stack = loop_sem("att_stacks_loaded")
        g_mt = loop_sem("att_max_tile")
        g_mx = loop_sem("att_max")
        g_mp = loop_sem("att_max_of_pairs")
        g_mT = loop_sem("att_max_turned")
        g_shi = loop_sem("att_shift_hi")
        g_slo = loop_sem("att_shift_lo")
        g_shl = loop_sem("att_shift_loaded")
        g_s = loop_sem("att_scores")
        g_e = loop_sem("att_exp")
        g_av = loop_sem("att_pv")
        g_o = loop_sem("att_o_copied")
        g_ost = [loop_sem(f"att_o_stored{i}") for i in range(QH)]
        c_x0 = loop_sem("mid_x_loaded")
        c_in = loop_sem("mid_in_loaded")
        c_kv = loop_sem("cross_ctx_loaded")
        c_xb = [loop_sem(f"post_x_bias{i}") for i in range(3)]
        c_den = [loop_sem(f"post_den_loaded{i}") for i in range(2)]
        c_rd = [loop_sem(f"post_inv_den{i}") for i in range(2)]
        c_inv = [loop_sem(f"post_inv_stored{i}") for i in range(2)]
        c_on = [loop_sem(f"post_o_normed{i}") for i in range(2)]
        c_wo = [loop_sem(f"post_wo{i}") for i in range(2)]
        c_x = [loop_sem(f"post_x{i + 1}") for i in range(3)]
        c_st = [loop_sem(f"post_stats{i}") for i in range(2)]
        c_mv = [loop_sem(f"post_mean_var{i}") for i in range(2)]
        c_ve = [loop_sem(f"post_var_eps{i}") for i in range(2)]
        c_rs = [loop_sem(f"post_rstd{i}") for i in range(2)]
        c_xn = [loop_sem(f"post_normalised{i}") for i in range(2)]
        c_T = [loop_sem(f"post_turned{i}") for i in range(3)]
        c_y = [loop_sem(f"post_y{i}") for i in range(3)]
        c_q2 = loop_sem("post_q2")
        c_q2f = loop_sem("mid_q2_copied")
        c_q2hi = loop_sem("post_q2_hi")
        c_q2rest = loop_sem("post_q2_rest")
        c_q2mid = loop_sem("post_q2_mid")
        c_q2lo = loop_sem("post_q2_lo")
        c_q2st = loop_sem("post_q2_stored")
        c_q2stack = loop_sem("post_q2_stack_loaded")
        c_mt = loop_sem("post_max_tile")
        c_mx = loop_sem("post_max")
        c_mT = loop_sem("post_max_turned")
        c_shi = loop_sem("post_shift_hi")
        c_slo = loop_sem("post_shift_lo")
        c_shl = loop_sem("post_shift_loaded")
        c_s = loop_sem("post_scores")
        c_e = loop_sem("post_exp")
        c_av = loop_sem("post_pv")
        c_o = loop_sem("cross_o_copied")
        c_ost = loop_sem("post_o_stored")
        c_o2 = loop_sem("last_in_loaded")
        c_f1 = loop_sem("post_ff1")
        c_th = loop_sem("post_tanh")
        c_gb = loop_sem("post_gate_half")
        c_gt = loop_sem("post_gate")
        c_h = loop_sem("post_hidden")
        c_f2 = loop_sem("post_ff2")
        c_qp = loop_sem("post_qp")
        c_qpb = loop_sem("post_qp_biased")
        c_s3 = loop_sem("post_scores3")
        c_mx3 = loop_sem("post_max3")
        c_nm3 = loop_sem("post_neg_max3")
        c_e3 = loop_sem("post_exp3")
        c_inv3 = loop_sem("post_inv_sum3")
        c_pT = loop_sem("post_probs3_turned")
        c_pTc = loop_sem("post_probs3T")
        c_av3 = loop_sem("post_pv3")
        c_out = loop_sem("post_out")
        c_outst = loop_sem("post_out_stored")

        Q2F = 6

        def q2_heads(f):
            h0 = 3 * (f % Q2F)
            return f // Q2F, h0, min(3, H - h0)

        def within(v, hi):
            return v if isinstance(v, int) else nc.s_assert_within(
                v, 0, hi, skip_runtime_bounds_check_because="the loops' bounds are fixed by the shapes")

        def run(eng, body, segments):
            for n0, n1 in segments:
                if n1 - n0 <= 2:
                    for n in range(n0, n1):
                        body(n, n % 2, stages(n), stages(n - 1)[2], stages(n + 1))
                    continue
                with eng.Fori(n0 // 2, n1 // 2) as pair:
                    for u in range(2):
                        body(pair * 2 + u, u, stages(n0 + u), stages(n0 + u - 1)[2], stages(n0 + u + 1))

        def walk(n, flags, pre, mid, cross, last, att_work, max_work, tail, loads=lambda slot: None,
                 late_last=False):
            has_pre, has_max, has_att, has_mid, has_cross, has_last = flags

            def pre_mid():
                work = mid(n - MID_LAG, has_pre) if has_mid else iter(())
                for _ in range(2 * has_mid):
                    next(work)
                    yield
                if has_pre:
                    yield from pre(n)
                yield from work

            chains = [
                (last(n - LAST_LAG) if has_last else iter(()), LAST_STEPS * has_last, LAST_AT),
                (cross(n - CROSS_LAG) if has_cross else iter(()), CROSS_STEPS * has_cross, CROSS_AT),
                (pre_mid(), PRE_STEPS * has_pre + MID_STEPS * has_mid, PRE_AT),
            ]

            def advance(i, slot, place=0, places=1):
                work, total, at = chains[i]
                at = [x * places for x in at]
                now = slot * places + place
                for _ in range(share(total, now - 1, at), share(total, now, at)):
                    next(work)

            for slot in range(SLOTS):
                for place in range(SUB):
                    if has_max:
                        max_work(SUB * slot + place)
                    if place == 0 and has_att:
                        att_work(slot)
                    if place == 1 and not late_last:
                        advance(0, slot)
                    if place == 2:
                        advance(2, slot)
                        if late_last:
                            advance(0, slot)
                        loads(slot)
                    advance(1, slot, place, SUB)
            tail()
            assert all(next(work, None) is None for work, _, _ in chains)

        block = ctx.enter_context(nc.Block())

        @block.sync
        def _(sp):
            def wt(w):
                return w.rearrange("(k p) n -> p k n", p=P)

            def row(v):
                return v.partition_broadcast(P)

            def load_x(p):
                sp.dma_start(pre_x[:, :, :], t["x"].rearrange("b s d -> (b s) d").rearrange(
                    "(c i p) d -> c p i d", i=TT, p=P)[p]).then_inc(a_x, 16)

            for sem_ in loop_sems:
                sp.sem_inc(sem_, ON)
            load_x(0)
            at = 0
            for name in VECTORS:
                rows = t[name].shape[0] // P
                sp.dma_start(cols_n[at:at + rows, :], t[name].rearrange("(k p) -> k p", p=P)).then_inc(s_load, 16)
                at += rows
            for dst, name in ((wq1, "Wq1"), (wkv1, "Wkv1")):
                sp.dma_start(dst[:, :, :], wt(t["L0_xattn_" + name])).then_inc(s_load, 16)
            loads = [
                (ctx_n, t["ctx_1024"].rearrange("b (a p) d -> p (b a) d", p=CT)),
                (wkv2, wt(t["L0_xattn_Wkv2"])),
                (wl_n[0], wt(t["L1_xattn_Wq"])), (wl_n[1], wt(t["L1_xattn_Wk"])), (wl_n[2], wt(t["L1_xattn_Wv"])),
                (bvl[:, :], row(t["L1_xattn_bv"])),
                (wo1[:, :, :], wt(t["L0_xattn_Wo1"])), (wq2[:, :, :], wt(t["L0_xattn_Wq2"])),
                (wo2[:, :, :], wt(t["L0_xattn_Wo2"])), (wff1[:, :, :], wt(t["L0_xattn_Wff1"])),
                (wff2[:, :, :], wt(t["L0_xattn_Wff2"])),
                (bo1[:, :], row(t["L0_xattn_bo1"])), (bo2[:, :], row(t["L0_xattn_bo2"])),
                (bff2[:, :], row(t["L0_xattn_bff2"])),
            ]
            assert len(loads) == N_REST
            for dst, src in loads:
                sp.dma_start(dst, src).then_inc(s_load2, 16)

            def context():
                sp.wait_ge(s_k2hi, 4)
                sp.wait_ge(s_k2mid, 4)
                sp.wait_ge(s_k2lo, 4)
                for i in range(3):
                    sp.dma_start(k2_s.rearrange("(p t) b n -> t p (b n)", t=3)[PART_AT[1][i]],
                                 k2_part[i].rearrange("p b k n -> p (b k n)")).then_inc(s_store, 16)
                sp.wait_ge(s_kpb, 4)
                sp.dma_start(kp_s.rearrange("(k p) n -> p k n", p=P), kp_all[:, :, :]).then_inc(s_store, 16)
                sp.wait_ge(s_v2c, NCT)
                sp.dma_start(v2_s.rearrange("(c p) n -> p c n", p=CT), v2_all).then_inc(s_store, 16)
                sp.wait_ge(s_vpb, NCT)
                sp.dma_start(vp_s.rearrange("(c p) n -> p c n", p=CT), vp_all).then_inc(s_store, 16)
                sp.wait_ge(s_store, 6 * 16)

            def wait(of, count):
                sp.wait_ge(of, count)
                sp.sem_inc(p_sp, 1)

            def pre(p):
                for _ in range(4):
                    yield
                wait(a_T, ON + p + 1)
                load_x((p + 1) % NCH)
                for _ in range(3):
                    yield
                b, c = within(p // (S // CH), B - 1), p % (S // CH)
                for kind in range(2):
                    wait(a_lo[kind], ON + p + 1)
                    sp.dma_start(parts_s[kind].rearrange("(b p t) k (c s) -> b c p (t k) s", b=B, p=P, s=CH)[b, c],
                                 qk_parts[kind][:, :, :].rearrange("p t (k s) -> p (t k) s", k=KD)).then_inc(a_qkst, 16)
                wait(a_vc, ON + p + 1)
                sp.dma_start(v_s.rearrange("(c i p) n -> c p i n", i=TT, p=P)[p],
                             v_sb[:, :, :, :].rearrange("p i h w -> p i (h w)")).then_inc(a_vst, 16)
                yield

            def load_stacks(m, par):
                b, k, a = within(m // G, B - 1), (m % G) // 2, m % 2
                wait(a_qkst, ON + (b + 1) * (S // CH) * 32)
                wait(a_vst, ON + (b + 1) * (S // CH) * 16)
                later = not isinstance(m, int) or m >= 2
                if later:
                    wait(g_s, ON + (m - 1) * 64)
                for kind, stack in ((0, qst), (1, kst)):
                    sp.dma_start(stack[par][0:3 * DH, :, :], parts_s[kind].rearrange(
                        "(b a j x) k s -> b a k x j s", b=B, a=2, j=G)[b, a, k]).then_inc(g_stack, 16)
                    for i, part in enumerate(STACK[kind]):
                        sp.dma_start(stack[par][(3 + i) * DH:(4 + i) * DH, :, :], parts_s[kind].rearrange(
                            "(b a j d t) k s -> b a k t d j s", b=B, a=2, j=G, t=3)[b, a, k, part]
                                     ).then_inc(g_stack, 16)
                if later:
                    wait(g_av, ON + (m - 1) * STEPS)
                src = v_s.rearrange("(b k p) (g n) -> b g p k n", b=B, p=P, g=H // G)
                sp.dma_start(vg[par][:, :, :], src[b, m % G]).then_inc(g_stack, 16)

            def packed(which, rows):
                return (rows.rearrange("(r w) (c s) -> r c w s", w=W, c=P // H)[:, :, DH, :],
                        den_c[which][:, :])

            def load_den(which, rows):
                dram, tile = packed(which, rows)
                sp.dma_start(tile, dram).then_inc(c_den[which], 16)

            def store_inv(which, rows):
                dram, tile = packed(which, rows)
                sp.dma_start(dram, tile).then_inc(c_inv[which], 16)

            def load_sums(dst, rows, done):
                for k in range(KD):
                    sp.dma_start(dst[:, k, :], rows.rearrange("(k h w) s -> k h w s", k=KD, w=W)[k, :, 0:DH, :]
                                 ).then_inc(done, 16)

            def load_inv(dst, rows, done):
                for k in range(KD):
                    sp.dma_start(dst[:, k, :], rows.rearrange("(k h w) s -> k h w s", k=KD, w=W)[
                        k, :, DH:DH + 1, :].to_broadcast([P // DH, DH, CH])).then_inc(done, 16)

            def mid(o, has_pre):
                b, c = within(o // (S // CH), B - 1), o % (S // CH)
                wait(c_q2, ON + o)
                wait(c_x[0], ON + o)
                sp.dma_start(x0[:, :, :], t["x"].rearrange("b s d -> (b s) d").rearrange(
                    "(c i p) d -> c p i d", i=TT, p=P)[o]).then_inc(c_x0, 16)
                for i in range(QH):
                    wait(g_ost[i], ON + (o // (S // CH) + 1) * (H // G) * 16)
                rows = o1_s.rearrange("(b r) (c s) -> b c r s", b=B, s=CH)[b, c]
                load_den(0, rows)
                load_sums(oT, rows, c_in)
                yield
                wait(c_rd[0], ON + o + 1)
                store_inv(0, rows)
                yield
                wait(c_inv[0], ON + (o + 1) * 16)
                load_inv(den, rows, c_in)
                for _ in range(MID_STEPS - 3):
                    yield
                wait(c_q2lo, ON + o + 1)
                sp.dma_start(q2_s.rearrange("(o p t) k s -> o p (t k s)", p=P, t=3)[o],
                             q2_parts[:, :, :].rearrange("p t n -> p (t n)")).then_inc(c_q2st, 16)
                yield

            def load_cross(o):
                b = within(o // (S // CH), B - 1)
                wait(c_s, ON + o * H)
                wait(c_q2st, ON + (o + 1) * 16)
                q2, k2 = [x.rearrange("x (e k) s -> x e (k s)", k=KD) for x in (q2st, k2st[:, :, :])]
                sp.dma_start(q2[0:3 * DH, :, :], q2_s.rearrange("(o e x) k s -> o x e (k s)", o=NCH, e=H // KD)[o]
                             ).then_inc(c_q2stack, 16)
                sp.dma_start(k2[0:3 * DH, :, :], k2_s.rearrange("(e x) b n -> b x e n", e=H // KD)[b]
                             ).then_inc(c_kv, 16)
                for i in range(3):
                    rows = slice((3 + i) * DH, (4 + i) * DH)
                    sp.dma_start(q2[rows, :, :], q2_s.rearrange(
                        "(o e d t) k s -> o t d e (k s)", o=NCH, e=H // KD, t=3)[o, STACK[0][i]]
                                 ).then_inc(c_q2stack, 16)
                    sp.dma_start(k2[rows, :, :], k2_s.rearrange(
                        "(e d t) b n -> b t d e n", e=H // KD, t=3)[b, STACK[1][i]]).then_inc(c_kv, 16)
                wait(c_av, ON + o * 4)
                sp.dma_start(v2[:, :, :], v2_s.rearrange("(b a p) n -> b p a n", b=B, p=CT)[b]).then_inc(c_kv, 16)

            def cross(o):
                for _ in range(14):
                    yield
                wait(c_slo, ON + o + 1)
                for row_, part in ((ROWS, sh2_hi), (ROWS + 1, sh2_lo)):
                    sp.dma_start(q2st[row_:row_ + 1, :, :].rearrange("a h (i p) -> a (h i) p", i=TT),
                                 part[:, :]).then_inc(c_shl, 16)
                for _ in range(11):
                    yield
                store_o2(o, 0)
                for _ in range(10):
                    yield
                store_o2(o, 1)
                yield

            def store_o2(o, e):
                wait(c_o, ON + o * 4 + 2 * e + 2)
                sp.dma_start(o2_s.rearrange("(o e g p) s -> o e p g s", e=2, g=2, p=P)[o, e],
                             o2_sb[:, e, :].rearrange("p (g s) -> p g s", g=2)).then_inc(c_ost, 16)

            def o2_rows(o):
                return o2_s.rearrange("(o r) s -> o r s", o=NCH)[o]

            def load_last_den(o):
                wait(c_ost, ON + (o + 1) * 32)
                load_den(1, o2_rows(o))

            def store_last_inv(o):
                wait(c_rd[1], ON + o + 1)
                store_inv(1, o2_rows(o))

            def load_last(o):
                wait(c_s3, ON + o)
                load_sums(oT2, o2_rows(o), c_o2)
                sp.dma_start(kpT[:, :, :], kp_s.rearrange("(k p) (b n) -> b p k n", p=P, b=B)[
                    within(o // (S // CH), B - 1)]).then_inc(c_o2, 16)

            def load_last_inv(o):
                wait(c_qp, ON + o)
                wait(c_inv[1], ON + (o + 1) * 16)
                load_inv(den2, o2_rows(o), c_o2)
                wait(c_av3, ON + o)
                sp.dma_start(vp[:, :, :], vp_s.rearrange("(b a p) n -> b p a n", b=B, p=CT)[
                    within(o // (S // CH), B - 1)]).then_inc(c_o2, 16)

            def last(o):
                for _ in range(LAST_STEPS - 1):
                    yield
                wait(c_out, ON + (o + 1) * 2)
                sp.dma_start(out.rearrange("b s d -> (b s) d").rearrange(
                    "(c i p) d -> c p i d", i=TT, p=P)[o], xb[:, :, :]).then_inc(c_outst, 16)
                yield

            def body(n, u, flags, att_before, after):
                has_max, has_att = flags[1:3]
                grp, m = n - ATT_LAG, n - MAX_LAG

                def store_o(group, qh):
                    wait(g_o, ON + group * QH + qh + 1)
                    sp.dma_start(o1_s.rearrange("(m p) (q s) -> m q p s", p=P, q=QH)[group, qh],
                                 o_sb[:, qh, :]).then_inc(g_ost[qh], 16)

                if has_max:
                    load_stacks(m, u)
                if att_before:
                    store_o(grp - 1, 1)

                def max_work(at):
                    if at == SUB * MAX_TURN:
                        wait(g_slo, ON + m + 1)
                        for row_, part in ((ROWS, sh_hi), (ROWS + 1, sh_lo)):
                            sp.dma_start(qst[u][row_:row_ + 1, :, :].rearrange("a j (q p) -> a (j q) p", p=P),
                                         part[:, :]).then_inc(g_shl, 16)

                def att_work(slot):
                    if slot == SLOTS // 2 + 2:
                        store_o(grp, 0)

                def loads(slot):
                    if after[4] and slot == CROSS_LOAD:
                        load_cross(n + 1 - CROSS_LAG)
                    if after[5]:
                        for at, step in ((DEN_LOAD, load_last_den), (DEN_INV, store_last_inv),
                                         (LAST_LOAD, load_last), (SLOTS - 1, load_last_inv)):
                            if slot == at:
                                step(n + 1 - LAST_LAG)

                walk(n, flags, pre, mid, cross, last, att_work, max_work, lambda: None, loads)

            run(sp, body, SEGMENTS[:1])
            context()
            run(sp, body, SEGMENTS[1:])
            sp.wait_ge(c_outst, ON + NCH * 16)

        @block.gpsimd
        def _(pool):
            nc.gpsimd.memset(ident[:, :], 0.0).then_inc(s_const, 1)
            pool.wait_ge(s_const, 1)
            nc.gpsimd.affine_select(out=ident[:, :], in_=ident[:, :], compare_op=ALU.not_equal, fill=1.0, base=0,
                                    pattern=[[-1, P]], channel_multiplier=1).then_inc(s_const, 1)
            nc.gpsimd.memset(neghalf[:, :], -0.5).then_inc(s_const, 1)
            v = v_sb[:, :, :, :]
            nc.gpsimd.memset(v, 0.0).then_inc(s_const, 1)
            pool.wait_ge(s_const, 4)
            nc.gpsimd.memset(v[:, :, :, DH:DH + 1], 1.0).then_inc(s_const, 1)
            def context():
                nc.gpsimd.memset(v2_all, 0.0).then_inc(s_zero, 1)
                pool.wait_ge(s_zero, 1)
                nc.gpsimd.memset(v2_all.rearrange("p c (h w) -> p (c h) w", w=W)[:, :, DH:DH + 1], 1.0).then_inc(s_zero, 1)
                pool.wait_ge(s_cols, 1)
                nc.gpsimd.tensor_scalar(b_tanh[:, :], bff1[:, FM:2 * FM], GELU_A / 2, 0.0, ALU.mult, ALU.add).then_inc(s_bias, 1)
                nc.gpsimd.tensor_scalar(b_half[:, :], bff1[:, FM:2 * FM], 0.5, 0.0, ALU.mult, ALU.add).then_inc(s_bias, 1)
                for f in range(4):
                    k, bs = f // 2, slice((f % 2) * B // 2, (f % 2 + 1) * B // 2)
                    pool.wait_ge(s_k2rest, f + 1)
                    nc.gpsimd.tensor_copy(k2_part[1][:, bs, k, :], k2_rest[:, f % 2, :, :]).then_inc(s_k2mid, 1)
                    pool.wait_ge(s_k2mid, f + 1)
                    nc.gpsimd.tensor_tensor(k2_part[2][:, bs, k, :], k2_rest[:, f % 2, :, :],
                                            k2_part[1][:, bs, k, :], ALU.subtract).then_inc(s_k2lo, 1)

            def rstd(mean_var, var_eps, rstd_, ready, eps_done, done, count):
                pool.wait_ge(ready, ON + count * 2)
                pool.sem_inc(p_pool, 1)
                nc.gpsimd.tensor_scalar(var_eps[:, :], mean_var[:, :, 1], EPS, 0.0, ALU.add, ALU.add).then_inc(eps_done, 1)
                pool.wait_ge(eps_done, ON + count)
                nc.gpsimd.tensor_tensor(rstd_[:, :], var_eps[:, :], neghalf[:, :], ALU.pow).then_inc(done, 1)

            def parts(x, part, at, copied, hi_ready, rest_ready, mid_ready, lo_ready, count):
                hi, mid, lo = [part[:, i, :] for i in at]
                pool.wait_ge(hi_ready, ON + count)
                pool.wait_ge(copied, ON + count)
                nc.gpsimd.tensor_tensor(x[:, :], x[:, :], hi, ALU.subtract).then_inc(rest_ready, 1)
                pool.wait_ge(rest_ready, ON + count)
                pool.sem_inc(p_pool, 1)
                nc.gpsimd.tensor_copy(mid, x[:, :]).then_inc(mid_ready, 1)
                pool.wait_ge(mid_ready, ON + count)
                nc.gpsimd.tensor_tensor(lo, x[:, :], mid, ALU.subtract).then_inc(lo_ready, 1)

            def pre(p):
                yield
                rstd(pre_mv, pre_ve, pre_rs, a_mv, a_ve, a_rs, p + 1)
                for _ in range(3):
                    yield
                pool.wait_ge(a_qkst, ON + p * 32)
                for i in range(2):
                    parts(qk_f[i], qk_parts[i], PART_AT[i], a_f[i], a_hi[i], a_rest[i], a_mid[i], a_lo[i], p + 1)
                    yield
                for _ in range(2):
                    yield

            def add_bias(dst, x, bias, done):
                for i in range(TT):
                    last = nc.gpsimd.tensor_tensor(dst[:, i, :], x[:, i, :], bias[:, :], ALU.add)
                last.then_inc(done, 1)

            def mid(o, has_pre):
                yield
                pool.wait_ge(c_x0, ON + (o + 1) * 16)
                add_bias(x0, x0, bo1, c_xb[0])
                for _ in range(3):
                    yield
                rstd(mv[0], ve[0], rs[0], c_mv[0], c_ve[0], c_rs[0], o + 1)
                for _ in range(3):
                    yield
                pool.wait_ge(c_q2st, ON + o * 16)
                parts(q2_f, q2_parts, PART_AT[0], c_q2f, c_q2hi, c_q2rest, c_q2mid, c_q2lo, o + 1)
                yield
                yield

            def cross(o):
                for _ in range(CROSS_STEPS):
                    yield

            def last_by(u):
                def last(o):
                    pool.wait_ge(c_outst, ON + o * 16)
                    add_bias(xb, x1[u], bo2, c_xb[1])
                    for _ in range(4):
                        yield
                    rstd(mv[1], ve[1], rs[1], c_mv[1], c_ve[1], c_rs[1], o + 1)
                    yield
                    pool.wait_ge(c_x[1], ON + o + 1)
                    add_bias(xb, x2, bff2, c_xb[2])
                    for _ in range(LAST_STEPS - 5):
                        yield
                return last

            def body(n, u, flags, att_before, after):
                walk(n, flags, pre, mid, cross, last_by(1 - u), lambda slot: None, lambda at: None, lambda: None,
                     late_last=True)

            run(pool, body, SEGMENTS[:1])
            context()
            run(pool, body, SEGMENTS[1:])

        @block.scalar
        def _(act):
            act.wait_ge(s_colT, 1)
            nc.scalar.copy(cols[:, :], ps_o[:, 0:2 * FM + 8 * KD]).then_inc(s_cols, 1)
            act.wait_ge(s_cols, 1)
            act.wait_ge(s_const, 5)

            def context():
                for c in range(NCT):
                    act.wait_ge(s_ct, c + 1)
                    for k in range(KD):
                        copied = nc.scalar.copy(ctxT[k][:, c * CT:(c + 1) * CT], ps_w[c % 3][:, k * P:k * P + CT])
                    copied.then_inc(s_ctT, 1)
                for w in range(3):
                    act.wait_ge(s_wt, w + 1)
                    nc.scalar.copy(wlT[:, w, :, :].rearrange("p k n -> p (k n)"), ps_w[w][:, :]).then_inc(s_wlT, 1)
                half = B * CTX // 2
                for f in range(4):
                    k, span = f // 2, slice((f % 2) * half, (f % 2 + 1) * half)
                    bs = slice((f % 2) * B // 2, (f % 2 + 1) * B // 2)
                    act.wait_ge(s_k2, f + 1)
                    nc.scalar.copy(k2_part[0][:, bs, k, :], ps_s[f % 2][:, 0:half].rearrange("p (b n) -> p b n", n=CTX)
                                   ).then_inc(s_k2hi, 1)
                    act.wait_ge(s_kp, f + 1)
                    nc.scalar.activation(kp_all[:, k, span], ps_w[f % 2][:, 0:half], ACT.Identity,
                                         bias=bkl[:, k:k + 1]).then_inc(s_kpb, 1)
                act.wait_ge(s_zero, 2)
                for c in range(NCT):
                    act.wait_ge(s_v2, c + 1)
                    nc.scalar.copy(v2_all[:, c, :].rearrange("p (h w) -> p h w", w=W)[:, :, 0:DH],
                                   ps_w[c % 3][0:CT, 0:D].rearrange("p (h d) -> p h d", d=DH)).then_inc(s_v2c, 1)
                act.wait_ge(s_bias, 2)

            def affine(dst, src, layer, done):
                for k in range(KD):
                    nc.scalar.activation(dst[:, k, :], src[:, k * CH:(k + 1) * CH], ACT.Identity,
                                         scale=ln_s[:, layer, k:k + 1], bias=ln_b[:, layer, k:k + 1]).then_inc(done, 1)

            def pre(p):
                for _ in range(3):
                    yield
                act.wait_ge(a_T, ON + p + 1)
                affine(pre_yT, ps_pre, 0, a_y)
                yield
                for i in range(2):
                    act.wait_ge(a_p[i], ON + p + 1)
                    act.wait_ge(a_lo[i], ON + p)
                    act.wait_ge(a_qkst, ON + p * 32)
                    nc.scalar.copy(qk_parts[i][:, PART_AT[i][0], :], ps_pre[:, :]).then_inc(a_hi[i], 1)
                    nc.scalar.copy(qk_f[i][:, :], ps_pre[:, :]).then_inc(a_f[i], 1)
                    yield
                act.wait_ge(a_vst, ON + p * 16)
                act.wait_ge(a_v, ON + p + 1)
                nc.scalar.copy(v_sb[:, :, :, 0:DH].rearrange("p i h d -> p (i h) d"),
                               ps_pre[:, :].rearrange("p (n d) -> p n d", d=DH)).then_inc(a_vc, 1)
                yield
                yield

            def mid(o, has_pre):
                for _ in range(6):
                    yield
                act.wait_ge(c_T[0], ON + o + 1)
                affine(oT, ps_pre, 1, c_y[0])
                yield
                act.wait_ge(c_q2, ON + o + 1)
                act.wait_ge(c_q2lo, ON + o)
                act.wait_ge(c_q2st, ON + o * 16)
                nc.scalar.copy(q2_parts[:, PART_AT[0][0], :], ps_pre[:, :]).then_inc(c_q2hi, 1)
                nc.scalar.copy(q2_f[:, :], ps_pre[:, :]).then_inc(c_q2f, 1)
                yield
                yield

            def cross_by(spare):
                def cross(o):
                    for _ in range(16):
                        yield
                    for h in range(H):
                        act.wait_ge(c_s, ON + o * H + h + 1)
                        act.wait_ge(c_av, ON + o * 4 + max(0, h // G - 1))
                        nc.scalar.activation(probs2[:, h % 8, :], cross_banks[spare][h % 2][0:CT, :], ACT.Exp,
                                             scale=SCALE).then_inc(c_e, 1)
                        yield
                        if h % G == 0 and h or h == H - 1:
                            g = max(0, h - 1) // G
                            if g == 0:
                                act.wait_ge(c_ost, ON + o * 32)
                            act.wait_ge(c_av, ON + o * 4 + g + 1)
                            nc.scalar.copy(o2_sb[:, g // 2, (g % 2) * CH:(g % 2 + 1) * CH],
                                           ps_cross[:, 0:CH]).then_inc(c_o, 1)
                            yield
                return cross

            def last_by(spare):
                def last(o):
                    for _ in range(6):
                        yield
                    act.wait_ge(c_T[1], ON + o + 1)
                    affine(den2, ps_last, 2, c_y[1])
                    yield
                    for m in range(FM):
                        bank = last_banks[spare][m % 2]
                        act.wait_ge(c_f1, ON + o * FM + m + 1)
                        act.wait_ge(c_h, ON + o * FM + max(0, m - 1))
                        nc.scalar.activation(th[:, m % 2, :], bank[:, CH:2 * CH], ACT.Tanh, scale=GELU_A / 2,
                                             bias=b_tanh[:, m:m + 1]).then_inc(c_th, 1)
                        nc.scalar.activation(gb[:, m % 2, :], bank[:, CH:2 * CH], ACT.Identity, scale=0.5,
                                             bias=b_half[:, m:m + 1]).then_inc(c_gb, 1)
                        yield
                    for _ in range(5):
                        yield
                    act.wait_ge(c_T[2], ON + o + 1)
                    nc.scalar.copy(den2[:, :, :].rearrange("p k s -> p (k s)"), ps_last[:, :]).then_inc(c_y[2], 1)
                    yield
                    act.wait_ge(c_qp, ON + o + 1)
                    for k in range(KD):
                        nc.scalar.activation(oT2[:, k, :], ps_last[:, k * CH:(k + 1) * CH], ACT.Identity,
                                             bias=bql[:, k:k + 1]).then_inc(c_qpb, 1)
                    yield
                    yield
                    act.wait_ge(c_nm3, ON + o + 1)
                    for i in range(TT):
                        nc.scalar.activation(p3[:, i, :], ps_last[:, i * CH:i * CH + CTX], ACT.Exp,
                                             bias=nm3[:, i:i + 1], accum_out=sum3[:, i:i + 1]).then_inc(c_e3, 1)
                    yield
                    act.wait_ge(c_pT, ON + o + 1)
                    nc.scalar.copy(p3T[:, :, :].rearrange("p a s -> p (a s)"), ps_last[0:CT, :]).then_inc(c_pTc, 1)
                    yield
                    yield
                    yield
                return last

            def body(n, u, flags, att_before, after):
                grp = n - ATT_LAG

                def exp_tile(c, j):
                    act.wait_ge(g_s, ON + grp * 64 + c * G + j + 1)
                    act.wait_ge(g_av, ON + grp * STEPS + max(0, c - 1))
                    nc.scalar.activation(probs[:, c % 2, j, :], ps_s[j % 2][:, :], ACT.Exp, scale=SCALE).then_inc(g_e, 1)

                def o_copy(qh):
                    act.wait_ge(g_av, ON + grp * STEPS + (qh + 1) * KT)
                    act.wait_ge(g_ost[qh], ON + grp * 16)
                    nc.scalar.copy(o_sb[:, qh, :], ps_o[:, :]).then_inc(g_o, 1)

                def att_work(slot):
                    c, pair = divmod(slot, 2)
                    exp_tile(c, 2 * pair)
                    exp_tile(c, 2 * pair + 1)
                    if slot == SLOTS // 2:
                        o_copy(0)

                def tail():
                    if flags[2]:
                        o_copy(1)

                walk(n, flags, pre, mid, cross_by(not flags[2]), last_by(not flags[2]), att_work, lambda at: None, tail)

            run(act, body, SEGMENTS[:1])
            context()
            run(act, body, SEGMENTS[1:])

        @block.vector
        def _(dve):
            for tile in (kst[0], kst[1], k2st):
                nc.vector.memset(tile[ROWS:ROWS + SHIFT, :, :], 1.0).then_inc(s_ones, 1)
            def context():
                dve.wait_ge(s_load2, N_REST * 16)
                dve.wait_ge(s_cols, 1)
                half = B * CTX // 2
                for f in range(4):
                    k, bs = f // 2, slice((f % 2) * B // 2, (f % 2 + 1) * B // 2)
                    dve.wait_ge(s_k2hi, f + 1)
                    if f >= 2:
                        dve.wait_ge(s_k2lo, f - 1)
                    nc.vector.tensor_tensor(k2_rest[:, f % 2, :, :], ps_s[f % 2][:, 0:half].rearrange(
                        "p (b n) -> p b n", n=CTX), k2_part[0][:, bs, k, :], ALU.subtract).then_inc(s_k2rest, 1)
                for c in range(NCT):
                    dve.wait_ge(s_v2c, c + 1)
                    nc.vector.tensor_tensor(vp_all[:, c, :], ps_w[c % 3][0:CT, D:2 * D], bvl[0:CT, :],
                                            ALU.add).then_inc(s_vpb, 1)

            def stats(x, stat, mean_var, stat_done, mv_done, base):
                for i in range(TT):
                    nc.vector.bn_stats(stat[:, i, :], x[:, i, :]).then_inc(stat_done, 1)
                dve.wait_ge(stat_done, ON + base + TT)
                dve.sem_inc(p_dve, 1)
                for i in range(TT):
                    nc.vector.bn_aggr(mean_var[:, i, :], stat[:, i, :]).then_inc(mv_done, 1)

            def normalise(dst, x, mean_var, rstd_, done):
                for i in range(TT):
                    nc.vector.tensor_scalar(dst[:, i, :], x[:, i, :], mean_var[:, i, 0:1], rstd_[:, i:i + 1],
                                            ALU.subtract, ALU.mult).then_inc(done, 1)

            def pre(p):
                yield
                dve.wait_ge(a_x, ON + (p + 1) * 16)
                stats(pre_x, pre_st, pre_mv, a_st, a_mv, p * 2)
                yield
                dve.wait_ge(a_rs, ON + p + 1)
                normalise(pre_x, pre_x, pre_mv, pre_rs, a_xn)
                for _ in range(6):
                    yield

            def invert(which, o):
                dve.wait_ge(c_den[which], ON + (o + 1) * 16)
                nc.vector.reciprocal(den_c[which][:, :], den_c[which][:, :]).then_inc(c_rd[which], 1)

            def norm_o(which, sums, invs):
                o_flat = sums[:, :, :].rearrange("p k s -> p (k s)")
                nc.vector.tensor_tensor(o_flat, o_flat, invs[:, :, :].rearrange("p k s -> p (k s)"),
                                        ALU.mult).then_inc(c_on[which], 1)

            def residual(which, dst, bank, x, o):
                dve.wait_ge(c_xb[which], ON + o + 1)
                nc.vector.tensor_tensor(dst[:, :, :].rearrange("p i d -> p (i d)"), bank[:, :],
                                        x[:, :, :].rearrange("p i d -> p (i d)"), ALU.add).then_inc(c_x[which], 1)
                dve.wait_ge(c_x[which], ON + o + 1)

            def mid_by(u, has_last):
                def mid(o, has_pre):
                    yield
                    invert(0, o)
                    yield
                    yield
                    dve.wait_ge(c_in, ON + (o + 1) * 64)
                    norm_o(0, oT, den)
                    yield
                    dve.wait_ge(c_wo[0], ON + o + 1)
                    if has_last:
                        dve.wait_ge(c_xb[1], ON + o - LAST_LAG + MID_LAG + 1)
                    residual(0, x1[u], ps_pre, x0, o)
                    stats(x1[u], st[0], mv[0], c_st[0], c_mv[0], o * 2)
                    yield
                    dve.wait_ge(c_rs[0], ON + o + 1)
                    normalise(den_rows, x1[u], mv[0], rs[0], c_xn[0])
                    for _ in range(4):
                        yield
                return mid

            def cross_by(spare):
                def cross(o):
                    yield
                    for f in range(2 * Q2F):
                        i, h0, nh = q2_heads(f)
                        dve.wait_ge(c_mt, ON + o * 2 * Q2F + f + 1)
                        nc.vector.tensor_reduce(mx2[:, h0:h0 + nh, i], cross_banks[spare][f % 2][:, 0:nh * CTX].rearrange(
                            "p (h n) -> p h n", h=nh), AX_X, ALU.max).then_inc(c_mx, 1)
                        yield
                    dve.wait_ge(c_mT, ON + o + 1)
                    negative(ps_cross[0:H * TT, 0:P], sh2_hi, sh2_lo, c_shi, c_slo, o + 1)
                    for _ in range(CROSS_STEPS - 13):
                        yield
                return cross

            def last_by(spare):
                def last(o):
                    yield
                    yield
                    dve.wait_ge(c_o2, ON + (o + 1) * 96)
                    norm_o(1, oT2, den2)
                    yield
                    yield
                    dve.wait_ge(c_wo[1], ON + o + 1)
                    residual(1, x2, ps_last, xb, o)
                    stats(x2, st[1], mv[1], c_st[1], c_mv[1], o * 2)
                    yield
                    dve.wait_ge(c_rs[1], ON + o + 1)
                    normalise(oT2_rows, x2, mv[1], rs[1], c_xn[1])
                    yield
                    yield
                    for m in range(FM):
                        dve.wait_ge(c_th, ON + o * FM + m + 1)
                        dve.wait_ge(c_gb, ON + o * FM + m + 1)
                        nc.vector.scalar_tensor_tensor(th[:, m % 2, :], th[:, m % 2, :], 1.0, gb[:, m % 2, :],
                                                       ALU.add, ALU.mult).then_inc(c_gt, 1)
                        dve.wait_ge(c_gt, ON + o * FM + m + 1)
                        nc.vector.scalar_tensor_tensor(hT[:, m, :], last_banks[spare][m % 2][:, 0:CH], bff1[:, m:m + 1],
                                                       th[:, m % 2, :], ALU.add, ALU.mult).then_inc(c_h, 1)
                        yield
                    for _ in range(4):
                        yield
                    dve.wait_ge(c_f2, ON + o + 1)
                    residual(2, x2, ps_last, xb, o)
                    yield
                    yield
                    yield
                    dve.wait_ge(c_s3, ON + o + 1)
                    nc.vector.tensor_reduce(mx3[:, :], ps_last[:, :].rearrange("p (i n) -> p i n", i=TT)[:, :, 0:CTX],
                                            AX_X, ALU.max).then_inc(c_mx3, 1)
                    dve.wait_ge(c_mx3, ON + o + 1)
                    nc.vector.tensor_scalar(nm3[:, :], mx3[:, :], -1.0, None, ALU.mult).then_inc(c_nm3, 1)
                    yield
                    dve.wait_ge(c_e3, ON + (o + 1) * TT)
                    nc.vector.reciprocal(inv3[:, :], sum3[:, :]).then_inc(c_inv3, 1)
                    yield
                    yield
                    dve.wait_ge(c_inv3, ON + o + 1)
                    dve.wait_ge(c_av3, ON + o + 1)
                    for i in range(TT):
                        nc.vector.scalar_tensor_tensor(xb[:, i, :], ps_last[:, i * D:(i + 1) * D], inv3[:, i:i + 1],
                                                       x2[:, i, :], ALU.mult, ALU.add).then_inc(c_out, 1)
                    yield
                    yield
                return last

            def negative(src, hi, lo, hi_done, lo_done, count):
                nc.vector.tensor_scalar(hi[:, :], src, -1.0, None, ALU.mult).then_inc(hi_done, 1)
                dve.wait_ge(hi_done, ON + count)
                nc.vector.scalar_tensor_tensor(lo[:, :], src, -1.0, hi[:, :], ALU.mult, ALU.subtract).then_inc(lo_done, 1)

            def body(n, u, flags, att_before, after):
                m = n - MAX_LAG

                def max_work(at):
                    for i in range(max_tiles(at - 1), max_tiles(at)):
                        dve.wait_ge(g_mt, ON + m * 2 * PAIRS + i + 1)
                        nc.vector.tensor_reduce(mxh[:, i // 2, i % 2:i % 2 + 1], ps_max[i % 2][:, :], AX_X,
                                                ALU.max).then_inc(g_mx, 1)
                    if at == SUB * MAX_TURN - 1:
                        dve.wait_ge(g_mx, ON + (m + 1) * 2 * PAIRS)
                        nc.vector.tensor_reduce(mxq[:, :], mxh[:, :, :], AX_X, ALU.max).then_inc(g_mp, 1)
                    if at == SUB * MAX_TURN:
                        dve.wait_ge(g_mT, ON + m + 1)
                        dve.wait_ge(g_shl, ON + m * 32)
                        negative(ps_max[0][0:PAIRS, 0:P], sh_hi, sh_lo, g_shi, g_slo, m + 1)

                def inverses(slot):
                    if after[5] and slot == DEN_INV:
                        invert(1, n + 1 - LAST_LAG)

                walk(n, flags, pre, mid_by(1 - u, flags[5]), cross_by(not flags[2]), last_by(not flags[2]),
                     lambda slot: None, max_work, lambda: None, inverses, late_last=True)

            run(dve, body, SEGMENTS[:1])
            context()
            run(dve, body, SEGMENTS[1:])

        @block.tensor
        def _(pe):
            mm = nc.tensor.matmul
            pe.wait_ge(s_load, N_FIRST * 16)
            pe.wait_ge(s_const, 2)
            nc.tensor.transpose(ps_o[:, 0:2 * FM + 8 * KD], cols_n, ident[0:2 * FM + 8 * KD, 0:2 * FM + 8 * KD]
                                ).then_inc(s_colT, 1)
            pe.wait_ge(s_const, 5)

            def context():
                pe.wait_ge(s_load2, N_REST * 16)
                for c in range(NCT):
                    if c >= 3:
                        pe.wait_ge(s_ctT, c - 2)
                    for k in range(KD):
                        last = nc.tensor.transpose(ps_w[c % 3][:, k * P:k * P + CT], ctx_n[:, c, k * P:(k + 1) * P],
                                                   ident[0:CT, 0:CT])
                    last.then_inc(s_ct, 1)
                for w in range(3):
                    pe.wait_ge(s_ctT, NCT)
                    for kf in range(KD):
                        for kg in range(KD):
                            last = nc.tensor.transpose(ps_w[w][:, kf * D + kg * P:kf * D + (kg + 1) * P],
                                                       wl_n[w][:, kg, kf * P:(kf + 1) * P], ident[:, :])
                    last.then_inc(s_wt, 1)
                pe.wait_ge(s_wlT, 3)
                half = B * CTX // 2
                for f in range(4):
                    m, span = f // 2, slice((f % 2) * half, (f % 2 + 1) * half)
                    if f >= 2:
                        pe.wait_ge(s_k2rest, f - 1)
                    for k in range(KD):
                        last = mm(ps_s[f % 2][:, 0:half], wkv2[:, k, m * P:(m + 1) * P], ctxT[k][:, span],
                                  start=(k == 0), stop=(k == KD - 1))
                    last.then_inc(s_k2, 1)
                    if f >= 2:
                        pe.wait_ge(s_kpb, f - 1)
                    for k in range(KD):
                        last = mm(ps_w[f % 2][:, 0:half], wlT[:, 1, k, m * P:(m + 1) * P], ctxT[k][:, span],
                                  start=(k == 0), stop=(k == KD - 1))
                    last.then_inc(s_kp, 1)
                pe.wait_ge(s_kpb, 4)
                for c in range(NCT):
                    if c >= 3:
                        pe.wait_ge(s_vpb, c - 2)
                    for k in range(KD):
                        mm(ps_w[c % 3][0:CT, 0:D], ctxT[k][:, c * CT:(c + 1) * CT], wkv2[:, k, D:2 * D],
                           start=(k == 0), stop=(k == KD - 1))
                    for k in range(KD):
                        last = mm(ps_w[c % 3][0:CT, D:2 * D], ctxT[k][:, c * CT:(c + 1) * CT], wlT[:, 2, k, :],
                                  start=(k == 0), stop=(k == KD - 1))
                    last.then_inc(s_v2, 1)
                pe.wait_ge(s_vpb, NCT)
                pe.wait_ge(s_ones, 3)

            def turn(bank, x):
                for k in range(KD):
                    for i in range(TT):
                        last = nc.tensor.transpose(bank[:, k * CH + i * P:k * CH + (i + 1) * P],
                                                   x[:, i, k * P:(k + 1) * P], ident[:, :])
                return last

            def project(bank, w, y):
                for m in range(KD):
                    for k in range(KD):
                        last = mm(bank[:, m * CH:(m + 1) * CH], w[:, k, m * P:(m + 1) * P], y[:, k, :],
                                  start=(k == 0), stop=(k == KD - 1))
                return last

            def project_rows(bank, y, w):
                for i in range(TT):
                    for k in range(KD):
                        last = mm(bank[:, i * D:(i + 1) * D], y[:, k, i * P:(i + 1) * P], w[:, k, :],
                                  start=(k == 0), stop=(k == KD - 1))
                return last

            def pre_by(has_mid):
                def pre(p):
                    for _ in range(3):
                        yield
                    pe.wait_ge(a_vc, ON + p)
                    if has_mid:
                        pe.wait_ge(c_q2f, ON + p - MID_LAG)
                    pe.wait_ge(a_xn, ON + (p + 1) * 2)
                    turn(ps_pre, pre_x).then_inc(a_T, 1)
                    yield
                    pe.wait_ge(a_y, ON + (p + 1) * 2)
                    project(ps_pre, wq1, pre_yT).then_inc(a_p[0], 1)
                    yield
                    pe.wait_ge(a_f[0], ON + p + 1)
                    project(ps_pre, wkv1, pre_yT).then_inc(a_p[1], 1)
                    yield
                    pe.wait_ge(a_f[1], ON + p + 1)
                    project_rows(ps_pre, pre_yT, wkv1[:, :, D:2 * D]).then_inc(a_v, 1)
                    yield
                    yield
                return pre

            def mid(o, has_pre):
                for _ in range(3):
                    yield
                if has_pre:
                    pe.wait_ge(a_vc, ON + o + MID_LAG + 1)
                pe.wait_ge(c_q2f, ON + o)
                pe.wait_ge(c_on[0], ON + o + 1)
                project_rows(ps_pre, oT, wo1).then_inc(c_wo[0], 1)
                yield
                yield
                yield
                pe.wait_ge(c_xn[0], ON + (o + 1) * 2)
                turn(ps_pre, den_rows).then_inc(c_T[0], 1)
                yield
                pe.wait_ge(c_y[0], ON + (o + 1) * 2)
                project(ps_pre, wq2, oT).then_inc(c_q2, 1)
                yield
                yield

            def cross_by(spare):
                def cross(o):
                    yield
                    for f in range(2 * Q2F):
                        if f == 0:
                            pe.wait_ge(c_q2stack, ON + (o + 1) * 64)
                            pe.wait_ge(c_kv, ON + (o + 1) * 80)
                            pe.wait_ge(c_o, ON + o * 4)
                        else:
                            pe.wait_ge(c_mx, ON + o * 2 * Q2F + f - spare)
                        i, h0, nh = q2_heads(f)
                        for j in range(nh):
                            last = mm(cross_banks[spare][f % 2][:, j * CTX:(j + 1) * CTX], q2st[0:ROWS, h0 + j, i * P:(i + 1) * P],
                                      k2st[0:ROWS, h0 + j, :], start=True, stop=True)
                        last.then_inc(c_mt, 1)
                        yield
                    pe.wait_ge(c_mx, ON + (o + 1) * 2 * Q2F)
                    nc.tensor.transpose(ps_cross[0:H * TT, 0:P], mx2[:, :, :].rearrange("p h i -> p (h i)"),
                                        ident[:, :]).then_inc(c_mT, 1)
                    for _ in range(3):
                        yield
                    for h in range(H):
                        if h == 0:
                            pe.wait_ge(c_shl, ON + (o + 1) * 32)
                        elif h % G == 1 and h > 1 and not spare:
                            pe.wait_ge(c_o, ON + o * 4 + h // G)
                        else:
                            pe.wait_ge(c_e, ON + o * H + h - spare)
                        at = h % (H // KD) * KD + h // (H // KD)
                        for a in range(2):
                            last = mm(cross_banks[spare][h % 2][0:CT, a * CH:(a + 1) * CH], k2st[:, at, a * CT:(a + 1) * CT],
                                      q2st[:, at, :], start=True, stop=True)
                        last.then_inc(c_s, 1)
                        yield
                        if h % G == 0 and h or h == H - 1:
                            g = max(0, h - 1) // G
                            pe.wait_ge(c_e, ON + o * H + h + 1)
                            if spare:
                                pe.wait_ge(c_o, ON + o * 4 + g)
                            for a in range(2):
                                for j in range(G):
                                    i = G * g + j
                                    last = mm(ps_cross[j * W:(j + 1) * W, 0:CH],
                                              v2[:, a, i * W:(i + 1) * W], probs2[:, i % 8, a * CH:(a + 1) * CH],
                                              start=(a == 0), stop=(a == 1), tile_position=(0, j * W))
                            last.then_inc(c_av, 1)
                            yield
                return cross

            def last_by(spare):
                def last(o):
                    for _ in range(3):
                        yield
                    pe.wait_ge(c_on[1], ON + o + 1)
                    pe.wait_ge(c_out, ON + o * 2)
                    project_rows(ps_last, oT2, wo2).then_inc(c_wo[1], 1)
                    yield
                    yield
                    yield
                    pe.wait_ge(c_xn[1], ON + (o + 1) * 2)
                    turn(ps_last, oT2_rows).then_inc(c_T[1], 1)
                    yield
                    pe.wait_ge(c_y[1], ON + (o + 1) * 2)
                    for m in range(FM):
                        if m > spare:
                            pe.wait_ge(c_h, ON + o * FM + m - spare)
                        for part in range(2):
                            for k in range(KD):
                                last = mm(last_banks[spare][m % 2][:, part * CH:(part + 1) * CH],
                                          wff1[:, k, (part * FM + m) * P:(part * FM + m + 1) * P], den2[:, k, :],
                                          start=(k == 0), stop=(k == KD - 1))
                        last.then_inc(c_f1, 1)
                        yield
                    pe.wait_ge(c_h, ON + (o + 1) * FM)
                    for q in range(4):
                        i = q // 2
                        for m in range((q % 2) * FM // 2, (q % 2 + 1) * FM // 2):
                            last = mm(ps_last[:, i * D:(i + 1) * D], hT[:, m, i * P:(i + 1) * P], wff2[:, m, :],
                                      start=(m == 0), stop=(m == FM - 1))
                        if q == 3:
                            last.then_inc(c_f2, 1)
                        yield
                    yield
                    pe.wait_ge(c_x[2], ON + o + 1)
                    turn(ps_last, x2).then_inc(c_T[2], 1)
                    yield
                    pe.wait_ge(c_y[2], ON + o + 1)
                    project(ps_last, wlT[:, 0, :, :], den2).then_inc(c_qp, 1)
                    yield
                    pe.wait_ge(c_qpb, ON + (o + 1) * 2)
                    for i in range(TT):
                        for k in range(KD):
                            last = mm(ps_last[:, i * CH:i * CH + CTX], oT2[:, k, i * P:(i + 1) * P], kpT[:, k, :],
                                      start=(k == 0), stop=(k == KD - 1))
                    last.then_inc(c_s3, 1)
                    yield
                    yield
                    pe.wait_ge(c_e3, ON + (o + 1) * TT)
                    for a in range(2):
                        for i in range(TT):
                            last = nc.tensor.transpose(ps_last[0:CT, a * CH + i * P:a * CH + (i + 1) * P],
                                                       p3[:, i, a * CT:(a + 1) * CT], ident[:, :])
                    last.then_inc(c_pT, 1)
                    yield
                    pe.wait_ge(c_pTc, ON + o + 1)
                    for i in range(TT):
                        for a in range(2):
                            last = mm(ps_last[:, i * D:(i + 1) * D], p3T[:, a, i * P:(i + 1) * P], vp[:, a, :],
                                      start=(a == 0), stop=(a == 1))
                    last.then_inc(c_av3, 1)
                    yield
                    yield
                return last

            def body(n, u, flags, att_before, after):
                grp, m = n - ATT_LAG, n - MAX_LAG

                def max_work(at):
                    qs, ks = qst[u], kst[u]
                    for i in range(max_tiles(at - 1), max_tiles(at)):
                        j, q, k = i // 2 // NQ, i // 2 % NQ, i % 2
                        if i == 0:
                            pe.wait_ge(g_stack, ON + (m + 1) * 9 * 16)
                            pe.wait_ge(g_slo, ON + m)
                        pe.wait_ge(g_mx, ON + m * 2 * PAIRS + max(0, i - 1))
                        mm(ps_max[i % 2][:, :], qs[0:ROWS, j, q * P:(q + 1) * P],
                           ks[0:ROWS, j, k * 512:(k + 1) * 512], start=True, stop=True).then_inc(g_mt, 1)
                    if at == SUB * MAX_TURN:
                        pe.wait_ge(g_mp, ON + m + 1)
                        nc.tensor.transpose(ps_max[0][0:PAIRS, 0:P], mxq[:, :], ident[:, :]).then_inc(g_mT, 1)

                def scores(c, j):
                    qh, kt = divmod(c, KT)
                    if c == 0 and j == 0:
                        pe.wait_ge(g_shl, ON + (grp + 1) * 32)
                    pe.wait_ge(g_e, ON + grp * 64 + max(0, c * G + j - 1))
                    mm(ps_s[j % 2][:, :], kst[1 - u][:, j, kt * P:(kt + 1) * P],
                       qst[1 - u][:, j, qh * QW:(qh + 1) * QW], start=True, stop=True).then_inc(g_s, 1)

                def values(c):
                    qh, kt = divmod(c, KT)
                    pe.wait_ge(g_e, ON + grp * 64 + (c + 1) * G)
                    if kt == 0:
                        pe.wait_ge(g_o, ON + grp * QH + qh)
                    for j in range(G):
                        last = mm(ps_o[j * W:(j + 1) * W, :], vg[1 - u][:, kt, j * W:(j + 1) * W],
                                  probs[:, c % 2, j, :], start=(kt == 0), stop=(kt == KT - 1),
                                  tile_position=(0, j * W))
                    last.then_inc(g_av, 1)

                def att_work(slot):
                    c, pair = divmod(slot, 2)
                    scores(c, 2 * pair)
                    scores(c, 2 * pair + 1)
                    if pair == 0 and c > 0:
                        values(c - 1)

                def tail():
                    if flags[2]:
                        values(STEPS - 1)

                walk(n, flags, pre_by(flags[3]), mid, cross_by(not flags[2]), last_by(not flags[2]), att_work, max_work, tail)

            run(pe, body, SEGMENTS[:1])
            context()
            run(pe, body, SEGMENTS[1:])


VECTORS = ["L0_xattn_bff1"] + [f"L0_xattn_ln{i + 1}_{c}" for c in "sb" for i in range(3)] + [
    "L1_xattn_bq", "L1_xattn_bk"]
N_FIRST = len(VECTORS) + 2
N_REST = 14

_INS = ["x", "ctx_1024"] + ["L0_xattn_" + s for s in (
    "Wq1", "Wkv1", "Wo1", "bo1", "Wq2", "Wkv2", "Wo2", "bo2", "Wff1", "bff1", "Wff2", "bff2",
    "ln1_s", "ln1_b", "ln2_s", "ln2_b", "ln3_s", "ln3_b")] + ["L1_xattn_" + s for s in (
        "Wq", "bq", "Wk", "bk", "Wv", "bv")]


def kernel(**inputs):
    import numpy as _np
    import concourse.bacc as _bacc
    from concourse import mybir as _mybir
    from concourse.bass_utils import run_bass_kernel_spmd as _run

    nc = _bacc.Bacc("TRN2", target_bir_lowering=False, num_devices=1)
    arrays, tensors = {}, {}
    for name in _INS:
        a = _np.ascontiguousarray(inputs[name])
        arrays[f"in_{name}_dram"] = a
        tensors[name] = nc.dram_tensor(f"in_{name}_dram", a.shape, _mybir.dt.from_np(a.dtype),
                                       kind="ExternalInput").ap()
    out = nc.dram_tensor("out_dram", (B, S, D), _mybir.dt.from_np(_np.dtype("float32")), kind="ExternalOutput").ap()
    xattn_kernel(nc, tensors, out)
    r = _run(nc, [arrays], core_ids=[0])
    return r.results[0]["out_dram"]
```

```python
from contextlib import ExitStack

import concourse.bass as bass
from concourse import mybir

F32 = mybir.dt.float32
BF16 = mybir.dt.bfloat16
F32R = mybir.dt.float32r
ALU = mybir.AluOpType
ACT = mybir.ActivationFunctionType
AX_X = mybir.AxisListType.X

P = 128
B, S, D = 4, 1024, 256
H, DH = 16, 16
KD = D // P
CTX = 154
CT = CTX // 2
NCT = B * 2
CH = 256
TT = CH // P
NCH = B * S // CH
G = 4
W = P // G
NG = B * H // G
QH, QW = 2, 512
KT = S // P
STEPS = QH * KT
SLOTS = 2 * STEPS
NQ = S // P
PAIRS = G * NQ
FF = 4 * D
FM = FF // P
PR2 = 5
EPS = 1e-5
SCALE = 64 ** -0.5
GELU_A = 1.702

PART_AT = ((0, 1, 2), (2, 1, 0))
STACK = ((0, 1, 0), (1, 2, 2))
ROWS = 6 * DH
SHIFT = 2

MAX_LAG, ATT_LAG, MID_LAG, CROSS_LAG, LAST_LAG = 4, 5, 9, 10, 11
PRE_STEPS, MID_STEPS, CROSS_STEPS, LAST_STEPS = 8, 9, 36, 26
PRE_AT, CROSS_AT, LAST_AT = (1, 5, 22), (0, 0, 24), (1, 1, 32)
CROSS_LOAD, DEN_LOAD, DEN_INV, LAST_LOAD, V_LOAD = 26, 25, 27, 29, 8
SUB = 3
PV_PLACE, LAST_PLACE = 1, 1
MAX_FROM, MAX_MID, MAX_END, MAX_TURN = 5, 12, 29, 29
MAX_EARLY = 14


def stages(n):
    return (n < NCH,) + tuple(0 <= n - lag < NCH for lag in (MAX_LAG, ATT_LAG, MID_LAG, CROSS_LAG, LAST_LAG))


ON = 1
SEGMENTS = [(0, 4), (4, 6), (6, 8), (8, 10), (10, 12), (12, 16), (16, 20), (20, 22), (22, 24), (24, 26), (26, 27)]


def share(total, slot, at):
    if slot < at[0] or total == 0:
        return 0
    return 1 + min(total - 1, max(0, -(-(total - 1) * (slot + 1 - at[1]) // (at[2] - at[1]))))


def max_tiles(at):
    place = at + 1 - SUB * MAX_FROM
    early, late = SUB * (MAX_MID - MAX_FROM), SUB * (MAX_END - MAX_MID)
    if place <= early:
        return max(0, -(-MAX_EARLY * place // early))
    return min(2 * PAIRS, MAX_EARLY - (MAX_EARLY - 2 * PAIRS) * (place - early) // late)


def xattn_kernel(nc, t, out):
    ctx = ExitStack()
    with ctx:
        def sb(name, shape, dt=F32):
            return ctx.enter_context(nc.sbuf_tensor(name, shape, dt))

        def ps(name, shape):
            return ctx.enter_context(nc.psum_tensor(name, shape, F32))

        def sem(name):
            return ctx.enter_context(nc.semaphore(name))

        parts_s = nc.dram_tensor("parts_s", (2, B * P * 3, KD, S), BF16).ap()
        v_s = nc.dram_tensor("v_s", (B * S, H * W), F32).ap()
        o1_s = nc.dram_tensor("o1_s", (B * H * W, S), F32).ap()
        q2_s = nc.dram_tensor("q2_s", (NCH * P * 3, KD, CH), BF16).ap()
        o2_s = nc.dram_tensor("o2_s", (NCH * H * W, CH), F32).ap()
        k2_s = nc.dram_tensor("k2_s", (P * 3, B, KD * CTX), BF16).ap()
        v2_s = nc.dram_tensor("v2_s", (B * CTX, H * W), F32).ap()
        m_s = nc.dram_tensor("m_s", (D + 1, B * CTX), F32).ap()
        vp_s = nc.dram_tensor("vp_s", (B * CTX, D), F32).ap()

        ident = sb("ident", [P, P])
        neghalf = sb("neghalf", [P, TT])
        wq1 = sb("wq1", [P, KD, D])
        wkv1 = sb("wkv1", [P, KD, 2 * D])
        wo1 = sb("wo1", [P, KD, D])
        wq2 = sb("wq2", [P, KD, D])
        wo2 = sb("wo2", [P, KD, D])
        wff1 = [sb(f"wff1_{part}", [P, KD, 2 * FF], F32R) for part in ("hi", "lo")]
        y3 = [sb(f"y3_{part}", [P, KD, CH], F32R) for part in ("hi", "lo")]
        wff2 = sb("wff2", [P, FM, D])
        bo1 = sb("bo1", [P, D])
        bo2 = sb("bo2", [P, D])
        bff2 = sb("bff2", [P, D])
        bvl = sb("bvl", [P, D])
        cols = sb("cols", [P, 2 * FM + 8 * KD])
        bff1 = cols[:, 0:2 * FM]
        ln_s, ln_b = [cols[:, 2 * FM + 3 * KD * i:2 * FM + 3 * KD * (i + 1)].rearrange(
            "p (l k) -> p l k", l=3) for i in range(2)]
        bql, bkl = [cols[:, 2 * FM + KD * i:2 * FM + KD * (i + 1)] for i in (6, 7)]
        b_tanh = sb("b_tanh", [P, FM])
        b_half = sb("b_half", [P, FM])
        ones = sb("ones", [1, P])
        qst_full = [sb(f"qst{u}", [P, G, S], BF16) for u in range(2)]
        qst = [q[0:ROWS + SHIFT, :, :] for q in qst_full]
        kst = [sb(f"kst{u}", [ROWS + SHIFT, G, S], BF16) for u in range(2)]
        vg = [sb(f"vg{u}", [P, KT, G * W]) for u in range(2)]
        probs = sb("probs", [P, 2, G, QW])
        o_sb = sb("o_sb", [P, QH, QW])
        mxh = sb("mxh", [P, PAIRS, 2])
        mxq = sb("mxq", [P, PAIRS])
        sh_hi = sb("sh_hi", [PAIRS, P], BF16)
        sh_lo = sb("sh_lo", [PAIRS, P], BF16)
        pre_x = sb("pre_x", [P, TT, D])
        pre_st = sb("pre_st", [P, TT, 6])
        pre_mv = sb("pre_mv", [P, TT, 2])
        pre_ve = sb("pre_ve", [P, TT])
        pre_rs = sb("pre_rs", [P, TT])
        pre_yT = sb("pre_yT", [P, KD, CH])
        qk_parts = [sb(f"qk_parts{i}", [P, 3, KD * CH], BF16) for i in range(2)]
        qk_f = [sb(f"qk_f{i}", [P, KD * CH]) for i in range(2)]
        v_sb = sb("v_sb", [P, TT, H, W])
        x0 = sb("x0", [P, TT, D])
        x1 = [sb(f"x1_{u}", [P, TT, D]) for u in range(2)]
        oT = sb("oT", [P, KD, CH])
        den = sb("den", [P, KD, CH])
        x2 = sb("x2", [P, TT, D])
        xb = sb("xb", [P, TT, D])
        oT2 = sb("oT2", [P, KD, CH])
        den2 = sb("den2", [P, KD, CH])
        st, mv, ve, rs = [[sb(f"{name}{i}", shape) for i in range(2)] for name, shape in (
            ("st", [P, TT, 6]), ("mv", [P, TT, 2]), ("ve", [P, TT]), ("rs", [P, TT]))]
        q2_parts, q2_f = qk_parts[0], qk_f[0]
        q2st_full = sb("q2st", [P, H, CH], BF16)
        q2st = q2st_full[0:ROWS + SHIFT, :, :]
        k2st = sb("k2st", [ROWS + SHIFT, H, CTX], BF16)
        v2_full = sb("v2", [P, 2, H * W])
        v2 = v2_full[0:CT, :, :]
        m3 = sb("m3", [P, KD, CTX])
        m3_b = sb("m3_b", [1, CTX])
        vp = sb("vp", [CT, 2, D])
        mx2 = sb("mx2", [P, H, TT])
        sh2_hi = sb("sh2_hi", [H * TT, P], BF16)
        sh2_lo = sb("sh2_lo", [H * TT, P], BF16)
        probs2_full = sb("probs2", [P, PR2, 2 * CH])
        probs2 = probs2_full[0:CT, :, :]
        o2_sb = sb("o2_sb", [P, 2, 2 * CH])
        th = sb("th", [P, 2, CH])
        gb = sb("gb", [P, 2, CH])
        hT = sb("hT", [P, FM, CH])
        mx3 = sb("mx3", [P, TT])
        nm3 = sb("nm3", [P, TT])
        sum3 = sb("sum3", [P, TT])
        inv3 = sb("inv3", [P, TT])
        den_c = [sb(f"den_c{i}", [P, H * CH // P]) for i in range(2)]
        p3 = th[:, :, 0:CTX]
        p3T = gb[0:CT, :, :]
        oT_rows, den_rows, oT2_rows = [x[:, :, :].rearrange("p k s -> p (k s)").rearrange(
            "p (i d) -> p i d", i=TT) for x in (oT, den, oT2)]
        v2_all = probs[0:CT, :, :, :].rearrange("p a g q -> p (a g q)").rearrange("p (c n) -> p c n", c=NCT)
        vp_all = probs2[0:CT, 0:4, :].rearrange("p a q -> p (a q)").rearrange("p (c n) -> p c n", c=NCT)
        room = qst_full[1][:, :, :].rearrange("p g s -> p (g s)").bitcast(F32)
        ctx_n = room[0:CT, :].rearrange("p (c n) -> p c n", c=NCT)
        cols_n = den[0:2 * FM + 8 * KD, 0, 0:P]
        wkv2 = hT[:, 0:4, :].rearrange("p a q -> p (a q)").rearrange("p (k n) -> p k n", k=KD)
        wl_n = [x[:, :, :] for x in (x0, xb, x2)]
        ctxT = [hT[:, 4:8, :].rearrange("p a q -> p (a q)")[:, 0:B * CTX],
                v2_full[:, :, :].rearrange("p a n -> p (a n)")[:, 0:B * CTX]]
        wlT = o2_sb[:, :, :].rearrange("p a (k n) -> p a k n", k=KD)
        m_all = [v[:, :, :].rearrange("p t n -> p (t n)")[:, 0:B * CTX] for v in vg]
        m_bias = [x[0:1, :, :].rearrange("p k s -> p (k s)")[:, 0:B * CTX // 2] for x in (oT2, den2)]
        kp_all = room[:, 0:KD * B * CTX].rearrange("p (k n) -> p k n", k=KD)
        k2_part = [q2st_full[:, :, :].rearrange("p h s -> p (h s)")[:, i * KD * B * CTX:(i + 1) * KD * B * CTX].rearrange(
            "p (b k n) -> p b k n", b=B, k=KD) for i in range(3)]
        k2_rest = o_sb[:, :, 0:B * CTX // 2].rearrange("p f (b n) -> p f b n", n=CTX)

        ff1_raw = [hT[:, :, :].rearrange("p m s -> p (m s)"), probs2_full[:, 0:4, :].rearrange("p a q -> p (a q)")]
        FF1_PIECES = 4

        def ff1_piece(part, i):
            k, n = divmod(i, FF1_PIECES)
            cols_ = slice(n * 2 * FF // FF1_PIECES, (n + 1) * 2 * FF // FF1_PIECES)
            return part[:, k, cols_], ff1_raw[k][:, cols_]

        ps_max = [ps(f"ps_max{i}", [P, 512]) for i in range(2)]
        ps_s = [ps(f"ps_s{i}", [P, 512]) for i in range(2)]
        ps_o = ps("ps_o", [P, 512])
        ps_last = ps("ps_last", [P, 512])
        ps_cross = ps("ps_cross", [P, 512])
        ps_pre = ps("ps_pre", [P, 512])
        cross_max_banks = ([ps_cross, ps_pre], ps_s)
        cross_banks = ([ps_cross, ps_cross], ps_s)
        last_banks = ([ps_last, ps_last], [ps_last, ps_max[0]])
        ps_w = [ps_last, ps_cross, ps_max[0]]

        s_load = sem("setup_pre_loaded")
        s_load2 = sem("setup_rest_loaded")
        s_const = sem("setup_constants")
        s_ct = sem("setup_ctx_turned")
        s_ctT = sem("setup_ctxT")
        s_wt = sem("setup_weight_turned")
        s_wlT = sem("setup_wlT")
        s_k2 = sem("setup_k2")
        s_k2hi = sem("setup_k2_hi")
        s_k2rest = sem("setup_k2_rest")
        s_k2mid = sem("setup_k2_mid")
        s_k2lo = sem("setup_k2_lo")
        s_kp = sem("setup_kp")
        s_kpb = sem("setup_kp_biased")
        s_m = sem("setup_m")
        s_mc = sem("setup_m_copied")
        s_v2 = sem("setup_v2_vp")
        s_v2c = sem("setup_v2_copied")
        s_vpb = sem("setup_vp_biased")
        s_zero = sem("setup_v2_zeroed")
        s_store = sem("setup_stored")
        s_ones = sem("setup_ones_rows")
        s_colT = sem("setup_cols_turned")
        s_cols = sem("setup_cols")
        s_bias = sem("setup_gate_biases")
        s_ff = sem("setup_ff1_loaded")
        s_ffhi = sem("setup_ff1_hi")
        s_fflo = sem("setup_ff1_lo")
        p_sp = sem("sp_passed")
        p_pool = sem("pool_passed")
        p_dve = sem("dve_passed")
        loop_sems = []

        def loop_sem(name):
            loop_sems.append(sem(name))
            return loop_sems[-1]

        a_x = loop_sem("pre_x_loaded")
        a_st = loop_sem("pre_stats")
        a_mv = loop_sem("pre_mean_var")
        a_ve = loop_sem("pre_var_eps")
        a_rs = loop_sem("pre_rstd")
        a_xn = loop_sem("pre_normalised")
        a_T = loop_sem("pre_turned")
        a_y = loop_sem("pre_y")
        a_p = [loop_sem("pre_q"), loop_sem("pre_k")]
        a_f = [loop_sem("pre_q_copied"), loop_sem("pre_k_copied")]
        a_hi = [loop_sem("pre_q_hi"), loop_sem("pre_k_hi")]
        a_rest = [loop_sem("pre_q_rest"), loop_sem("pre_k_rest")]
        a_mid = [loop_sem("pre_q_mid"), loop_sem("pre_k_mid")]
        a_lo = [loop_sem("pre_q_lo"), loop_sem("pre_k_lo")]
        a_v = loop_sem("pre_v")
        a_vc = loop_sem("pre_v_copied")
        a_qkst = loop_sem("pre_parts_stored")
        a_vst = loop_sem("pre_v_stored")
        g_stack = [loop_sem(f"att_stacks_loaded{i}") for i in range(2)]
        g_v = loop_sem("att_values_loaded")
        g_mt = loop_sem("att_max_tile")
        g_mx = loop_sem("att_max")
        g_mp = loop_sem("att_max_of_pairs")
        g_mT = loop_sem("att_max_turned")
        g_shi = loop_sem("att_shift_hi")
        g_slo = loop_sem("att_shift_lo")
        g_shl = loop_sem("att_shift_loaded")
        g_s = loop_sem("att_scores")
        g_e = loop_sem("att_exp")
        g_av = loop_sem("att_pv")
        g_o = loop_sem("att_o_copied")
        g_ost = [loop_sem(f"att_o_stored{i}") for i in range(QH)]
        c_x0 = loop_sem("mid_x_loaded")
        c_in = loop_sem("mid_in_loaded")
        c_kv = loop_sem("cross_ctx_loaded")
        c_xb = [loop_sem(f"{c}_x_bias") for c in ("mid", "last", "last_end")]
        c_den = [loop_sem(f"{c}_den_loaded") for c in ("mid", "last")]
        c_rd = [loop_sem(f"{c}_inv_den") for c in ("mid", "last")]
        c_inv = [loop_sem(f"{c}_inv_stored") for c in ("mid", "last")]
        c_on = [loop_sem(f"{c}_o_normed") for c in ("mid", "last")]
        c_wo = [loop_sem(f"{c}_wo") for c in ("mid", "last")]
        c_x = [loop_sem(f"{c}_x") for c in ("mid", "last", "last_end")]
        c_st = [loop_sem(f"{c}_stats") for c in ("mid", "last")]
        c_mv = [loop_sem(f"{c}_mean_var") for c in ("mid", "last")]
        c_ve = [loop_sem(f"{c}_var_eps") for c in ("mid", "last")]
        c_rs = [loop_sem(f"{c}_rstd") for c in ("mid", "last")]
        c_xn = [loop_sem(f"{c}_normalised") for c in ("mid", "last")]
        c_T = [loop_sem(f"{c}_turned") for c in ("mid", "last", "last_end")]
        c_y = [loop_sem(f"{c}_y") for c in ("mid", "last", "last_end")]
        c_y3hi = loop_sem("last_y3_hi")
        c_y3lo = loop_sem("last_y3_lo")
        c_q2 = loop_sem("mid_q2")
        c_q2f = loop_sem("mid_q2_copied")
        c_q2hi = loop_sem("mid_q2_hi")
        c_q2rest = loop_sem("mid_q2_rest")
        c_q2mid = loop_sem("mid_q2_mid")
        c_q2lo = loop_sem("mid_q2_lo")
        c_q2st = loop_sem("mid_q2_stored")
        c_q2stack = loop_sem("cross_q2_stack_loaded")
        c_mt = loop_sem("cross_max_tile")
        c_mx = loop_sem("cross_max")
        c_mT = loop_sem("cross_max_turned")
        c_shi = loop_sem("cross_shift_hi")
        c_slo = loop_sem("cross_shift_lo")
        c_shl = loop_sem("cross_shift_loaded")
        c_s = loop_sem("cross_scores")
        c_e = loop_sem("cross_exp")
        c_av = loop_sem("cross_pv")
        c_o = loop_sem("cross_o_copied")
        c_ost = loop_sem("cross_o_stored")
        c_o2 = loop_sem("last_in_loaded")
        c_f1 = loop_sem("last_ff1")
        c_th = loop_sem("last_tanh")
        c_gb = loop_sem("last_gate_half")
        c_gt = loop_sem("last_gate")
        c_h = loop_sem("last_hidden")
        c_f2 = loop_sem("last_ff2")
        c_s3 = loop_sem("last_scores3")
        c_mx3 = loop_sem("last_max3")
        c_nm3 = loop_sem("last_neg_max3")
        c_e3 = loop_sem("last_exp3")
        c_inv3 = loop_sem("last_inv_sum3")
        c_pT = loop_sem("last_probs3_turned")
        c_pTc = loop_sem("last_probs3T")
        c_av3 = loop_sem("last_pv3")
        c_out = loop_sem("last_out")
        c_outst = loop_sem("last_out_stored")

        Q2F = 6

        def q2_heads(f):
            h0 = 3 * (f % Q2F)
            return f // Q2F, h0, min(3, H - h0)

        def within(v, hi):
            return v if isinstance(v, int) else nc.s_assert_within(
                v, 0, hi, skip_runtime_bounds_check_because="the loops' bounds are fixed by the shapes")

        def run(eng, body, segments):
            for n0, n1 in segments:
                if n1 - n0 <= 2:
                    for n in range(n0, n1):
                        body(n, n % 2, stages(n), stages(n - 1)[2], stages(n + 1))
                    continue
                with eng.Fori(n0 // 2, n1 // 2) as pair:
                    for u in range(2):
                        body(pair * 2 + u, u, stages(n0 + u), stages(n0 + u - 1)[2], stages(n0 + u + 1))

        def walk(n, flags, pre, mid, cross, last, att_work, max_work, tail, loads=lambda slot: None,
                 late_last=False):
            has_pre, has_max, has_att, has_mid, has_cross, has_last = flags

            def pre_mid():
                work = mid(n - MID_LAG, has_pre) if has_mid else iter(())
                for _ in range(3 * has_mid):
                    next(work)
                    yield
                if has_pre:
                    yield from pre(n)
                yield from work

            chains = [
                (last(n - LAST_LAG) if has_last else iter(()), LAST_STEPS * has_last, LAST_AT),
                (cross(n - CROSS_LAG) if has_cross else iter(()), CROSS_STEPS * has_cross, CROSS_AT),
                (pre_mid(), PRE_STEPS * has_pre + MID_STEPS * has_mid, PRE_AT),
            ]

            def advance(i, slot, place=0, places=1):
                work, total, at = chains[i]
                at = [x * places for x in at]
                now = slot * places + place
                for _ in range(share(total, now - 1, at), share(total, now, at)):
                    next(work)

            for slot in range(SLOTS):
                for place in range(SUB):
                    if has_max:
                        max_work(SUB * slot + place)
                    if has_att:
                        att_work(slot, place)
                    if place == LAST_PLACE and not late_last:
                        advance(0, slot)
                    if place == SUB - 1:
                        advance(2, slot)
                        if late_last:
                            advance(0, slot)
                        loads(slot)
                    advance(1, slot, place, SUB)
            tail()
            assert all(next(work, None) is None for work, _, _ in chains)

        block = ctx.enter_context(nc.Block())

        @block.sync
        def _(sp):
            def wt(w):
                return w.rearrange("(k p) n -> p k n", p=P)

            def row(v):
                return v.partition_broadcast(P)

            def load_x(p):
                sp.dma_start(pre_x[:, :, :], t["x"].rearrange("b s d -> (b s) d").rearrange(
                    "(c i p) d -> c p i d", i=TT, p=P)[p]).then_inc(a_x, 16)

            for sem_ in loop_sems:
                sp.sem_inc(sem_, ON)
            load_x(0)
            at = 0
            for name in VECTORS:
                rows = t[name].shape[0] // P
                sp.dma_start(cols_n[at:at + rows, :], t[name].rearrange("(k p) -> k p", p=P)).then_inc(s_load, 16)
                at += rows
            for dst, name in ((wq1, "Wq1"), (wkv1, "Wkv1")):
                sp.dma_start(dst[:, :, :], wt(t["L0_xattn_" + name])).then_inc(s_load, 16)
            loads = [
                (ctx_n, t["ctx_1024"].rearrange("b (a p) d -> p (b a) d", p=CT)),
                (wkv2, wt(t["L0_xattn_Wkv2"])),
                (wl_n[0], wt(t["L1_xattn_Wq"])), (wl_n[1], wt(t["L1_xattn_Wk"])), (wl_n[2], wt(t["L1_xattn_Wv"])),
                (bvl[:, :], row(t["L1_xattn_bv"])),
                (wo1[:, :, :], wt(t["L0_xattn_Wo1"])), (wq2[:, :, :], wt(t["L0_xattn_Wq2"])),
                (wo2[:, :, :], wt(t["L0_xattn_Wo2"])), 
                (wff2[:, :, :], wt(t["L0_xattn_Wff2"])),
                (bo1[:, :], row(t["L0_xattn_bo1"])), (bo2[:, :], row(t["L0_xattn_bo2"])),
                (bff2[:, :], row(t["L0_xattn_bff2"])),
            ]
            assert len(loads) == N_REST
            for dst, src in loads:
                sp.dma_start(dst, src).then_inc(s_load2, 16)

            def context():
                sp.wait_ge(s_k2hi, 4)
                sp.wait_ge(s_k2mid, 4)
                sp.wait_ge(s_k2lo, 4)
                for i in range(3):
                    sp.dma_start(k2_s.rearrange("(p t) b n -> t p (b n)", t=3)[PART_AT[1][i]],
                                 k2_part[i].rearrange("p b k n -> p (b k n)")).then_inc(s_store, 16)
                sp.wait_ge(s_mc, 2 * KD + 2)
                for k in range(KD):
                    sp.dma_start(m_s[k * P:(k + 1) * P, :], m_all[k]).then_inc(s_store, 16)
                for i in range(2):
                    span = slice(i * B * CTX // 2, (i + 1) * B * CTX // 2)
                    sp.dma_start(m_s[D:D + 1, span], m_bias[i]).then_inc(s_store, 16)
                sp.wait_ge(s_v2c, NCT)
                sp.dma_start(v2_s.rearrange("(c p) n -> p c n", p=CT), v2_all).then_inc(s_store, 16)
                sp.wait_ge(s_vpb, NCT)
                sp.dma_start(vp_s.rearrange("(c p) n -> p c n", p=CT), vp_all).then_inc(s_store, 16)
                sp.wait_ge(s_store, 9 * 16)
                for k in range(KD):
                    sp.dma_start(ff1_raw[k], t["L0_xattn_Wff1"][k * P:(k + 1) * P, :]).then_inc(s_ff, 16)

            def wait(of, count):
                sp.wait_ge(of, count)
                sp.sem_inc(p_sp, 1)

            def pre(p):
                for _ in range(4):
                    yield
                wait(a_T, ON + p + 1)
                load_x((p + 1) % NCH)
                for _ in range(3):
                    yield
                b, c = within(p // (S // CH), B - 1), p % (S // CH)
                for kind in range(2):
                    wait(a_lo[kind], ON + p + 1)
                    sp.dma_start(parts_s[kind].rearrange("(b p t) k (c s) -> b c p (t k) s", b=B, p=P, s=CH)[b, c],
                                 qk_parts[kind][:, :, :].rearrange("p t (k s) -> p (t k) s", k=KD)).then_inc(a_qkst, 16)
                wait(a_vc, ON + p + 1)
                sp.dma_start(v_s.rearrange("(c i p) n -> c p i n", i=TT, p=P)[p],
                             v_sb[:, :, :, :].rearrange("p i h w -> p i (h w)")).then_inc(a_vst, 16)
                yield

            def load_stacks(m, par):
                b, k, a = within(m // G, B - 1), (m % G) // 2, m % 2
                wait(a_qkst, ON + (b + 1) * (S // CH) * 32)
                if not isinstance(m, int) or m >= 2:
                    wait(g_s, ON + (m - 1) * 64)
                for kind, stack in ((0, qst), (1, kst)):
                    sp.dma_start(stack[par][0:3 * DH, :, :], parts_s[kind].rearrange(
                        "(b a j x) k s -> b a k x j s", b=B, a=2, j=G)[b, a, k]).then_inc(g_stack[par], 16)
                    for i, part in enumerate(STACK[kind]):
                        sp.dma_start(stack[par][(3 + i) * DH:(4 + i) * DH, :, :], parts_s[kind].rearrange(
                            "(b a j d t) k s -> b a k t d j s", b=B, a=2, j=G, t=3)[b, a, k, part]
                                     ).then_inc(g_stack[par], 16)

            def load_values(m, par):
                wait(a_vst, ON + (m // G + 1) * (S // CH) * 16)
                if not isinstance(m, int) or m >= 2:
                    wait(g_av, ON + (m - 1) * STEPS)
                sp.dma_start(vg[par][:, :, :], v_s.rearrange("(b k p) (g n) -> b g p k n", b=B, p=P, g=H // G)[
                    within(m // G, B - 1), m % G]).then_inc(g_v, 16)

            def packed(which, rows):
                return (rows.rearrange("(r w) (c s) -> r c w s", w=W, c=P // H)[:, :, DH, :],
                        den_c[which][:, :])

            def load_den(which, rows):
                dram, tile = packed(which, rows)
                sp.dma_start(tile, dram).then_inc(c_den[which], 16)

            def store_inv(which, rows):
                dram, tile = packed(which, rows)
                sp.dma_start(dram, tile).then_inc(c_inv[which], 16)

            def load_sums(dst, rows, done):
                for k in range(KD):
                    sp.dma_start(dst[:, k, :], rows.rearrange("(k h w) s -> k h w s", k=KD, w=W)[k, :, 0:DH, :]
                                 ).then_inc(done, 16)

            def load_inv(dst, rows, done):
                for k in range(KD):
                    sp.dma_start(dst[:, k, :], rows.rearrange("(k h w) s -> k h w s", k=KD, w=W)[
                        k, :, DH:DH + 1, :].to_broadcast([P // DH, DH, CH])).then_inc(done, 16)

            def mid(o, has_pre):
                b, c = within(o // (S // CH), B - 1), o % (S // CH)
                wait(c_q2, ON + o)
                wait(c_x[0], ON + o)
                sp.dma_start(x0[:, :, :], t["x"].rearrange("b s d -> (b s) d").rearrange(
                    "(c i p) d -> c p i d", i=TT, p=P)[o]).then_inc(c_x0, 16)
                for i in range(QH):
                    wait(g_ost[i], ON + (o // (S // CH) + 1) * (H // G) * 16)
                rows = o1_s.rearrange("(b r) (c s) -> b c r s", b=B, s=CH)[b, c]
                load_den(0, rows)
                load_sums(oT, rows, c_in)
                yield
                wait(c_rd[0], ON + o + 1)
                store_inv(0, rows)
                yield
                wait(c_inv[0], ON + (o + 1) * 16)
                load_inv(den, rows, c_in)
                for _ in range(MID_STEPS - 3):
                    yield
                wait(c_q2lo, ON + o + 1)
                sp.dma_start(q2_s.rearrange("(o p t) k s -> o p (t k s)", p=P, t=3)[o],
                             q2_parts[:, :, :].rearrange("p t n -> p (t n)")).then_inc(c_q2st, 16)
                yield

            def load_cross(o):
                b = within(o // (S // CH), B - 1)
                wait(c_s, ON + o * H)
                wait(c_q2st, ON + (o + 1) * 16)
                q2, k2 = [x.rearrange("x (e k) s -> x e (k s)", k=KD) for x in (q2st, k2st[:, :, :])]
                sp.dma_start(q2[0:3 * DH, :, :], q2_s.rearrange("(o e x) k s -> o x e (k s)", o=NCH, e=H // KD)[o]
                             ).then_inc(c_q2stack, 16)
                sp.dma_start(k2[0:3 * DH, :, :], k2_s.rearrange("(e x) b n -> b x e n", e=H // KD)[b]
                             ).then_inc(c_kv, 16)
                for i in range(3):
                    rows = slice((3 + i) * DH, (4 + i) * DH)
                    sp.dma_start(q2[rows, :, :], q2_s.rearrange(
                        "(o e d t) k s -> o t d e (k s)", o=NCH, e=H // KD, t=3)[o, STACK[0][i]]
                                 ).then_inc(c_q2stack, 16)
                    sp.dma_start(k2[rows, :, :], k2_s.rearrange(
                        "(e d t) b n -> b t d e n", e=H // KD, t=3)[b, STACK[1][i]]).then_inc(c_kv, 16)
                wait(c_av, ON + o * 4)
                sp.dma_start(v2[:, :, :], v2_s.rearrange("(b a p) n -> b p a n", b=B, p=CT)[b]).then_inc(c_kv, 16)

            def cross(o):
                for _ in range(14):
                    yield
                wait(c_slo, ON + o + 1)
                for row_, part in ((ROWS, sh2_hi), (ROWS + 1, sh2_lo)):
                    sp.dma_start(q2st[row_:row_ + 1, :, :].rearrange("a h (i p) -> a (h i) p", i=TT),
                                 part[:, :]).then_inc(c_shl, 16)
                for _ in range(11):
                    yield
                store_o2(o, 0)
                for _ in range(10):
                    yield
                store_o2(o, 1)
                yield

            def store_o2(o, e):
                wait(c_o, ON + o * 4 + 2 * e + 2)
                sp.dma_start(o2_s.rearrange("(o e g p) s -> o e p g s", e=2, g=2, p=P)[o, e],
                             o2_sb[:, e, :].rearrange("p (g s) -> p g s", g=2)).then_inc(c_ost, 16)

            def o2_rows(o):
                return o2_s.rearrange("(o r) s -> o r s", o=NCH)[o]

            def load_last_den(o):
                wait(c_ost, ON + (o + 1) * 32)
                load_den(1, o2_rows(o))

            def store_last_inv(o):
                wait(c_rd[1], ON + o + 1)
                store_inv(1, o2_rows(o))

            def load_last(o):
                wait(c_s3, ON + o)
                load_sums(oT2, o2_rows(o), c_o2)
                b = within(o // (S // CH), B - 1)
                sp.dma_start(m3_b[:, :], m_s[D:D + 1, :].rearrange("a (b n) -> b a n", b=B)[b]).then_inc(c_o2, 16)
                sp.dma_start(m3[:, :, :], m_s[0:D, :].rearrange("(k p) (b n) -> b p k n", p=P, b=B)[b]).then_inc(c_o2, 16)

            def load_last_inv(o):
                wait(c_s3, ON + o)
                wait(c_inv[1], ON + (o + 1) * 16)
                load_inv(den2, o2_rows(o), c_o2)
                wait(c_av3, ON + o)
                sp.dma_start(vp[:, :, :], vp_s.rearrange("(b a p) n -> b p a n", b=B, p=CT)[
                    within(o // (S // CH), B - 1)]).then_inc(c_o2, 16)

            def last(o):
                for _ in range(LAST_STEPS - 1):
                    yield
                wait(c_out, ON + (o + 1) * 2)
                sp.dma_start(out.rearrange("b s d -> (b s) d").rearrange(
                    "(c i p) d -> c p i d", i=TT, p=P)[o], xb[:, :, :]).then_inc(c_outst, 16)
                yield

            def body(n, u, flags, att_before, after):
                has_max, has_att = flags[1:3]
                grp, m = n - ATT_LAG, n - MAX_LAG

                def store_o(group, qh):
                    wait(g_o, ON + group * QH + qh + 1)
                    sp.dma_start(o1_s.rearrange("(m p) (q s) -> m q p s", p=P, q=QH)[group, qh],
                                 o_sb[:, qh, :]).then_inc(g_ost[qh], 16)

                if has_max and not (isinstance(n, int) and n == MAX_LAG):
                    load_stacks(m, u)
                if att_before:
                    store_o(grp - 1, 1)

                def max_work(at):
                    if at == SUB * MAX_TURN + 1:
                        wait(g_slo, ON + m + 1)
                        for row_, part in ((ROWS, sh_hi), (ROWS + 1, sh_lo)):
                            sp.dma_start(qst[u][row_:row_ + 1, :, :].rearrange("a j (q p) -> a (j q) p", p=P),
                                         part[:, :]).then_inc(g_shl, 16)

                def att_work(slot, place):
                    if slot == SLOTS // 2 + 2 and place == 0:
                        store_o(grp, 0)

                def loads(slot):
                    if has_max and slot == V_LOAD:
                        load_values(m, u)
                    if after[4] and slot == CROSS_LOAD:
                        load_cross(n + 1 - CROSS_LAG)
                    if after[5]:
                        for at, step in ((DEN_LOAD, load_last_den), (DEN_INV, store_last_inv),
                                         (LAST_LOAD, load_last), (SLOTS - 1, load_last_inv)):
                            if slot == at:
                                step(n + 1 - LAST_LAG)

                walk(n, flags, pre, mid, cross, last, att_work, max_work, lambda: None, loads)

            run(sp, body, SEGMENTS[:1])
            load_stacks(0, 0)
            context()
            run(sp, body, SEGMENTS[1:])
            sp.wait_ge(c_outst, ON + NCH * 16)

        @block.gpsimd
        def _(pool):
            nc.gpsimd.memset(ident[:, :], 0.0).then_inc(s_const, 1)
            pool.wait_ge(s_const, 1)
            nc.gpsimd.affine_select(out=ident[:, :], in_=ident[:, :], compare_op=ALU.not_equal, fill=1.0, base=0,
                                    pattern=[[-1, P]], channel_multiplier=1).then_inc(s_const, 1)
            nc.gpsimd.memset(neghalf[:, :], -0.5).then_inc(s_const, 1)
            nc.gpsimd.memset(ones[:, :], 1.0).then_inc(s_const, 1)
            v = v_sb[:, :, :, :]
            nc.gpsimd.memset(v, 0.0).then_inc(s_const, 1)
            pool.wait_ge(s_const, 5)
            nc.gpsimd.memset(v[:, :, :, DH:DH + 1], 1.0).then_inc(s_const, 1)
            def context():
                nc.gpsimd.memset(v2_all, 0.0).then_inc(s_zero, 1)
                pool.wait_ge(s_zero, 1)
                nc.gpsimd.memset(v2_all.rearrange("p c (h w) -> p (c h) w", w=W)[:, :, DH:DH + 1], 1.0).then_inc(s_zero, 1)
                pool.wait_ge(s_cols, 1)
                nc.gpsimd.tensor_scalar(b_tanh[:, :], bff1[:, FM:2 * FM], GELU_A / 2, 0.0, ALU.mult, ALU.add).then_inc(s_bias, 1)
                nc.gpsimd.tensor_scalar(b_half[:, :], bff1[:, FM:2 * FM], 0.5, 0.0, ALU.mult, ALU.add).then_inc(s_bias, 1)
                for f in range(4):
                    k, bs = f // 2, slice((f % 2) * B // 2, (f % 2 + 1) * B // 2)
                    pool.wait_ge(s_k2rest, f + 1)
                    nc.gpsimd.tensor_copy(k2_part[1][:, bs, k, :], k2_rest[:, f % 2, :, :]).then_inc(s_k2mid, 1)
                    pool.wait_ge(s_k2mid, f + 1)
                    nc.gpsimd.tensor_tensor(k2_part[2][:, bs, k, :], k2_rest[:, f % 2, :, :],
                                            k2_part[1][:, bs, k, :], ALU.subtract).then_inc(s_k2lo, 1)

                for i in range(KD * FF1_PIECES):
                    lo, raw = ff1_piece(wff1[1], i)
                    pool.wait_ge(s_ffhi, i + 1)
                    nc.gpsimd.tensor_tensor(lo, raw, ff1_piece(wff1[0], i)[0].bitcast(F32),
                                            ALU.subtract).then_inc(s_fflo, 1)

            def rstd(mean_var, var_eps, rstd_, ready, eps_done, done, count):
                pool.wait_ge(ready, ON + count * 2)
                pool.sem_inc(p_pool, 1)
                nc.gpsimd.tensor_scalar(var_eps[:, :], mean_var[:, :, 1], EPS, 0.0, ALU.add, ALU.add).then_inc(eps_done, 1)
                pool.wait_ge(eps_done, ON + count)
                nc.gpsimd.tensor_tensor(rstd_[:, :], var_eps[:, :], neghalf[:, :], ALU.pow).then_inc(done, 1)

            def parts(x, part, at, copied, hi_ready, rest_ready, mid_ready, lo_ready, count):
                hi, mid, lo = [part[:, i, :] for i in at]
                pool.wait_ge(hi_ready, ON + count)
                pool.wait_ge(copied, ON + count)
                nc.gpsimd.tensor_tensor(x[:, :], x[:, :], hi, ALU.subtract).then_inc(rest_ready, 1)
                pool.wait_ge(rest_ready, ON + count)
                pool.sem_inc(p_pool, 1)
                nc.gpsimd.tensor_copy(mid, x[:, :]).then_inc(mid_ready, 1)
                pool.wait_ge(mid_ready, ON + count)
                nc.gpsimd.tensor_tensor(lo, x[:, :], mid, ALU.subtract).then_inc(lo_ready, 1)

            def pre(p):
                yield
                rstd(pre_mv, pre_ve, pre_rs, a_mv, a_ve, a_rs, p + 1)
                for _ in range(3):
                    yield
                pool.wait_ge(a_qkst, ON + p * 32)
                for i in range(2):
                    parts(qk_f[i], qk_parts[i], PART_AT[i], a_f[i], a_hi[i], a_rest[i], a_mid[i], a_lo[i], p + 1)
                    yield
                for _ in range(2):
                    yield

            def add_bias(dst, x, bias, done):
                for i in range(TT):
                    last = nc.gpsimd.tensor_tensor(dst[:, i, :], x[:, i, :], bias[:, :], ALU.add)
                last.then_inc(done, 1)

            def mid(o, has_pre):
                yield
                pool.wait_ge(c_x0, ON + (o + 1) * 16)
                add_bias(x0, x0, bo1, c_xb[0])
                for _ in range(3):
                    yield
                rstd(mv[0], ve[0], rs[0], c_mv[0], c_ve[0], c_rs[0], o + 1)
                for _ in range(3):
                    yield
                pool.wait_ge(c_q2st, ON + o * 16)
                parts(q2_f, q2_parts, PART_AT[0], c_q2f, c_q2hi, c_q2rest, c_q2mid, c_q2lo, o + 1)
                yield
                yield

            def cross(o):
                for _ in range(CROSS_STEPS):
                    yield

            def last_by(u):
                def last(o):
                    pool.wait_ge(c_outst, ON + o * 16)
                    add_bias(xb, x1[u], bo2, c_xb[1])
                    for _ in range(4):
                        yield
                    rstd(mv[1], ve[1], rs[1], c_mv[1], c_ve[1], c_rs[1], o + 1)
                    yield
                    pool.wait_ge(c_x[1], ON + o + 1)
                    add_bias(xb, x2, bff2, c_xb[2])
                    for _ in range(LAST_STEPS - 5):
                        yield
                return last

            def body(n, u, flags, att_before, after):
                walk(n, flags, pre, mid, cross, last_by(1 - u), lambda slot, place: None, lambda at: None, lambda: None,
                     late_last=True)

            run(pool, body, SEGMENTS[:1])
            context()
            run(pool, body, SEGMENTS[1:])

        @block.scalar
        def _(act):
            act.wait_ge(s_colT, 1)
            nc.scalar.copy(cols[:, :], ps_o[:, 0:2 * FM + 8 * KD]).then_inc(s_cols, 1)
            act.wait_ge(s_cols, 1)
            act.wait_ge(s_const, 6)

            def context():
                for c in range(NCT):
                    act.wait_ge(s_ct, c + 1)
                    for k in range(KD):
                        copied = nc.scalar.copy(ctxT[k][:, c * CT:(c + 1) * CT], ps_w[c % 3][:, k * P:k * P + CT])
                    copied.then_inc(s_ctT, 1)
                for w in range(2):
                    act.wait_ge(s_wt, w + 1)
                    nc.scalar.copy(wlT[:, w, :, :].rearrange("p k n -> p (k n)"), ps_w[w][:, :]).then_inc(s_wlT, 1)
                half = B * CTX // 2
                for f in range(4):
                    k, span = f // 2, slice((f % 2) * half, (f % 2 + 1) * half)
                    bs = slice((f % 2) * B // 2, (f % 2 + 1) * B // 2)
                    act.wait_ge(s_k2, f + 1)
                    nc.scalar.copy(k2_part[0][:, bs, k, :], ps_s[f % 2][:, 0:half].rearrange("p (b n) -> p b n", n=CTX)
                                   ).then_inc(s_k2hi, 1)
                    act.wait_ge(s_kp, f + 1)
                    nc.scalar.activation(kp_all[:, k, span], ps_w[f % 2][:, 0:half], ACT.Identity,
                                         bias=bkl[:, k:k + 1]).then_inc(s_kpb, 1)
                for g in range(2 * KD + 2):
                    k, span = g // 2, slice((g % 2) * half, (g % 2 + 1) * half)
                    act.wait_ge(s_m, g + 1)
                    if k < KD:
                        nc.scalar.copy(m_all[k][:, span], ps_s[g % 2][:, 0:half]).then_inc(s_mc, 1)
                    else:
                        nc.scalar.copy(m_bias[g % 2], ps_s[g % 2][0:1, 0:half]).then_inc(s_mc, 1)
                act.wait_ge(s_zero, 2)
                for c in range(NCT):
                    act.wait_ge(s_v2, c + 1)
                    nc.scalar.copy(v2_all[:, c, :].rearrange("p (h w) -> p h w", w=W)[:, :, 0:DH],
                                   ps_w[c % 3][0:CT, 0:D].rearrange("p (h d) -> p h d", d=DH)).then_inc(s_v2c, 1)
                act.wait_ge(s_bias, 2)
                act.wait_ge(s_ff, KD * 16)
                for i in range(KD * FF1_PIECES):
                    nc.scalar.copy(*ff1_piece(wff1[0], i)).then_inc(s_ffhi, 1)

            def affine(dst, src, layer, done):
                for k in range(KD):
                    nc.scalar.activation(dst[:, k, :], src[:, k * CH:(k + 1) * CH], ACT.Identity,
                                         scale=ln_s[:, layer, k:k + 1], bias=ln_b[:, layer, k:k + 1]).then_inc(done, 1)

            def pre_by(has_mid):
                def pre(p):
                    for _ in range(3):
                        yield
                    act.wait_ge(a_T, ON + p + 1)
                    affine(pre_yT, ps_pre, 0, a_y)
                    yield
                    for i in range(2):
                        act.wait_ge(a_p[i], ON + p + 1)
                        act.wait_ge(a_lo[i], ON + p)
                        act.wait_ge(a_qkst, ON + p * 32)
                        if has_mid and i == 0:
                            act.wait_ge(c_q2st, ON + (p - MID_LAG) * 16)
                        nc.scalar.copy(qk_parts[i][:, PART_AT[i][0], :], ps_pre[:, :]).then_inc(a_hi[i], 1)
                        nc.scalar.copy(qk_f[i][:, :], ps_pre[:, :]).then_inc(a_f[i], 1)
                        yield
                    act.wait_ge(a_vst, ON + p * 16)
                    act.wait_ge(a_v, ON + p + 1)
                    nc.scalar.copy(v_sb[:, :, :, 0:DH].rearrange("p i h d -> p (i h) d"),
                                   ps_pre[:, :].rearrange("p (n d) -> p n d", d=DH)).then_inc(a_vc, 1)
                    yield
                    yield
                return pre

            def mid(o, has_pre):
                for _ in range(6):
                    yield
                act.wait_ge(c_T[0], ON + o + 1)
                affine(oT, ps_pre, 1, c_y[0])
                yield
                act.wait_ge(c_q2, ON + o + 1)
                act.wait_ge(c_q2lo, ON + o)
                act.wait_ge(c_q2st, ON + o * 16)
                done = o + MID_LAG + 1 if has_pre else NCH
                act.wait_ge(a_qkst, ON + done * 32)
                nc.scalar.copy(q2_parts[:, PART_AT[0][0], :], ps_pre[:, :]).then_inc(c_q2hi, 1)
                nc.scalar.copy(q2_f[:, :], ps_pre[:, :]).then_inc(c_q2f, 1)
                yield
                yield

            def cross_by(spare):
                def cross(o):
                    for _ in range(16):
                        yield
                    for h in range(H):
                        act.wait_ge(c_s, ON + o * H + h + 1)
                        act.wait_ge(c_av, ON + o * 4 + max(0, (h - PR2) // G + 1))
                        nc.scalar.activation(probs2[:, h % PR2, :], cross_banks[spare][h % 2][0:CT, :], ACT.Exp,
                                             scale=SCALE).then_inc(c_e, 1)
                        yield
                        if h % G == 0 and h or h == H - 1:
                            g = max(0, h - 1) // G
                            if g == 0:
                                act.wait_ge(c_ost, ON + o * 32)
                            act.wait_ge(c_av, ON + o * 4 + g + 1)
                            nc.scalar.copy(o2_sb[:, g // 2, (g % 2) * CH:(g % 2 + 1) * CH],
                                           ps_cross[:, 0:CH]).then_inc(c_o, 1)
                            yield
                return cross

            def last_by(spare):
                def last(o):
                    for _ in range(6):
                        yield
                    act.wait_ge(c_T[1], ON + o + 1)
                    affine(den2, ps_last, 2, c_y[1])
                    act.wait_ge(c_y[1], ON + (o + 1) * 2)
                    nc.scalar.copy(y3[0][:, :, :], den2[:, :, :]).then_inc(c_y3hi, 1)
                    yield
                    for m in range(FM):
                        bank = last_banks[spare][m % 2]
                        act.wait_ge(c_f1, ON + o * FM + m + 1)
                        act.wait_ge(c_h, ON + o * FM + max(0, m - 1))
                        nc.scalar.activation(th[:, m % 2, :], bank[:, CH:2 * CH], ACT.Tanh, scale=GELU_A / 2,
                                             bias=b_tanh[:, m:m + 1]).then_inc(c_th, 1)
                        nc.scalar.activation(gb[:, m % 2, :], bank[:, CH:2 * CH], ACT.Identity, scale=0.5,
                                             bias=b_half[:, m:m + 1]).then_inc(c_gb, 1)
                        yield
                    for _ in range(5):
                        yield
                    act.wait_ge(c_T[2], ON + o + 1)
                    nc.scalar.copy(den2[:, :, :].rearrange("p k s -> p (k s)"), ps_last[:, :]).then_inc(c_y[2], 1)
                    yield
                    yield
                    act.wait_ge(c_nm3, ON + o + 1)
                    for i in range(TT):
                        nc.scalar.activation(p3[:, i, :], ps_last[:, i * CH:i * CH + CTX], ACT.Exp,
                                             bias=nm3[:, i:i + 1], accum_out=sum3[:, i:i + 1]).then_inc(c_e3, 1)
                    yield
                    act.wait_ge(c_pT, ON + o + 1)
                    nc.scalar.copy(p3T[:, :, :].rearrange("p a s -> p (a s)"), ps_last[0:CT, :]).then_inc(c_pTc, 1)
                    yield
                    yield
                    yield
                return last

            def body(n, u, flags, att_before, after):
                grp = n - ATT_LAG

                def exp_tile(c, j):
                    act.wait_ge(g_s, ON + grp * 64 + c * G + j + 1)
                    act.wait_ge(g_av, ON + grp * STEPS + max(0, c - 1))
                    nc.scalar.activation(probs[:, c % 2, j, :], ps_s[j % 2][:, :], ACT.Exp, scale=SCALE).then_inc(g_e, 1)

                def o_copy(qh):
                    act.wait_ge(g_av, ON + grp * STEPS + (qh + 1) * KT)
                    act.wait_ge(g_ost[qh], ON + grp * 16)
                    nc.scalar.copy(o_sb[:, qh, :], ps_o[:, :]).then_inc(g_o, 1)

                def att_work(slot, place):
                    c, pair = divmod(slot, 2)
                    if place == 0:
                        exp_tile(c, 2 * pair)
                        exp_tile(c, 2 * pair + 1)
                    if slot == SLOTS // 2 and place == SUB - 1:
                        o_copy(0)

                def tail():
                    if flags[2]:
                        o_copy(1)

                walk(n, flags, pre_by(flags[3]), mid, cross_by(not flags[2]), last_by(not flags[2]), att_work, lambda at: None, tail)

            run(act, body, SEGMENTS[:1])
            context()
            run(act, body, SEGMENTS[1:])

        @block.vector
        def _(dve):
            for tile in (kst[0], kst[1], k2st):
                nc.vector.memset(tile[ROWS:ROWS + SHIFT, :, :], 1.0).then_inc(s_ones, 1)
            def context():
                dve.wait_ge(s_load2, N_REST * 16)
                dve.wait_ge(s_cols, 1)
                half = B * CTX // 2
                for f in range(4):
                    k, bs = f // 2, slice((f % 2) * B // 2, (f % 2 + 1) * B // 2)
                    dve.wait_ge(s_k2hi, f + 1)
                    if f >= 2:
                        dve.wait_ge(s_k2lo, f - 1)
                    nc.vector.tensor_tensor(k2_rest[:, f % 2, :, :], ps_s[f % 2][:, 0:half].rearrange(
                        "p (b n) -> p b n", n=CTX), k2_part[0][:, bs, k, :], ALU.subtract).then_inc(s_k2rest, 1)
                for c in range(NCT):
                    dve.wait_ge(s_v2c, c + 1)
                    nc.vector.tensor_tensor(vp_all[:, c, :], ps_w[c % 3][0:CT, D:2 * D], bvl[0:CT, :],
                                            ALU.add).then_inc(s_vpb, 1)

            def stats(x, stat, mean_var, stat_done, mv_done, base):
                for i in range(TT):
                    nc.vector.bn_stats(stat[:, i, :], x[:, i, :]).then_inc(stat_done, 1)
                dve.wait_ge(stat_done, ON + base + TT)
                dve.sem_inc(p_dve, 1)
                for i in range(TT):
                    nc.vector.bn_aggr(mean_var[:, i, :], stat[:, i, :]).then_inc(mv_done, 1)

            def normalise(dst, x, mean_var, rstd_, done):
                for i in range(TT):
                    nc.vector.tensor_scalar(dst[:, i, :], x[:, i, :], mean_var[:, i, 0:1], rstd_[:, i:i + 1],
                                            ALU.subtract, ALU.mult).then_inc(done, 1)

            def pre(p):
                yield
                dve.wait_ge(a_x, ON + (p + 1) * 16)
                stats(pre_x, pre_st, pre_mv, a_st, a_mv, p * 2)
                yield
                dve.wait_ge(a_rs, ON + p + 1)
                normalise(pre_x, pre_x, pre_mv, pre_rs, a_xn)
                for _ in range(6):
                    yield

            def invert(which, o):
                dve.wait_ge(c_den[which], ON + (o + 1) * 16)
                nc.vector.reciprocal(den_c[which][:, :], den_c[which][:, :]).then_inc(c_rd[which], 1)

            def norm_o(which, sums, invs):
                o_flat = sums[:, :, :].rearrange("p k s -> p (k s)")
                nc.vector.tensor_tensor(o_flat, o_flat, invs[:, :, :].rearrange("p k s -> p (k s)"),
                                        ALU.mult).then_inc(c_on[which], 1)

            def residual(which, dst, bank, x, o):
                dve.wait_ge(c_xb[which], ON + o + 1)
                nc.vector.tensor_tensor(dst[:, :, :].rearrange("p i d -> p (i d)"), bank[:, :],
                                        x[:, :, :].rearrange("p i d -> p (i d)"), ALU.add).then_inc(c_x[which], 1)
                dve.wait_ge(c_x[which], ON + o + 1)

            def mid_by(u, has_last):
                def mid(o, has_pre):
                    yield
                    invert(0, o)
                    yield
                    yield
                    dve.wait_ge(c_in, ON + (o + 1) * 64)
                    norm_o(0, oT, den)
                    yield
                    dve.wait_ge(c_wo[0], ON + o + 1)
                    if has_last:
                        dve.wait_ge(c_xb[1], ON + o - LAST_LAG + MID_LAG + 1)
                    residual(0, x1[u], ps_pre, x0, o)
                    stats(x1[u], st[0], mv[0], c_st[0], c_mv[0], o * 2)
                    yield
                    dve.wait_ge(c_rs[0], ON + o + 1)
                    normalise(den_rows, x1[u], mv[0], rs[0], c_xn[0])
                    for _ in range(4):
                        yield
                return mid

            def cross_by(spare):
                def cross(o):
                    yield
                    for f in range(2 * Q2F):
                        i, h0, nh = q2_heads(f)
                        dve.wait_ge(c_mt, ON + o * 2 * Q2F + f + 1)
                        nc.vector.tensor_reduce(mx2[:, h0:h0 + nh, i], cross_max_banks[spare][f % 2][:, 0:nh * CTX].rearrange(
                            "p (h n) -> p h n", h=nh), AX_X, ALU.max).then_inc(c_mx, 1)
                        yield
                    dve.wait_ge(c_mT, ON + o + 1)
                    negative(ps_cross[0:H * TT, 0:P], sh2_hi, sh2_lo, c_shi, c_slo, o + 1)
                    for _ in range(CROSS_STEPS - 13):
                        yield
                return cross

            def last_by(spare):
                def last(o):
                    yield
                    yield
                    dve.wait_ge(c_o2, ON + (o + 1) * 112)
                    norm_o(1, oT2, den2)
                    yield
                    yield
                    dve.wait_ge(c_wo[1], ON + o + 1)
                    residual(1, x2, ps_last, xb, o)
                    stats(x2, st[1], mv[1], c_st[1], c_mv[1], o * 2)
                    yield
                    dve.wait_ge(c_rs[1], ON + o + 1)
                    normalise(oT2_rows, x2, mv[1], rs[1], c_xn[1])
                    yield
                    dve.wait_ge(c_y3hi, ON + o + 1)
                    nc.vector.tensor_tensor(y3[1][:, :, :], den2[:, :, :], y3[0][:, :, :].bitcast(F32),
                                            ALU.subtract).then_inc(c_y3lo, 1)
                    yield
                    for m in range(FM):
                        dve.wait_ge(c_th, ON + o * FM + m + 1)
                        dve.wait_ge(c_gb, ON + o * FM + m + 1)
                        nc.vector.scalar_tensor_tensor(th[:, m % 2, :], th[:, m % 2, :], 1.0, gb[:, m % 2, :],
                                                       ALU.add, ALU.mult).then_inc(c_gt, 1)
                        dve.wait_ge(c_gt, ON + o * FM + m + 1)
                        nc.vector.scalar_tensor_tensor(hT[:, m, :], last_banks[spare][m % 2][:, 0:CH], bff1[:, m:m + 1],
                                                       th[:, m % 2, :], ALU.add, ALU.mult).then_inc(c_h, 1)
                        yield
                    for _ in range(4):
                        yield
                    dve.wait_ge(c_f2, ON + o + 1)
                    residual(2, x2, ps_last, xb, o)
                    yield
                    yield
                    dve.wait_ge(c_s3, ON + o + 1)
                    nc.vector.tensor_reduce(mx3[:, :], ps_last[:, :].rearrange("p (i n) -> p i n", i=TT)[:, :, 0:CTX],
                                            AX_X, ALU.max).then_inc(c_mx3, 1)
                    dve.wait_ge(c_mx3, ON + o + 1)
                    nc.vector.tensor_scalar(nm3[:, :], mx3[:, :], -1.0, None, ALU.mult).then_inc(c_nm3, 1)
                    yield
                    dve.wait_ge(c_e3, ON + (o + 1) * TT)
                    nc.vector.reciprocal(inv3[:, :], sum3[:, :]).then_inc(c_inv3, 1)
                    yield
                    yield
                    dve.wait_ge(c_inv3, ON + o + 1)
                    dve.wait_ge(c_av3, ON + o + 1)
                    for i in range(TT):
                        nc.vector.scalar_tensor_tensor(xb[:, i, :], ps_last[:, i * D:(i + 1) * D], inv3[:, i:i + 1],
                                                       x2[:, i, :], ALU.mult, ALU.add).then_inc(c_out, 1)
                    yield
                    yield
                return last

            def negative(src, hi, lo, hi_done, lo_done, count):
                nc.vector.tensor_scalar(hi[:, :], src, -1.0, None, ALU.mult).then_inc(hi_done, 1)
                dve.wait_ge(hi_done, ON + count)
                nc.vector.scalar_tensor_tensor(lo[:, :], src, -1.0, hi[:, :], ALU.mult, ALU.subtract).then_inc(lo_done, 1)

            def body(n, u, flags, att_before, after):
                m = n - MAX_LAG

                def max_work(at):
                    for i in range(max_tiles(at - 1), max_tiles(at)):
                        dve.wait_ge(g_mt, ON + m * 2 * PAIRS + i + 1)
                        nc.vector.tensor_reduce(mxh[:, i // 2, i % 2:i % 2 + 1], ps_max[i % 2][:, :], AX_X,
                                                ALU.max).then_inc(g_mx, 1)
                    if at == SUB * MAX_TURN - 1:
                        dve.wait_ge(g_mx, ON + (m + 1) * 2 * PAIRS)
                        nc.vector.tensor_reduce(mxq[:, :], mxh[:, :, :], AX_X, ALU.max).then_inc(g_mp, 1)
                    if at == SUB * MAX_TURN + 1:
                        dve.wait_ge(g_mT, ON + m + 1)
                        dve.wait_ge(g_shl, ON + m * 32)
                        negative(ps_max[0][0:PAIRS, 0:P], sh_hi, sh_lo, g_shi, g_slo, m + 1)

                def inverses(slot):
                    if after[5] and slot == DEN_INV:
                        invert(1, n + 1 - LAST_LAG)

                walk(n, flags, pre, mid_by(1 - u, flags[5]), cross_by(not flags[2]), last_by(not flags[2]),
                     lambda slot, place: None, max_work, lambda: None, inverses, late_last=True)

            run(dve, body, SEGMENTS[:1])
            context()
            run(dve, body, SEGMENTS[1:])

        @block.tensor
        def _(pe):
            mm = nc.tensor.matmul
            pe.wait_ge(s_load, N_FIRST * 16)
            pe.wait_ge(s_const, 2)
            nc.tensor.transpose(ps_o[:, 0:2 * FM + 8 * KD], cols_n, ident[0:2 * FM + 8 * KD, 0:2 * FM + 8 * KD]
                                ).then_inc(s_colT, 1)
            pe.wait_ge(s_const, 6)

            def context():
                pe.wait_ge(s_load2, N_REST * 16)
                for c in range(NCT):
                    if c >= 3:
                        pe.wait_ge(s_ctT, c - 2)
                    for k in range(KD):
                        last = nc.tensor.transpose(ps_w[c % 3][:, k * P:k * P + CT], ctx_n[:, c, k * P:(k + 1) * P],
                                                   ident[0:CT, 0:CT])
                    last.then_inc(s_ct, 1)
                for w in range(2):
                    pe.wait_ge(s_ctT, NCT)
                    for kf in range(KD):
                        for kg in range(KD):
                            last = nc.tensor.transpose(ps_w[w][:, kf * D + kg * P:kf * D + (kg + 1) * P],
                                                       wl_n[w + 1][:, kg, kf * P:(kf + 1) * P], ident[:, :])
                    last.then_inc(s_wt, 1)
                pe.wait_ge(s_wlT, 2)
                half = B * CTX // 2
                for f in range(4):
                    m, span = f // 2, slice((f % 2) * half, (f % 2 + 1) * half)
                    if f >= 2:
                        pe.wait_ge(s_k2rest, f - 1)
                    for k in range(KD):
                        last = mm(ps_s[f % 2][:, 0:half], wkv2[:, k, m * P:(m + 1) * P], ctxT[k][:, span],
                                  start=(k == 0), stop=(k == KD - 1))
                    last.then_inc(s_k2, 1)
                    if f >= 2:
                        pe.wait_ge(s_kpb, f - 1)
                    for k in range(KD):
                        last = mm(ps_w[f % 2][:, 0:half], wlT[:, 0, k, m * P:(m + 1) * P], ctxT[k][:, span],
                                  start=(k == 0), stop=(k == KD - 1))
                    last.then_inc(s_kp, 1)
                pe.wait_ge(s_kpb, 4)
                pe.wait_ge(s_k2rest, 4)
                for g in range(2 * KD + 2):
                    kf, span = g // 2, slice((g % 2) * half, (g % 2 + 1) * half)
                    if g >= 2:
                        pe.wait_ge(s_mc, g - 1)
                    for k in range(KD):
                        w = wl_n[0][:, k, kf * P:(kf + 1) * P] if kf < KD else bql[:, k:k + 1]
                        last = mm(ps_s[g % 2][0:w.shape[1], 0:half], w, kp_all[:, k, span],
                                  start=(k == 0), stop=(k == KD - 1))
                    last.then_inc(s_m, 1)
                for c in range(NCT):
                    if c >= 3:
                        pe.wait_ge(s_vpb, c - 2)
                    for k in range(KD):
                        mm(ps_w[c % 3][0:CT, 0:D], ctxT[k][:, c * CT:(c + 1) * CT], wkv2[:, k, D:2 * D],
                           start=(k == 0), stop=(k == KD - 1))
                    for k in range(KD):
                        last = mm(ps_w[c % 3][0:CT, D:2 * D], ctxT[k][:, c * CT:(c + 1) * CT], wlT[:, 1, k, :],
                                  start=(k == 0), stop=(k == KD - 1))
                    last.then_inc(s_v2, 1)
                pe.wait_ge(s_vpb, NCT)
                pe.wait_ge(s_ones, 3)

            def turn(bank, x):
                for k in range(KD):
                    for i in range(TT):
                        last = nc.tensor.transpose(bank[:, k * CH + i * P:k * CH + (i + 1) * P],
                                                   x[:, i, k * P:(k + 1) * P], ident[:, :])
                return last

            def project(bank, w, y):
                for m in range(KD):
                    for k in range(KD):
                        last = mm(bank[:, m * CH:(m + 1) * CH], w[:, k, m * P:(m + 1) * P], y[:, k, :],
                                  start=(k == 0), stop=(k == KD - 1))
                return last

            def project_rows(bank, y, w):
                for i in range(TT):
                    for k in range(KD):
                        last = mm(bank[:, i * D:(i + 1) * D], y[:, k, i * P:(i + 1) * P], w[:, k, :],
                                  start=(k == 0), stop=(k == KD - 1))
                return last

            def pre_by(has_mid, has_cross):
                def pre(p):
                    for _ in range(3):
                        yield
                    pe.wait_ge(a_vc, ON + p)
                    if has_mid:
                        pe.wait_ge(c_q2f, ON + p - MID_LAG)
                    if has_cross:
                        pe.wait_ge(c_mx, ON + (p - CROSS_LAG + 1) * 2 * Q2F)
                    pe.wait_ge(a_xn, ON + (p + 1) * 2)
                    turn(ps_pre, pre_x).then_inc(a_T, 1)
                    yield
                    pe.wait_ge(a_y, ON + (p + 1) * 2)
                    project(ps_pre, wq1, pre_yT).then_inc(a_p[0], 1)
                    yield
                    pe.wait_ge(a_f[0], ON + p + 1)
                    project(ps_pre, wkv1, pre_yT).then_inc(a_p[1], 1)
                    yield
                    pe.wait_ge(a_f[1], ON + p + 1)
                    project_rows(ps_pre, pre_yT, wkv1[:, :, D:2 * D]).then_inc(a_v, 1)
                    yield
                    yield
                return pre

            def mid_by(takes_bank):
                def mid(o, has_pre):
                    for _ in range(3):
                        yield
                    if has_pre:
                        pe.wait_ge(a_vc, ON + o + MID_LAG + 1)
                    elif takes_bank:
                        pe.wait_ge(c_mx, ON + (o - CROSS_LAG + MID_LAG + 1) * 2 * Q2F)
                    pe.wait_ge(c_q2f, ON + o)
                    pe.wait_ge(c_on[0], ON + o + 1)
                    project_rows(ps_pre, oT, wo1).then_inc(c_wo[0], 1)
                    yield
                    yield
                    yield
                    pe.wait_ge(c_xn[0], ON + (o + 1) * 2)
                    turn(ps_pre, den_rows).then_inc(c_T[0], 1)
                    yield
                    pe.wait_ge(c_y[0], ON + (o + 1) * 2)
                    project(ps_pre, wq2, oT).then_inc(c_q2, 1)
                    yield
                    yield
                return mid

            def cross_by(spare):
                def cross(o):
                    yield
                    pe.wait_ge(s_fflo, KD * FF1_PIECES)
                    for f in range(2 * Q2F):
                        if f == 0:
                            pe.wait_ge(c_q2stack, ON + (o + 1) * 64)
                            pe.wait_ge(c_kv, ON + (o + 1) * 80)
                            pe.wait_ge(c_o, ON + o * 4)
                        else:
                            pe.wait_ge(c_mx, ON + o * 2 * Q2F + f - 1)
                        i, h0, nh = q2_heads(f)
                        for j in range(nh):
                            last = mm(cross_max_banks[spare][f % 2][:, j * CTX:(j + 1) * CTX], q2st[0:ROWS, h0 + j, i * P:(i + 1) * P],
                                      k2st[0:ROWS, h0 + j, :], start=True, stop=True)
                        last.then_inc(c_mt, 1)
                        yield
                    pe.wait_ge(c_mx, ON + (o + 1) * 2 * Q2F)
                    nc.tensor.transpose(ps_cross[0:H * TT, 0:P], mx2[:, :, :].rearrange("p h i -> p (h i)"),
                                        ident[:, :]).then_inc(c_mT, 1)
                    for _ in range(3):
                        yield
                    for h in range(H):
                        if h == 0:
                            pe.wait_ge(c_shl, ON + (o + 1) * 32)
                        elif h % G == 1 and h > 1 and not spare:
                            pe.wait_ge(c_o, ON + o * 4 + h // G)
                        else:
                            pe.wait_ge(c_e, ON + o * H + h - spare)
                        at = h % (H // KD) * KD + h // (H // KD)
                        for a in range(2):
                            last = mm(cross_banks[spare][h % 2][0:CT, a * CH:(a + 1) * CH], k2st[:, at, a * CT:(a + 1) * CT],
                                      q2st[:, at, :], start=True, stop=True)
                        last.then_inc(c_s, 1)
                        yield
                        if h % G == 0 and h or h == H - 1:
                            g = max(0, h - 1) // G
                            pe.wait_ge(c_e, ON + o * H + h + 1)
                            if spare:
                                pe.wait_ge(c_o, ON + o * 4 + g)
                            for a in range(2):
                                for j in range(G):
                                    i = G * g + j
                                    last = mm(ps_cross[j * W:(j + 1) * W, 0:CH],
                                              v2[:, a, i * W:(i + 1) * W], probs2[:, i % PR2, a * CH:(a + 1) * CH],
                                              start=(a == 0), stop=(a == 1), tile_position=(0, j * W))
                            last.then_inc(c_av, 1)
                            yield
                return cross

            def last_by(spare):
                def last(o):
                    for _ in range(3):
                        yield
                    pe.wait_ge(c_on[1], ON + o + 1)
                    pe.wait_ge(c_out, ON + o * 2)
                    project_rows(ps_last, oT2, wo2).then_inc(c_wo[1], 1)
                    yield
                    yield
                    yield
                    pe.wait_ge(c_xn[1], ON + (o + 1) * 2)
                    turn(ps_last, oT2_rows).then_inc(c_T[1], 1)
                    yield
                    pe.wait_ge(c_y3lo, ON + o + 1)
                    for m in range(FM):
                        if m > spare:
                            pe.wait_ge(c_h, ON + o * FM + m - spare)
                        for part in range(2):
                            cols_ = slice((part * FM + m) * P, (part * FM + m + 1) * P)
                            terms = [(k, w, y) for k in range(KD) for w, y in ((0, 0), (0, 1), (1, 0))]
                            for i, (k, w, y) in enumerate(terms):
                                last = mm(last_banks[spare][m % 2][:, part * CH:(part + 1) * CH],
                                          wff1[w][:, k, cols_], y3[y][:, k, :],
                                          start=(i == 0), stop=(i == len(terms) - 1))
                        last.then_inc(c_f1, 1)
                        yield
                    pe.wait_ge(c_h, ON + (o + 1) * FM)
                    for q in range(4):
                        i = q // 2
                        for m in range((q % 2) * FM // 2, (q % 2 + 1) * FM // 2):
                            last = mm(ps_last[:, i * D:(i + 1) * D], hT[:, m, i * P:(i + 1) * P], wff2[:, m, :],
                                      start=(m == 0), stop=(m == FM - 1))
                        if q == 3:
                            last.then_inc(c_f2, 1)
                        yield
                    yield
                    pe.wait_ge(c_x[2], ON + o + 1)
                    turn(ps_last, x2).then_inc(c_T[2], 1)
                    yield
                    pe.wait_ge(c_y[2], ON + o + 1)
                    for i in range(TT):
                        for k in range(KD):
                            mm(ps_last[:, i * CH:i * CH + CTX], den2[:, k, i * P:(i + 1) * P], m3[:, k, :],
                               start=(k == 0), stop=False)
                        last = mm(ps_last[:, i * CH:i * CH + CTX], ones[:, :], m3_b[:, :], start=False, stop=True)
                    last.then_inc(c_s3, 1)
                    yield
                    yield
                    pe.wait_ge(c_e3, ON + (o + 1) * TT)
                    for a in range(2):
                        for i in range(TT):
                            last = nc.tensor.transpose(ps_last[0:CT, a * CH + i * P:a * CH + (i + 1) * P],
                                                       p3[:, i, a * CT:(a + 1) * CT], ident[:, :])
                    last.then_inc(c_pT, 1)
                    yield
                    pe.wait_ge(c_pTc, ON + o + 1)
                    for i in range(TT):
                        for a in range(2):
                            last = mm(ps_last[:, i * D:(i + 1) * D], p3T[:, a, i * P:(i + 1) * P], vp[:, a, :],
                                      start=(a == 0), stop=(a == 1))
                    last.then_inc(c_av3, 1)
                    yield
                    yield
                return last

            def body(n, u, flags, att_before, after):
                grp, m = n - ATT_LAG, n - MAX_LAG

                def max_work(at):
                    qs, ks = qst[u], kst[u]
                    for i in range(max_tiles(at - 1), max_tiles(at)):
                        j, q, k = i // 2 // NQ, i // 2 % NQ, i % 2
                        if i == 0:
                            pe.wait_ge(g_stack[u], ON + (m // 2 + 1) * 8 * 16)
                            pe.wait_ge(g_slo, ON + m)
                        pe.wait_ge(g_mx, ON + m * 2 * PAIRS + max(0, i - 1))
                        mm(ps_max[i % 2][:, :], qs[0:ROWS, j, q * P:(q + 1) * P],
                           ks[0:ROWS, j, k * 512:(k + 1) * 512], start=True, stop=True).then_inc(g_mt, 1)
                    if at == SUB * MAX_TURN + 1:
                        pe.wait_ge(g_mp, ON + m + 1)
                        nc.tensor.transpose(ps_max[0][0:PAIRS, 0:P], mxq[:, :], ident[:, :]).then_inc(g_mT, 1)

                def scores(c, j):
                    qh, kt = divmod(c, KT)
                    if c == 0 and j == 0:
                        pe.wait_ge(g_shl, ON + (grp + 1) * 32)
                    pe.wait_ge(g_e, ON + grp * 64 + max(0, c * G + j - 1))
                    mm(ps_s[j % 2][:, :], kst[1 - u][:, j, kt * P:(kt + 1) * P],
                       qst[1 - u][:, j, qh * QW:(qh + 1) * QW], start=True, stop=True).then_inc(g_s, 1)

                def values(c):
                    qh, kt = divmod(c, KT)
                    pe.wait_ge(g_e, ON + grp * 64 + (c + 1) * G)
                    if c == 0:
                        pe.wait_ge(g_v, ON + (grp + 1) * 16)
                    if kt == 0:
                        pe.wait_ge(g_o, ON + grp * QH + qh)
                    for j in range(G):
                        last = mm(ps_o[j * W:(j + 1) * W, :], vg[1 - u][:, kt, j * W:(j + 1) * W],
                                  probs[:, c % 2, j, :], start=(kt == 0), stop=(kt == KT - 1),
                                  tile_position=(0, j * W))
                    last.then_inc(g_av, 1)

                def att_work(slot, place):
                    c, pair = divmod(slot, 2)
                    if place == 0:
                        scores(c, 2 * pair)
                        scores(c, 2 * pair + 1)
                    if pair == 0 and c > 0 and place == PV_PLACE:
                        values(c - 1)

                def tail():
                    if flags[2]:
                        values(STEPS - 1)

                walk(n, flags, pre_by(flags[3], flags[4]), mid_by(flags[4] and flags[2]), cross_by(not flags[2]), last_by(not flags[2]), att_work, max_work, tail)

            run(pe, body, SEGMENTS[:1])
            context()
            run(pe, body, SEGMENTS[1:])


VECTORS = ["L0_xattn_bff1"] + [f"L0_xattn_ln{i + 1}_{c}" for c in "sb" for i in range(3)] + [
    "L1_xattn_bq", "L1_xattn_bk"]
N_FIRST = len(VECTORS) + 2
N_REST = 13

_INS = ["x", "ctx_1024"] + ["L0_xattn_" + s for s in (
    "Wq1", "Wkv1", "Wo1", "bo1", "Wq2", "Wkv2", "Wo2", "bo2", "Wff1", "bff1", "Wff2", "bff2",
    "ln1_s", "ln1_b", "ln2_s", "ln2_b", "ln3_s", "ln3_b")] + ["L1_xattn_" + s for s in (
        "Wq", "bq", "Wk", "bk", "Wv", "bv")]


def kernel(**inputs):
    import numpy as _np
    import concourse.bacc as _bacc
    from concourse import mybir as _mybir
    from concourse.bass_utils import run_bass_kernel_spmd as _run

    nc = _bacc.Bacc("TRN2", target_bir_lowering=False, num_devices=1)
    arrays, tensors = {}, {}
    for name in _INS:
        a = _np.ascontiguousarray(inputs[name])
        arrays[f"in_{name}_dram"] = a
        tensors[name] = nc.dram_tensor(f"in_{name}_dram", a.shape, _mybir.dt.from_np(a.dtype),
                                       kind="ExternalInput").ap()
    out = nc.dram_tensor("out_dram", (B, S, D), _mybir.dt.from_np(_np.dtype("float32")), kind="ExternalOutput").ap()
    xattn_kernel(nc, tensors, out)
    r = _run(nc, [arrays], core_ids=[0])
    return r.results[0]["out_dram"]
```
